# Optimizing a Trainium2 kernel written in Bass

```python
import numpy as np
import jax
import jax.numpy as jnp

def _softmax(x, axis=-1):
    return jax.nn.softmax(x, axis=axis)

def _gelu(x):
    return jax.nn.gelu(x, approximate=True)

def _silu(x):
    return jax.nn.silu(x)

def _sigmoid(x):
    return jax.nn.sigmoid(x)

def _layernorm(x, axis=-1, eps=1e-05):
    m = jnp.mean(x, axis=axis, keepdims=True)
    v = jnp.var(x, axis=axis, keepdims=True)
    return (x - m) / jnp.sqrt(v + eps)

def _scatter_add(tgt, idx, src, axis=0):
    return tgt.at[idx].add(src)

def _segment_sum(src, seg, n):
    return jax.ops.segment_sum(src, seg, n)
kernel_name = 'mk_macaron_d1_jaxref_r4_5df440'

def setup_inputs(seed: int=0):
    np.random.seed(seed)
    _w = jnp.asarray

    def _L0_attn_setup():
        import jax, jax.numpy as jnp
        import numpy as np
        import math
        DIM = 256
        N_HEADS = 16
        HEAD_DIM = DIM // N_HEADS

        def rope(x):
            S = x.shape[-2]
            D = x.shape[-1]
            pos = jnp.arange(S, dtype=x.dtype)[:, None]
            dim = jnp.arange(D // 2, dtype=x.dtype)[None, :]
            theta = pos / jnp.exp(2.0 * dim / D * math.log(10000.0))
            sin = jnp.sin(theta)[None, None]
            cos = jnp.cos(theta)[None, None]
            x1 = x[..., ::2]
            x2 = x[..., 1::2]
            out1 = x1 * cos - x2 * sin
            out2 = x1 * sin + x2 * cos
            return jnp.stack([out1, out2], axis=-1).reshape(x.shape)
        key = jax.random.key(seed)
        ks = jax.random.split(key, 9)
        B, S = (2, 512)
        s = 1.0 / math.sqrt(DIM)
        inp = {'x': jax.random.normal(ks[0], (B, S, DIM), dtype=jnp.float32), 'wq': jax.random.normal(ks[1], (DIM, DIM), dtype=jnp.float32) * s, 'bq': jnp.zeros((DIM,), dtype=jnp.float32), 'wk': jax.random.normal(ks[2], (DIM, DIM), dtype=jnp.float32) * s, 'bk': jnp.zeros((DIM,), dtype=jnp.float32), 'wv': jax.random.normal(ks[3], (DIM, DIM), dtype=jnp.float32) * s, 'bv': jnp.zeros((DIM,), dtype=jnp.float32), 'wo': jax.random.normal(ks[4], (DIM, DIM), dtype=jnp.float32) * s, 'bo': jnp.zeros((DIM,), dtype=jnp.float32)}
        return inp
    _L0_attn_in = _L0_attn_setup()

    def _L0_ffn_setup():
        import jax, jax.numpy as jnp
        import numpy as np
        DIM = 256
        DEPTH = 2
        HEADS = 8
        DIM_HEAD = 64
        WINDOW = 128
        INNER = HEADS * DIM_HEAD
        HID = int(DIM * 4 * 2 / 3)
        B, N = (2, 2048)
        QK_SCALE = 8.0

        def shift_token(t):
            t1, t2 = jnp.split(t, 2, axis=-1)
            t2 = jnp.pad(t2, ((0, 0), (1, 0), (0, 0)))[:, :-1]
            return jnp.concatenate([t1, t2], axis=-1)

        def l2norm(t):
            return t / jnp.clip(jnp.linalg.norm(t, axis=-1, keepdims=True), 1e-12)

        def rotate_half(x):
            x1, x2 = jnp.split(x, 2, axis=-1)
            return jnp.concatenate([-x2, x1], axis=-1)

        def rotary_xpos(q, k):
            n = q.shape[-2]
            half_idx = jnp.arange(0, DIM_HEAD, 2, dtype=jnp.float32)
            inv_freq = 1.0 / 10000.0 ** (half_idx / DIM_HEAD)
            t = jnp.arange(n, dtype=jnp.float32)
            freqs = t[:, None] * inv_freq[None, :]
            freqs = jnp.concatenate([freqs, freqs], axis=-1)
            base = (half_idx + 0.4 * DIM_HEAD) / (1.4 * DIM_HEAD)
            power = (t - n // 2) / float(WINDOW // 2)
            scale = base[None, :] ** power[:, None]
            scale = jnp.concatenate([scale, scale], axis=-1)
            cos, sin = (jnp.cos(freqs), jnp.sin(freqs))
            q = q * cos * scale + rotate_half(q) * sin * scale
            k = k * cos / scale + rotate_half(k) * sin / scale
            return (q, k)

        def local_attention(q, k, v):
            b, h, n, d = q.shape
            w = n // WINDOW
            bq = q.reshape(b, h, w, WINDOW, d) * QK_SCALE
            bk = k.reshape(b, h, w, WINDOW, d)
            bv = v.reshape(b, h, w, WINDOW, d)

            def look_around(t):
                p = jnp.pad(t, ((0, 0), (0, 0), (1, 0), (0, 0), (0, 0)))
                return jnp.concatenate([p[:, :, :w], p[:, :, 1:]], axis=3)
            bk, bv = (look_around(bk), look_around(bv))
            bt = jnp.arange(n).reshape(w, WINDOW)
            btp = jnp.pad(bt, ((1, 0), (0, 0)), constant_values=-1)
            btk = jnp.concatenate([btp[:w], btp[1:]], axis=1)
            sim = jnp.einsum('bhwid,bhwjd->bhwij', bq, bk)
            i = bt[:, :, None]
            j = btk[:, None, :]
            mask = (i < j) | (i > j + WINDOW) | (j == -1)
            sim = jnp.where(mask, -jnp.finfo(sim.dtype).max, sim)
            attn = jax.nn.softmax(sim, axis=-1)
            out = jnp.einsum('bhwij,bhwjd->bhwid', attn, bv)
            return out.reshape(b, h, n, d)

        def _layer(x, wqkv, qs, ksc, wo, lg, lb, w1, b1, w2, b2):
            b, n, _ = x.shape
            h = shift_token(x)
            qkv = h @ wqkv
            q, k, v = jnp.split(qkv, 3, axis=-1)
            to_heads = lambda t: t.reshape(b, n, HEADS, DIM_HEAD).transpose(0, 2, 1, 3)
            q, k, v = (to_heads(q), to_heads(k), to_heads(v))
            q = l2norm(q) * qs
            k = l2norm(k) * ksc
            q, k = rotary_xpos(q, k)
            o = local_attention(q, k, v)
            o = o.transpose(0, 2, 1, 3).reshape(b, n, INNER)
            x = x + o @ wo
            h = shift_token(x)
            mu = h.mean(-1, keepdims=True)
            var = h.var(-1, keepdims=True)
            h = (h - mu) / jnp.sqrt(var + 1e-05) * lg + lb
            h = h @ w1 + b1
            a, g = jnp.split(h, 2, axis=-1)
            h = a * jax.nn.gelu(g, approximate=False)
            x = x + h @ w2 + b2
            return x
        key = jax.random.key(seed)
        ks = jax.random.split(key, 6)
        return {'x': jax.random.normal(ks[0], (B, N, DIM), jnp.float32), 'wqkv': jax.random.normal(ks[1], (DEPTH, DIM, 3 * INNER), jnp.float32) * 0.02, 'q_scale': jnp.ones((DEPTH, DIM_HEAD), jnp.float32), 'k_scale': jnp.ones((DEPTH, DIM_HEAD), jnp.float32), 'wo': jax.random.normal(ks[2], (DEPTH, INNER, DIM), jnp.float32) * 0.02, 'ln_g': jnp.ones((DEPTH, DIM), jnp.float32), 'ln_b': jnp.zeros((DEPTH, DIM), jnp.float32), 'w1': jax.random.normal(ks[3], (DEPTH, DIM, 2 * HID), jnp.float32) * 0.02, 'b1': jnp.zeros((DEPTH, 2 * HID), jnp.float32), 'w2': jax.random.normal(ks[4], (DEPTH, HID, DIM), jnp.float32) * 0.02, 'b2': jnp.zeros((DEPTH, DIM), jnp.float32)}
    _L0_ffn_in = _L0_ffn_setup()
    _d = {'L0_attn_x': _L0_attn_in['x'], 'L0_attn_wq': _L0_attn_in['wq'], 'L0_attn_bq': _L0_attn_in['bq'], 'L0_attn_wk': _L0_attn_in['wk'], 'L0_attn_bk': _L0_attn_in['bk'], 'L0_attn_wv': _L0_attn_in['wv'], 'L0_attn_bv': _L0_attn_in['bv'], 'L0_attn_wo': _L0_attn_in['wo'], 'L0_attn_bo': _L0_attn_in['bo'], 'L0_ffn_wqkv': _L0_ffn_in['wqkv'], 'L0_ffn_q_scale': _L0_ffn_in['q_scale'], 'L0_ffn_k_scale': _L0_ffn_in['k_scale'], 'L0_ffn_wo': _L0_ffn_in['wo'], 'L0_ffn_ln_g': _L0_ffn_in['ln_g'], 'L0_ffn_ln_b': _L0_ffn_in['ln_b'], 'L0_ffn_w1': _L0_ffn_in['w1'], 'L0_ffn_b1': _L0_ffn_in['b1'], 'L0_ffn_w2': _L0_ffn_in['w2'], 'L0_ffn_b2': _L0_ffn_in['b2']}
    _x0 = _d['L0_attn_x']
    _d['L0_attn_x'] = jax.random.normal(jax.random.fold_in(jax.random.key(seed), 1), (1, 4096, 256), dtype=_x0.dtype)
    del _x0
    return _d

def reference(L0_attn_x, L0_attn_wq, L0_attn_bq, L0_attn_wk, L0_attn_bk, L0_attn_wv, L0_attn_bv, L0_attn_wo, L0_attn_bo, L0_ffn_wqkv, L0_ffn_q_scale, L0_ffn_k_scale, L0_ffn_wo, L0_ffn_ln_g, L0_ffn_ln_b, L0_ffn_w1, L0_ffn_b1, L0_ffn_w2, L0_ffn_b2):

    def _L0_attn_ref(x, wq, bq, wk, bk, wv, bv, wo, bo):
        import jax, jax.numpy as jnp
        import numpy as np
        import math
        DIM = 256
        N_HEADS = 16
        HEAD_DIM = DIM // N_HEADS

        def rope(x):
            S = x.shape[-2]
            D = x.shape[-1]
            pos = jnp.arange(S, dtype=x.dtype)[:, None]
            dim = jnp.arange(D // 2, dtype=x.dtype)[None, :]
            theta = pos / jnp.exp(2.0 * dim / D * math.log(10000.0))
            sin = jnp.sin(theta)[None, None]
            cos = jnp.cos(theta)[None, None]
            x1 = x[..., ::2]
            x2 = x[..., 1::2]
            out1 = x1 * cos - x2 * sin
            out2 = x1 * sin + x2 * cos
            return jnp.stack([out1, out2], axis=-1).reshape(x.shape)
        B, S, _ = x.shape

        def proj(w, b):
            y = jnp.einsum('bsd,ed->bse', x, w) + b
            return y.reshape(B, S, N_HEADS, HEAD_DIM).transpose(0, 2, 1, 3)
        q = rope(proj(wq, bq))
        k = rope(proj(wk, bk))
        v = proj(wv, bv)
        score = jnp.einsum('bhqd,bhkd->bhqk', q, k) / math.sqrt(HEAD_DIM)
        causal = jnp.tril(jnp.ones((S, S), dtype=bool))
        score = jnp.where(causal[None, None], score, -jnp.inf)
        attn = jax.nn.softmax(score, axis=-1)
        out = jnp.einsum('bhqk,bhkd->bhqd', attn, v)
        out = out.transpose(0, 2, 1, 3).reshape(B, S, DIM)
        return jnp.einsum('bsd,ed->bse', out, wo) + bo

    def _L0_ffn_ref(x, wqkv, q_scale, k_scale, wo, ln_g, ln_b, w1, b1, w2, b2):
        import jax, jax.numpy as jnp
        import numpy as np
        DIM = 256
        DEPTH = 2
        HEADS = 8
        DIM_HEAD = 64
        WINDOW = 128
        INNER = HEADS * DIM_HEAD
        HID = int(DIM * 4 * 2 / 3)
        B, N = (2, 2048)
        QK_SCALE = 8.0

        def shift_token(t):
            t1, t2 = jnp.split(t, 2, axis=-1)
            t2 = jnp.pad(t2, ((0, 0), (1, 0), (0, 0)))[:, :-1]
            return jnp.concatenate([t1, t2], axis=-1)

        def l2norm(t):
            return t / jnp.clip(jnp.linalg.norm(t, axis=-1, keepdims=True), 1e-12)

        def rotate_half(x):
            x1, x2 = jnp.split(x, 2, axis=-1)
            return jnp.concatenate([-x2, x1], axis=-1)

        def rotary_xpos(q, k):
            n = q.shape[-2]
            half_idx = jnp.arange(0, DIM_HEAD, 2, dtype=jnp.float32)
            inv_freq = 1.0 / 10000.0 ** (half_idx / DIM_HEAD)
            t = jnp.arange(n, dtype=jnp.float32)
            freqs = t[:, None] * inv_freq[None, :]
            freqs = jnp.concatenate([freqs, freqs], axis=-1)
            base = (half_idx + 0.4 * DIM_HEAD) / (1.4 * DIM_HEAD)
            power = (t - n // 2) / float(WINDOW // 2)
            scale = base[None, :] ** power[:, None]
            scale = jnp.concatenate([scale, scale], axis=-1)
            cos, sin = (jnp.cos(freqs), jnp.sin(freqs))
            q = q * cos * scale + rotate_half(q) * sin * scale
            k = k * cos / scale + rotate_half(k) * sin / scale
            return (q, k)

        def local_attention(q, k, v):
            b, h, n, d = q.shape
            w = n // WINDOW
            bq = q.reshape(b, h, w, WINDOW, d) * QK_SCALE
            bk = k.reshape(b, h, w, WINDOW, d)
            bv = v.reshape(b, h, w, WINDOW, d)

            def look_around(t):
                p = jnp.pad(t, ((0, 0), (0, 0), (1, 0), (0, 0), (0, 0)))
                return jnp.concatenate([p[:, :, :w], p[:, :, 1:]], axis=3)
            bk, bv = (look_around(bk), look_around(bv))
            bt = jnp.arange(n).reshape(w, WINDOW)
            btp = jnp.pad(bt, ((1, 0), (0, 0)), constant_values=-1)
            btk = jnp.concatenate([btp[:w], btp[1:]], axis=1)
            sim = jnp.einsum('bhwid,bhwjd->bhwij', bq, bk)
            i = bt[:, :, None]
            j = btk[:, None, :]
            mask = (i < j) | (i > j + WINDOW) | (j == -1)
            sim = jnp.where(mask, -jnp.finfo(sim.dtype).max, sim)
            attn = jax.nn.softmax(sim, axis=-1)
            out = jnp.einsum('bhwij,bhwjd->bhwid', attn, bv)
            return out.reshape(b, h, n, d)

        def _layer(x, wqkv, qs, ksc, wo, lg, lb, w1, b1, w2, b2):
            b, n, _ = x.shape
            h = shift_token(x)
            qkv = h @ wqkv
            q, k, v = jnp.split(qkv, 3, axis=-1)
            to_heads = lambda t: t.reshape(b, n, HEADS, DIM_HEAD).transpose(0, 2, 1, 3)
            q, k, v = (to_heads(q), to_heads(k), to_heads(v))
            q = l2norm(q) * qs
            k = l2norm(k) * ksc
            q, k = rotary_xpos(q, k)
            o = local_attention(q, k, v)
            o = o.transpose(0, 2, 1, 3).reshape(b, n, INNER)
            x = x + o @ wo
            h = shift_token(x)
            mu = h.mean(-1, keepdims=True)
            var = h.var(-1, keepdims=True)
            h = (h - mu) / jnp.sqrt(var + 1e-05) * lg + lb
            h = h @ w1 + b1
            a, g = jnp.split(h, 2, axis=-1)
            h = a * jax.nn.gelu(g, approximate=False)
            x = x + h @ w2 + b2
            return x
        for l in range(DEPTH):
            x = _layer(x, wqkv[l], q_scale[l], k_scale[l], wo[l], ln_g[l], ln_b[l], w1[l], b1[l], w2[l], b2[l])
        return x
    x = L0_attn_x
    x = x + 0.5 * _L0_ffn_ref(_layernorm(x, axis=-1), L0_ffn_wqkv, L0_ffn_q_scale, L0_ffn_k_scale, L0_ffn_wo, L0_ffn_ln_g, L0_ffn_ln_b, L0_ffn_w1, L0_ffn_b1, L0_ffn_w2, L0_ffn_b2)
    x = x + _L0_attn_ref(_layernorm(x, axis=-1), L0_attn_wq, L0_attn_bq, L0_attn_wk, L0_attn_bk, L0_attn_wv, L0_attn_bv, L0_attn_wo, L0_attn_bo)
    x = x + 0.5 * _L0_ffn_ref(_layernorm(x, axis=-1), L0_ffn_wqkv, L0_ffn_q_scale, L0_ffn_k_scale, L0_ffn_wo, L0_ffn_ln_g, L0_ffn_ln_b, L0_ffn_w1, L0_ffn_b1, L0_ffn_w2, L0_ffn_b2)
    return x

_drawn_inputs = setup_inputs


def setup_inputs(seed=0):
    import zlib

    import numpy as np

    out = dict(_drawn_inputs(seed))
    spreads = {'L0_attn_bq': (0.0, 0.8),
     'L0_attn_bk': (0.0, 0.8),
     'L0_attn_bv': (0.0, 0.1),
     'L0_attn_bo': (0.0, 0.1),
     'L0_ffn_q_scale': (1.0, 0.6),
     'L0_ffn_k_scale': (1.0, 0.6),
     'L0_ffn_ln_g': (1.0, 0.6),
     'L0_ffn_ln_b': (0.0, 0.8),
     'L0_ffn_b1': (0.0, 0.701),
     'L0_ffn_b2': (0.0, 0.1)}
    factors = {'L0_ffn_wqkv': 3.022, 'L0_ffn_wo': 2.949}
    for name, (base, spread) in spreads.items():
        noise = np.random.default_rng([zlib.crc32(name.encode()), seed]).standard_normal(out[name].shape)
        drawn = base * np.exp(spread * noise) if base else spread * noise
        out[name] = jnp.asarray(drawn.astype(out[name].dtype))
    for name, factor in factors.items():
        out[name] = (out[name] * factor).astype(out[name].dtype)
    return out
```

```python
from collections import namedtuple
from contextlib import ExitStack

import numpy as np
import concourse.bass as bass
from concourse import mybir

F32 = mybir.dt.float32
BF16 = mybir.dt.bfloat16
ALU = mybir.AluOpType
ACT = mybir.ActivationFunctionType
AX = mybir.AxisListType

P = 128
D = 256
KC = D // P
S = 4096
NT = S // P
DEPTH = 2
WH = 8
WD = 64
INNER = WH * WD
HID = int(D * 4 * 2 / 3)
NC = -(-HID // P)
NH = 16
HD = D // NH
GT = 4
NG = NT // GT
GW = GT * P
NEG = -1e30
EPS = 1e-5

HEAD_ORDER = [0, 2, 1, 3, 4, 6, 5, 7]

Tile = namedtuple("Tile", "place count slot turn")


def tile_at(pair, before, odd, ahead=0):
    p, slot = pair + (odd + ahead) // 2, (odd + ahead) % 2
    return Tile(2 * p + slot, 2 * (p + before) + slot, slot, p + before)


def exists(pair, odd, ahead):
    return not isinstance(pair, int) or 0 <= 2 * pair + odd + ahead < NT


def pass_gate(eng, sem, semaphore, value):
    eng.wait_ge(semaphore, value)
    eng.sem_inc(sem.gates_passed, 1)


def stepped(eng, step, first, last):
    for s in range(first, 2):
        step(s // 2, s % 2)
    with eng.Fori(1, NT // 2 - 1) as pair:
        for odd in range(2):
            step(pair, odd)
    for s in range(NT - 2, last + 1):
        step(s // 2, s % 2)


def window_attention(nc, m, sem, before):
    with ExitStack() as ctx:
        def sb(name, shape, dt=F32):
            return ctx.enter_context(nc.sbuf_tensor(name + m.tag, shape, dt))

        def ps(name, shape, dt=F32):
            return ctx.enter_context(nc.psum_tensor(name + m.tag, shape, dt))

        X, h = m.X, sb("h", [P, 2, D])
        hT = sb("hT", [P, 2, KC, P])
        rope_raw = sb("rope_raw", [P, 2, 4, WD])
        rope = sb("rope", [P, 2, 4, WD])
        squares = sb("squares", [P, 2, INNER])
        ssq = sb("ssq", [P, 2, 2 * WH])
        rnorm = sb("rnorm", [P, 2, 2 * WH])
        turned = sb("turned", [P, 2, INNER])
        crossed = sb("crossed", [P, 2, INNER])
        qk = sb("qk", [P, 2, INNER])
        qT = sb("qT", [P, WH // 2, P])
        kT = sb("kT", [P, WH // 2, 2, P])
        v = sb("v", [P, 2, INNER])
        scores = sb("scores", [P, WH, 2 * P])
        smax = sb("smax", [P, 2, WH])
        nbias = sb("nbias", [P, 2, WH])
        probs = sb("probs", [P, 2, WH, 2 * P])
        psum_row = sb("psum_row", [P, 2, WH])
        rsum = sb("rsum", [P, 2, WH])
        probsT = sb("probsT", [P, WH, 2, P])
        o = sb("o", [P, INNER])
        oT = sb("oT", [P, INNER // P, P])

        qkv_ps = ps("qkv_ps", [P, 3, INNER])
        out_ps = ps("out_ps", [P, INNER])
        ring = ps("ring", [P, 4, INNER])
        QT, KT, HT = 0, 1, 2
        PT = [3, 0, 1, 2]
        SC = [3, 0, 1, 2]
        OS = 3

        block = ctx.enter_context(nc.Block())

        @block.sync
        def _(sp):
            nc.sync.dma_start(m.wqkv[:], m.wqkv_dram[m.layer]).then_inc(sem.w_attn_in, 16)
            nc.sync.dma_start(m.scales[:], m.scales_dram[m.layer].partition_broadcast(P)).then_inc(sem.w_attn_in, 16)
            nc.sync.dma_start(m.wo[:], m.wo_dram[m.layer]).then_inc(sem.w_attn_in, 16)

            def load(pair, odd):
                a = tile_at(pair, before, odd)
                if exists(pair, odd, -2):
                    sp.wait_ge(sem.hT_made, a.count - 1)
                    sp.wait_ge(sem.rope_made, a.count - 1)
                nc.sync.dma_start(h[:, a.slot, 0:P], X[:, a.place, 0:P]).then_inc(sem.h_in[a.slot], 16)
                nc.sync.dma_start(h[1:P, a.slot, P:D], X[0:P - 1, a.place, P:D]).then_inc(sem.h_in[a.slot], 16)
                last = m.zeros[0:1, 0:P] if not exists(pair, odd, -1) else X[P - 1:P, a.place - 1, P:D]
                nc.sync.dma_start(h[0:1, a.slot, P:D], last).then_inc(sem.h_in[a.slot], 16)
                nc.sync.dma_start(rope_raw[:, a.slot], m.rope_dram[a.place]).then_inc(sem.rope_in[a.slot], 16)
            for s in range(2):
                load(s // 2, s % 2)
            with sp.Fori(1, NT // 2) as pair:
                for odd in range(2):
                    load(pair, odd)
            for dst, src in m.mlp_weights(m.layer):
                nc.sync.dma_start(dst, src).then_inc(sem.w_mlp_in, 16)

        @block.tensor
        def _(pe):
            def step(pair, odd):
                cur, nxt, nxt2, prv = (tile_at(pair, before, odd, k) for k in (0, 1, 2, -1))
                is_cur, is_nxt, is_nxt2, is_prv = (exists(pair, odd, k) for k in (0, 1, 2, -1))
                is_prv2 = exists(pair, odd, -2)
                if is_cur:
                    pe.wait_ge(sem.qk_rotated, cur.count + 1)
                    for c, slot in ((0, QT), (1, KT)):
                        if is_prv:
                            pe.wait_ge(sem.masked, WH * prv.count + 4 + 2 * c)
                        for j in range(WH // 2):
                            mm = nc.tensor.transpose(ring[:, slot, j * P:(j + 1) * P], qk[:, c, j * P:(j + 1) * P], m.ident[:])
                        mm.then_inc(sem.qkT_made, 1)
                if is_nxt2:
                    pe.wait_ge(sem.h_in[nxt2.slot], 48 * nxt2.turn + 48)
                    if is_prv:
                        pe.wait_ge(sem.masked, WH * prv.count + 8)
                    elif is_nxt:
                        pe.wait_ge(sem.hT_copied, nxt.count + 1)
                    for c in range(KC):
                        mm = nc.tensor.transpose(ring[:, HT, c * P:(c + 1) * P], h[:, nxt2.slot, c * P:(c + 1) * P], m.ident[:])
                    mm.then_inc(sem.hT_made, 1)
                if is_prv:
                    for n in range(4):
                        pe.wait_ge(sem.probs_made, WH * prv.count + 2 * n + 2)
                        if n == 0 and is_prv2:
                            pe.wait_ge(sem.o_made, prv.count)
                        if n in (1, 2) and is_cur:
                            pe.wait_ge(sem.qkT_copied, 2 * cur.count + n)
                        if n == 3 and is_nxt2:
                            pe.wait_ge(sem.hT_copied, nxt2.count + 1)
                        for i in range(2):
                            for b in range(2):
                                mm = nc.tensor.transpose(ring[:, PT[n], (2 * i + b) * P:(2 * i + b + 1) * P],
                                                         probs[:, prv.slot, HEAD_ORDER[2 * n + i], b * P:(b + 1) * P], m.ident[:])
                        mm.then_inc(sem.pT_made, 1)
                if is_cur:
                    pe.wait_ge(sem.qkT_copied, 2 * cur.count + 2)
                    if not is_prv:
                        pe.wait_ge(sem.window_cleared, before // (NT // 2) * 2 + 2)
                        pe.wait_ge(sem.hT_copied, nxt2.count + 1)
                    for half in range(2):
                        if is_prv:
                            pe.wait_ge(sem.pT_copied, 4 * prv.count + 2 * half + 2)
                        for n in range(4):
                            head = 4 * half + n
                            row = WD * (head % 2)
                            mm = nc.tensor.matmul(ring[:, SC[2 * half + n % 2], (n // 2) * 2 * P:(n // 2 + 1) * 2 * P],
                                                  qT[row:row + WD, head // 2],
                                                  kT[row:row + WD, head // 2].rearrange("p b t -> p (b t)"), start=True, stop=True)
                            if n >= 2:
                                mm.then_inc(sem.scores_made, 1)
                if is_prv:
                    pe.wait_ge(sem.pT_copied, 4 * prv.count + 4)
                    pe.wait_ge(sem.v_copied, prv.count + 1)
                    if is_cur:
                        pe.wait_ge(sem.masked, WH * cur.count + 2)
                    for head in range(WH):
                        for b in range(2):
                            mm = nc.tensor.matmul(ring[:, OS, head * WD:(head + 1) * WD], probsT[:, head, b],
                                                  v[:, b, head * WD:(head + 1) * WD], start=(b == 0), stop=(b == 1))
                    mm.then_inc(sem.o_summed, 1)
                if is_nxt:
                    pe.wait_ge(sem.hT_copied, nxt.count + 1)
                    if not exists(pair, odd, 0):
                        pe.wait_ge(sem.w_attn_in, m.w_attn_count(before))
                    if is_cur:
                        pe.wait_ge(sem.qk_read, cur.count + 1)
                    for j in range(2):
                        for c in range(KC):
                            mm = nc.tensor.matmul(qkv_ps[:, j], hT[:, nxt.slot, c], m.wqkv[:, c, j * INNER:(j + 1) * INNER],
                                                  start=(c == 0), stop=(c == KC - 1))
                    mm.then_inc(sem.qk_made, 1)
                if is_prv:
                    pe.wait_ge(sem.o_made, prv.count + 1)
                    if is_prv2:
                        pe.wait_ge(sem.x_added, prv.count)
                    for j in range(INNER // P):
                        mm = nc.tensor.transpose(out_ps[:, j * P:(j + 1) * P], o[:, j * P:(j + 1) * P], m.ident[:])
                    mm.then_inc(sem.oT_made, 1)
                if is_nxt:
                    if is_cur:
                        pe.wait_ge(sem.v_copied, cur.count + 1)
                    for c in range(KC):
                        mm = nc.tensor.matmul(qkv_ps[:, 2], hT[:, nxt.slot, c], m.wqkv[:, c, 2 * INNER:3 * INNER],
                                              start=(c == 0), stop=(c == KC - 1))
                    mm.then_inc(sem.v_made, 1)
                if is_prv:
                    pe.wait_ge(sem.oT_copied, prv.count + 1)
                    for j in range(INNER // P):
                        mm = nc.tensor.matmul(out_ps[:, 0:D], oT[:, j], m.wo[:, j], start=(j == 0), stop=(j == INNER // P - 1))
                    mm.then_inc(sem.out_made, 1)
            stepped(pe, step, -2, NT)

        @block.scalar
        def _(act):
            def step(pair, odd):
                cur, nxt, nxt2, prv = (tile_at(pair, before, odd, k) for k in (0, 1, 2, -1))
                is_cur, is_nxt, is_nxt2, is_prv = (exists(pair, odd, k) for k in (0, 1, 2, -1))
                if is_cur:
                    act.wait_ge(sem.qkT_made, 2 * cur.count + 1)
                    nc.scalar.copy(qT[:], ring[:, QT].rearrange("p (j t) -> p j t", t=P)).then_inc(sem.qkT_copied, 1)
                    act.wait_ge(sem.qkT_made, 2 * cur.count + 2)
                    nc.scalar.copy(kT[:, :, cur.slot], ring[:, KT].rearrange("p (j t) -> p j t", t=P)).then_inc(sem.qkT_copied, 1)
                if is_nxt2:
                    act.wait_ge(sem.hT_made, nxt2.count + 1)
                    nc.scalar.copy(hT[:, nxt2.slot], ring[:, HT, 0:D].rearrange("p (c t) -> p c t", t=P)).then_inc(sem.hT_copied, 1)
                if is_prv:
                    for n in range(4):
                        act.wait_ge(sem.pT_made, 4 * prv.count + n + 1)
                        a = HEAD_ORDER[2 * n]
                        nc.scalar.copy(probsT[:, a:a + 3:2], ring[:, PT[n]].rearrange("p (i b t) -> p i b t", i=2, b=2)).then_inc(sem.pT_copied, 1)
                if is_cur:
                    for n, head in enumerate(HEAD_ORDER):
                        if n % 4 == 0:
                            act.wait_ge(sem.nbias_made, 2 * cur.count + n // 4 + 1)
                        nc.scalar.activation(probs[:, cur.slot, head], scores[:, head], ACT.Exp,
                                             bias=nbias[:, cur.slot, head:head + 1], scale=rnorm[:, cur.slot, head:head + 1],
                                             accum_out=psum_row[:, cur.slot, head:head + 1]).then_inc(sem.probs_made, 1)
                if is_nxt:
                    act.wait_ge(sem.qk_made, nxt.count + 1)
                    if is_cur:
                        act.wait_ge(sem.ssq_made, cur.count + 1)
                    for j in range(2):
                        nc.scalar.activation(squares[:, j], qkv_ps[:, j], ACT.Square).then_inc(sem.squared, 1)
            stepped(act, step, -2, NT)

        @block.vector
        def _(dve):
            def step(pair, odd):
                cur, nxt, nxt2, prv = (tile_at(pair, before, odd, k) for k in (0, 1, 2, -1))
                is_cur, is_nxt, is_nxt2, is_prv = (exists(pair, odd, k) for k in (0, 1, 2, -1))
                if is_cur:
                    mask = m.mask_first if not is_prv else m.masks[:, cur.slot]
                    for n, head in enumerate(HEAD_ORDER):
                        if n % 2 == 0:
                            pass_gate(dve, sem, sem.scores_made, 4 * cur.count + n // 2 + 1)
                        c = n % 2
                        nc.vector.tensor_tensor_reduce(out=scores[:, head], in0=ring[:, SC[n // 2], c * 2 * P:(c + 1) * 2 * P], in1=mask,
                                                       scale=1.0, scalar=-3e38, op0=ALU.add, op1=ALU.max,
                                                       accum_out=smax[:, cur.slot, head:head + 1]).then_inc(sem.masked, 1)
                        if n % 4 == 3:
                            k = 4 * (n // 4)
                            dve.wait_ge(sem.masked, WH * cur.count + n + 1)
                            nc.vector.scalar_tensor_tensor(out=nbias[:, cur.slot, k:k + 4], in0=smax[:, cur.slot, k:k + 4], scalar=-1.0,
                                                           in1=rnorm[:, cur.slot, k:k + 4], op0=ALU.mult, op1=ALU.mult).then_inc(sem.nbias_made, 1)
                if is_prv:
                    dve.wait_ge(sem.probs_made, WH * prv.count + WH)
                    nc.vector.reciprocal(rsum[:, prv.slot], psum_row[:, prv.slot]).then_inc(sem.rsum_made, 1)
                    dve.wait_ge(sem.rsum_made, prv.count + 1)
                    dve.wait_ge(sem.o_summed, prv.count + 1)
                    nc.vector.tensor_tensor(o[:].rearrange("p (h d) -> p h d", d=WD), ring[:, OS].rearrange("p (h d) -> p h d", d=WD),
                                            rsum[:, prv.slot].unsqueeze(2).broadcast_to([P, WH, WD]), ALU.mult).then_inc(sem.o_made, 1)
                if is_cur:
                    dve.wait_ge(sem.v_made, cur.count + 1)
                    nc.vector.tensor_copy(v[:, cur.slot], qkv_ps[:, 2]).then_inc(sem.v_copied, 1)
                if is_prv:
                    dve.wait_ge(sem.oT_made, prv.count + 1)
                    nc.vector.tensor_copy(oT[:], out_ps[:].rearrange("p (j t) -> p j t", t=P)).then_inc(sem.oT_copied, 1)
                if is_nxt:
                    dve.wait_ge(sem.squared, 2 * nxt.count + 2)
                    dve.wait_ge(sem.rope_made, nxt.count + 1)
                    if is_cur:
                        dve.wait_ge(sem.qk_rotated, cur.count + 1)
                    raw = qkv_ps[:, 0:2].rearrange("p c (h d) -> p c h d", d=WD)
                    tab = rope[:, nxt.slot].rearrange("p (c f) d -> p c f d", f=2)
                    nc.vector.tensor_tensor(turned[:].rearrange("p c (h d) -> p c h d", d=WD), raw,
                                            tab[:, :, 0].unsqueeze(2).broadcast_to([P, 2, WH, WD]), ALU.mult)
                    cr = crossed[:].rearrange("p c (h d) -> p c h d", d=WD)
                    H = WD // 2
                    nc.vector.tensor_tensor(cr[:, :, :, 0:H], raw[:, :, :, H:WD],
                                            tab[:, :, 1, 0:H].unsqueeze(2).broadcast_to([P, 2, WH, H]), ALU.mult)
                    nc.vector.tensor_tensor(cr[:, :, :, H:WD], raw[:, :, :, 0:H],
                                            tab[:, :, 1, H:WD].unsqueeze(2).broadcast_to([P, 2, WH, H]), ALU.mult).then_inc(sem.qk_read, 1)
                    nc.vector.tensor_reduce(ssq[:, nxt.slot], squares[:].rearrange("p c (h d) -> p (c h) d", d=WD), AX.X, ALU.add).then_inc(sem.ssq_made, 1)
                if is_prv:
                    dve.wait_ge(sem.out_made, prv.count + 1)
                    nc.vector.tensor_tensor(X[:, prv.place], X[:, prv.place], out_ps[:, 0:D], ALU.add).then_inc(sem.x_added, 1)
            stepped(dve, step, -2, NT)

        @block.gpsimd
        def _(pool):
            def scale_tables(pair, odd, ahead):
                a = tile_at(pair, before, odd, ahead)
                pool.wait_ge(sem.rope_in[a.slot], 16 * a.turn + 16)
                if exists(pair, odd, ahead - 2):
                    pool.wait_ge(sem.qk_read, a.count - 1)
                nc.gpsimd.tensor_tensor(rope[:, a.slot], rope_raw[:, a.slot], m.scales[:], ALU.mult).then_inc(sem.rope_made, 1)

            def step(pair, odd):
                cur, nxt, prv = (tile_at(pair, before, odd, k) for k in (0, 1, -1))
                if exists(pair, odd, 2):
                    if not exists(pair, odd, 0) and not exists(pair, odd, 1):
                        pool.wait_ge(sem.w_attn_in, m.w_attn_count(before))
                    scale_tables(pair, odd, 2)
                if not exists(pair, odd, 1):
                    return
                pass_gate(pool, sem, sem.ssq_made, nxt.count + 1)
                nc.gpsimd.tensor_scalar(ssq[:, nxt.slot], ssq[:, nxt.slot], 1e-24, None, ALU.max).then_inc(sem.ssq_kept, 1)
                pool.wait_ge(sem.ssq_kept, nxt.count + 1)
                nc.gpsimd.tensor_tensor(rnorm[:, nxt.slot], ssq[:, nxt.slot], m.minus_half[:, 0:2 * WH], ALU.pow).then_inc(sem.rnorm_made, 1)
                if exists(pair, odd, 0):
                    pool.wait_ge(sem.qkT_made, 2 * cur.count + 2)
                nc.gpsimd.tensor_tensor(turned[:, 1], turned[:, 1], crossed[:, 1], ALU.add).then_inc(sem.k_turned, 1)
                nc.gpsimd.tensor_tensor(qk[:, 0], turned[:, 0], crossed[:, 0], ALU.add)
                pool.wait_ge(sem.rnorm_made, nxt.count + 1)
                pool.wait_ge(sem.k_turned, nxt.count + 1)
                nc.gpsimd.tensor_tensor(qk[:, 1].rearrange("p (h d) -> p h d", d=WD), turned[:, 1].rearrange("p (h d) -> p h d", d=WD),
                                        rnorm[:, nxt.slot, WH:2 * WH].unsqueeze(2).broadcast_to([P, WH, WD]), ALU.mult).then_inc(sem.qk_rotated, 1)

            nc.gpsimd.memset(kT[:, :, 1], 0.0).then_inc(sem.window_cleared, 1)
            nc.gpsimd.memset(v[:, 1], 0.0).then_inc(sem.window_cleared, 1)
            stepped(pool, step, -2, NT)


def mlp(nc, m, sem, before):
    widths = [min(P, HID - c * P) for c in range(NC)]
    with ExitStack() as ctx:
        def sb(name, shape, dt=F32):
            return ctx.enter_context(nc.sbuf_tensor(name + m.tag, shape, dt))

        def ps(name, shape, dt=F32):
            return ctx.enter_context(nc.psum_tensor(name + m.tag, shape, dt))

        X, h = m.X, sb("mh", [P, GT, D])
        stats = sb("stats", [P, GT, nc.vector.BN_STATS_DIM])
        mv = sb("mv", [P, GT, 2])
        shifted_var = sb("shifted_var", [P, GT])
        rstd = sb("rstd", [P, GT])
        hn = sb("hn", [P, GT, D])
        hT = sb("mhT", [P, KC, GW])
        gate = sb("gate", [P, 2, GW])
        u = sb("u", [P, NC, GW])
        xb = sb("xb", [P, GT, D])
        turn_ps = ps("turn_ps", [P, 2, 4, P])
        ag_ps = ps("ag_ps", [P, 2, 2, GW])
        y_ps = ps("y_ps", [P, 2, 512])

        block = ctx.enter_context(nc.Block())

        def groups(eng, body):
            with eng.Fori(0, NG - 1) as g:
                body(g, before + g, True)
            body(NG - 1, before + NG - 1, False)

        @block.sync
        def _(sp):
            def load(g, count, first):
                if not first:
                    sp.wait_ge(sem.ln_applied, GT * count)
                nc.sync.dma_start(h[:, :, 0:P], X[:, bass.ds(g * GT, GT), 0:P]).then_inc(sem.mh_in, 16)
                nc.sync.dma_start(h[1:P, :, P:D], X[0:P - 1, bass.ds(g * GT, GT), P:D]).then_inc(sem.mh_in, 16)
                before_group = m.zeros[0:1, 0:P] if first else X[P - 1:P, g * GT - 1, P:D]
                nc.sync.dma_start(h[0:1, 0, P:D], before_group).then_inc(sem.mh_in, 16)
                nc.sync.dma_start(h[0:1, 1:GT, P:D], X[P - 1:P, bass.ds(g * GT, GT - 1), P:D]).then_inc(sem.mh_in, 16)
            load(0, before, True)
            with sp.Fori(1, NG) as g:
                load(g, before + g, False)

        @block.tensor
        def _(pe):
            def turn(count):
                for t in range(GT):
                    pe.wait_ge(sem.ln_applied, GT * count + t + 1)
                    if t >= 2:
                        pe.wait_ge(sem.mhT_copied, GT * count + t - 1)
                    for c in range(KC):
                        mm = nc.tensor.transpose(turn_ps[:, t % 2, c], hn[:, t, c * P:(c + 1) * P], m.ident[:])
                    mm.then_inc(sem.mhT_made, 1)

            pe.wait_ge(sem.w_mlp_in, m.w_mlp_count(before))
            turn(before)

            def body(g, count, more):
                pe.wait_ge(sem.mhT_copied, GT * count + GT)
                for c, w in enumerate(widths):
                    if c >= 2:
                        pe.wait_ge(sem.u_made, NC * count + c - 1)
                    for half in range(2):
                        for k in range(KC):
                            mm = nc.tensor.matmul(ag_ps[0:w, c % 2, half], m.w1[:, k, half * HID + c * P:half * HID + c * P + w],
                                                  hT[:, k], start=(k == 0), stop=(k == KC - 1))
                    mm.then_inc(sem.ag_made, 1)
                if more:
                    turn(count + 1)
                for t in range(GT):
                    if t == 0:
                        pe.wait_ge(sem.u_made, NC * count + NC)
                    if t >= 2:
                        pe.wait_ge(sem.mx_added, GT * count + t - 1)
                    for c, w in enumerate(widths):
                        mm = nc.tensor.matmul(y_ps[:, t % 2, 0:D], u[0:w, c, t * P:(t + 1) * P], m.w2[0:w, c],
                                              start=(c == 0), stop=(c == NC - 1))
                    mm.then_inc(sem.y_made, 1)
            groups(pe, body)

        @block.scalar
        def _(act):
            act.wait_ge(sem.w_mlp_in, m.w_mlp_count(before))

            def body(g, count, more):
                for c, w in enumerate(widths):
                    act.wait_ge(sem.ag_made, NC * count + c + 1)
                    act.wait_ge(sem.u_made, NC * count + c - 1 if c >= 2 else NC * count)
                    nc.scalar.activation(gate[0:w, c % 2], ag_ps[0:w, c % 2, 1], ACT.Gelu, bias=m.b1[0:w, 1, c:c + 1],
                                         scale=1.0).then_inc(sem.gelu_made, 1)
            groups(act, body)

        @block.vector
        def _(dve):
            def layernorm(count):
                dve.wait_ge(sem.mh_in, 64 * count + 64)
                for t in range(GT):
                    nc.vector.bn_stats(stats[:, t], h[:, t]).then_inc(sem.stats_made, 1)
                for t in range(GT):
                    pass_gate(dve, sem, sem.stats_made, GT * count + t + 1)
                    nc.vector.bn_aggr(mv[:, t], stats[:, t]).then_inc(sem.mv_made, 1)
                dve.wait_ge(sem.rstd_made, count + 1)
                for t in range(GT):
                    nc.vector.tensor_scalar(hn[:, t], h[:, t], mv[:, t, 0:1], rstd[:, t:t + 1], ALU.subtract, ALU.mult).then_inc(sem.ln_applied, 1)

            def hidden(c, w, count):
                dve.wait_ge(sem.gelu_made, NC * count + c + 1)
                nc.vector.scalar_tensor_tensor(out=u[0:w, c], in0=ag_ps[0:w, c % 2, 0], scalar=m.b1[0:w, 0, c:c + 1],
                                               in1=gate[0:w, c % 2], op0=ALU.add, op1=ALU.mult).then_inc(sem.u_made, 1)

            def copy_turned(t, count):
                dve.wait_ge(sem.mhT_made, GT * count + t + 1)
                for k in range(KC):
                    mm = nc.vector.tensor_scalar(hT[:, k, t * P:(t + 1) * P], turn_ps[:, t % 2, k],
                                                 m.ln[:, 0, k:k + 1], m.ln[:, 1, k:k + 1], ALU.mult, ALU.add)
                mm.then_inc(sem.mhT_copied, 1)

            dve.wait_ge(sem.w_mlp_in, m.w_mlp_count(before))
            layernorm(before)
            for t in range(GT):
                copy_turned(t, before)

            def body(g, count, more):
                for c, w in enumerate(widths):
                    if c == 2 and more:
                        layernorm(count + 1)
                    if c == 0 and not isinstance(count, int) or c == 0 and count > before:
                        dve.wait_ge(sem.y_made, GT * count)
                    hidden(c, w, count)
                if more:
                    for t in range(GT):
                        copy_turned(t, count + 1)
                for t in range(GT):
                    dve.wait_ge(sem.y_made, GT * count + t + 1)
                    if t == 0:
                        dve.wait_ge(sem.xb_made, count + 1)
                    nc.vector.tensor_tensor(X[:, g * GT + t], xb[:, t], y_ps[:, t % 2, 0:D], ALU.add).then_inc(sem.mx_added, 1)
            groups(dve, body)

        @block.gpsimd
        def _(pool):
            def rstds(count):
                pass_gate(pool, sem, sem.mv_made, GT * count + GT)
                nc.gpsimd.tensor_scalar(shifted_var[:], mv[:, :, 1], EPS, None, ALU.add).then_inc(sem.eps_added, 1)
                pool.wait_ge(sem.eps_added, count + 1)
                nc.gpsimd.tensor_tensor(rstd[:], shifted_var[:], m.minus_half[:, 0:GT], ALU.pow).then_inc(sem.rstd_made, 1)
            pool.wait_ge(sem.w_mlp_in, m.w_mlp_count(before))
            rstds(before)

            def body(g, count, more):
                if not isinstance(count, int) or count > before:
                    pool.wait_ge(sem.mx_added, GT * count)
                nc.gpsimd.tensor_tensor(xb[:], X[:, bass.ds(g * GT, GT)], m.b2[:].unsqueeze(1).broadcast_to([P, GT, D]), ALU.add).then_inc(sem.xb_made, 1)
                if more:
                    rstds(count + 1)
            groups(pool, body)


CT = 8
NQ = NT // CT


def rejoin(nc, m, sem, base, scale, store, normalise):
    X = m.X
    with ExitStack() as ctx:
        def sb(name, shape, dt=F32):
            return ctx.enter_context(nc.sbuf_tensor(name + m.tag, shape, dt))

        part = sb("part", [P, 2, CT, D])
        stats = sb("jstats", [P, CT, nc.vector.BN_STATS_DIM])
        mv = sb("jmv", [P, CT, 2])
        shifted_var = sb("jvar", [P, CT])
        rstd = sb("jrstd", [P, CT])
        base_in = [ctx.enter_context(nc.semaphore(f"base_in{n}" + m.tag)) for n in range(NQ)]
        stored = [ctx.enter_context(nc.semaphore(f"stored{n}" + m.tag)) for n in range(NQ)]
        joined, stats_made, mv_made, eps_added, rstd_made = (
            ctx.enter_context(nc.semaphore(n + m.tag)) for n in ("joined", "jstats_made", "jmv_made", "jeps", "jrstd_made"))

        def chunk(dram, q):
            return dram.rearrange("(t p) d -> p t d", p=P)[:, q * CT:(q + 1) * CT]

        block = ctx.enter_context(nc.Block())

        @block.sync
        def _(sp):
            for q in range(NQ if base is not None else 0):
                if scale is None:
                    nc.sync.dma_start(X[:, q * CT:(q + 1) * CT], chunk(base, q)).then_inc(base_in[q], 16)
                    continue
                if q >= 2:
                    sp.wait_ge(joined, q - 1)
                nc.sync.dma_start(part[:, q % 2], chunk(base, q)).then_inc(base_in[q], 16)

        @block.scalar
        def _(act):
            if store is not None:
                for q in range(NQ):
                    act.wait_ge(joined, q + 1)
                    nc.scalar.dma_start(chunk(store, q), X[:, q * CT:(q + 1) * CT]).then_inc(stored[q], 16)
                for q in range(NQ):
                    act.wait_ge(stored[q], 16)

        @block.vector
        def _(dve):
            if scale is not None:
                for q in range(NQ):
                    dve.wait_ge(base_in[q], 16)
                    x = X[:, q * CT:(q + 1) * CT].rearrange("p t d -> p (t d)")
                    nc.vector.scalar_tensor_tensor(out=x, in0=x, scalar=scale, in1=part[:, q % 2].rearrange("p t d -> p (t d)"),
                                                   op0=ALU.mult, op1=ALU.add).then_inc(joined, 1)
            if normalise:
                for q in range(NQ):
                    if scale is None and base is not None:
                        dve.wait_ge(base_in[q], 16)
                    elif scale is not None:
                        dve.wait_ge(joined, q + 1)
                    if store is not None:
                        dve.wait_ge(stored[q], 16)
                    for t in range(CT):
                        nc.vector.bn_stats(stats[:, t], X[:, q * CT + t]).then_inc(stats_made, 1)
                    for t in range(CT):
                        dve.wait_ge(stats_made, CT * q + t + 1)
                        nc.vector.bn_aggr(mv[:, t], stats[:, t]).then_inc(mv_made, 1)
                    dve.wait_ge(rstd_made, q + 1)
                    for t in range(CT):
                        nc.vector.tensor_scalar(X[:, q * CT + t], X[:, q * CT + t], mv[:, t, 0:1], rstd[:, t:t + 1],
                                                ALU.subtract, ALU.mult)

        @block.gpsimd
        def _(pool):
            if normalise:
                for q in range(NQ):
                    pool.wait_ge(mv_made, CT * (q + 1))
                    nc.gpsimd.tensor_scalar(shifted_var[:], mv[:, :, 1], EPS, None, ALU.add).then_inc(eps_added, 1)
                    pool.wait_ge(eps_added, q + 1)
                    nc.gpsimd.tensor_tensor(rstd[:], shifted_var[:], m.minus_half[:, 0:CT], ALU.pow).then_inc(rstd_made, 1)


def project_heads(nc, m, sem):
    X = m.X
    with ExitStack() as ctx:
        def sb(name, shape, dt=F32):
            return ctx.enter_context(nc.sbuf_tensor(name, shape, dt))

        def ps(name, shape, dt=F32):
            return ctx.enter_context(nc.psum_tensor(name, shape, dt))

        names = """c_w_in c_xT_made c_xT_copied qk_summed v_summed v_biased qk_biased turned_made crossed_made rot_made high_made
            rest_made mid_made parts_made partsT_made partsT_copied""".split()
        (w_in, xT_made, xT_copied, qk_summed, v_summed, v_biased, qk_biased, turned_made, crossed_made, rot_made, high_made,
         rest_made, mid_made, parts_made, partsT_made, partsT_copied) = (ctx.enter_context(nc.semaphore(n)) for n in names)
        tile_in = [ctx.enter_context(nc.semaphore(f"c_tile_in{i}")) for i in range(2)]
        parts_out = [ctx.enter_context(nc.semaphore(f"c_parts_out{i}")) for i in range(2)]

        w = sb("c_w", [P, KC, 3 * D])
        bias = sb("c_bias", [P, 3 * D])
        x = sb("c_x", [P, 2, D])
        tab = sb("c_tab", [P, 2, 2, 2, HD])
        xT = sb("c_xT", [P, 2, KC, P])
        qkb = sb("c_qkb", [P, 2, 2, D])
        turned = sb("c_turned", [P, 2, 2, D])
        crossed = sb("c_crossed", [P, 2, 2, D])
        rot = sb("c_rot", [P, 2, 2, D])
        rest = sb("c_rest", [P, 2, 2, D])
        parts = sb("c_parts", [P, 2, 2, 3, D], BF16)
        partsT = sb("c_partsT", [P, 2, 12, P], BF16)
        xT_ps = ps("c_xT_ps", [P, 512])
        qk_ps = ps("c_qk_ps", [P, 2 * D])
        v_ps = ps("c_v_ps", [P, 512])
        partsT_ps = ps("c_partsT_ps", [P, 2, 8, P], BF16)

        block = ctx.enter_context(nc.Block())

        @block.sync
        def _(sp):
            nc.sync.dma_start(w[:], m.cwqkv_dram).then_inc(w_in, 16)
            nc.sync.dma_start(bias[:], m.cbias_dram.partition_broadcast(P)).then_inc(w_in, 16)

            def load(pair, odd):
                a = tile_at(pair, 0, odd)
                if exists(pair, odd, -2):
                    sp.wait_ge(xT_made, a.count - 1)
                    sp.wait_ge(crossed_made, a.count - 1)
                    sp.wait_ge(turned_made, a.count - 1)
                nc.sync.dma_start(x[:, a.slot], X[:, a.place]).then_inc(tile_in[a.slot], 16)
                nc.sync.dma_start(tab[:, a.slot], m.crope_dram[a.place]).then_inc(tile_in[a.slot], 16)

            def store(pair, odd):
                a = tile_at(pair, 0, odd)
                sp.wait_ge(partsT_copied, 2 * a.count + 2)
                nc.sync.dma_start(m.parts_dram.rearrange("a (b p) s -> p (a b) s", p=P)[:, :, bass.ts(a.place, P)],
                                  partsT[:, a.slot]).then_inc(parts_out[a.slot], 16)
            for s in range(4):
                load(s // 2, s % 2)
            with sp.Fori(2, NT // 2) as pair:
                for odd in range(2):
                    load(pair, odd)
                    store(pair - 2, odd)
            for s in range(NT - 4, NT):
                store(s // 2, s % 2)
            for slot in range(2):
                sp.wait_ge(parts_out[slot], 16 * (NT // 2))

        @block.tensor
        def _(pe):
            def step(pair, odd):
                if exists(pair, odd, 1):
                    a = tile_at(pair, 0, odd, 1)
                    pe.wait_ge(tile_in[a.slot], 32 * a.turn + 32)
                    if exists(pair, odd, 0):
                        pe.wait_ge(xT_copied, a.count)
                    for c in range(KC):
                        mm = nc.tensor.transpose(xT_ps[:, c * P:(c + 1) * P], x[:, a.slot, c * P:(c + 1) * P], m.ident[:])
                    mm.then_inc(xT_made, 1)
                if exists(pair, odd, 0):
                    a = tile_at(pair, 0, odd)
                    pe.wait_ge(xT_copied, a.count + 1)
                    if exists(pair, odd, -1):
                        pe.wait_ge(qk_biased, a.count)
                        pe.wait_ge(v_biased, a.count)
                    else:
                        pe.wait_ge(w_in, 32)
                    for c in range(KC):
                        mm = nc.tensor.matmul(qk_ps[:], xT[:, a.slot, c], w[:, c, 0:2 * D], start=(c == 0), stop=(c == KC - 1))
                    mm.then_inc(qk_summed, 1)
                    for c in range(KC):
                        mm = nc.tensor.matmul(v_ps[:, 0:D], xT[:, a.slot, c], w[:, c, 2 * D:3 * D], start=(c == 0), stop=(c == KC - 1))
                    mm.then_inc(v_summed, 1)
                if exists(pair, odd, -2):
                    a = tile_at(pair, 0, odd, -2)
                    pe.wait_ge(parts_made, a.count + 1)
                    for qk in range(2):
                        if exists(pair, odd, -3):
                            pe.wait_ge(partsT_copied, 2 * a.count)
                        for n in range(6):
                            mm = nc.tensor.transpose(partsT_ps[:, qk, n], parts[:, a.slot, qk, n // 2, (n % 2) * P:(n % 2 + 1) * P], m.identb[:])
                        mm.then_inc(partsT_made, 1)
            stepped(pe, step, -1, NT + 1)

        @block.scalar
        def _(act):
            def step(pair, odd):
                if exists(pair, odd, 1):
                    a = tile_at(pair, 0, odd, 1)
                    act.wait_ge(xT_made, a.count + 1)
                    nc.scalar.copy(xT[:, a.slot], xT_ps[:, 0:D].rearrange("p (c t) -> p c t", t=P)).then_inc(xT_copied, 1)
                if exists(pair, odd, -1):
                    a = tile_at(pair, 0, odd, -1)
                    act.wait_ge(rot_made, a.count + 1)
                    if exists(pair, odd, -3):
                        act.wait_ge(partsT_made, 2 * a.count - 2)
                    nc.scalar.copy(parts[:, a.slot, :, 0], rot[:, a.slot]).then_inc(high_made, 1)
                    act.wait_ge(rest_made, a.count + 1)
                    nc.scalar.copy(parts[:, a.slot, :, 1], rest[:, a.slot]).then_inc(mid_made, 1)
                if exists(pair, odd, -2):
                    a = tile_at(pair, 0, odd, -2)
                    if exists(pair, odd, -4):
                        act.wait_ge(parts_out[a.slot], 16 * a.turn)
                    for qk in range(2):
                        act.wait_ge(partsT_made, 2 * a.count + 1 + qk)
                        nc.scalar.copy(partsT[:, a.slot, 6 * qk:6 * qk + 6], partsT_ps[:, qk, 0:6]).then_inc(partsT_copied, 1)
            stepped(act, step, -1, NT + 1)

        @block.vector
        def _(dve):
            dve.wait_ge(w_in, 32)

            def step(pair, odd):
                if exists(pair, odd, 0):
                    a = tile_at(pair, 0, odd)
                    dve.wait_ge(qk_summed, a.count + 1)
                    if exists(pair, odd, -2):
                        dve.wait_ge(crossed_made, a.count - 1)
                    nc.vector.tensor_tensor(qkb[:, a.slot].rearrange("p c n -> p (c n)"), qk_ps[:], bias[:, 0:2 * D], ALU.add).then_inc(qk_biased, 1)
                    pass_gate(dve, sem, v_summed, a.count + 1)
                    nc.vector.tensor_tensor(m.V[:, a.place, :, 0:HD], v_ps[:, 0:D].rearrange("p (h d) -> p h d", d=HD),
                                            bias[:, 2 * D:3 * D].rearrange("p (h d) -> p h d", d=HD), ALU.add).then_inc(v_biased, 1)
                    if exists(pair, odd, -2):
                        dve.wait_ge(rot_made, a.count - 1)
                    dve.wait_ge(tile_in[a.slot], 32 * a.turn + 32)
                    dve.wait_ge(qk_biased, a.count + 1)
                    nc.vector.tensor_tensor(turned[:, a.slot].rearrange("p c (h d) -> p c h d", d=HD),
                                            qkb[:, a.slot].rearrange("p c (h d) -> p c h d", d=HD),
                                            tab[:, a.slot, :, 0].unsqueeze(2).broadcast_to([P, 2, NH, HD]), ALU.mult).then_inc(turned_made, 1)
                if exists(pair, odd, -1):
                    a = tile_at(pair, 0, odd, -1)
                    dve.wait_ge(high_made, a.count + 1)
                    nc.vector.tensor_tensor(rest[:, a.slot], rot[:, a.slot], parts[:, a.slot, :, 0], ALU.subtract).then_inc(rest_made, 1)
                    dve.wait_ge(mid_made, a.count + 1)
                    nc.vector.tensor_tensor(parts[:, a.slot, :, 2], rest[:, a.slot], parts[:, a.slot, :, 1], ALU.subtract).then_inc(parts_made, 1)
            stepped(dve, step, -1, NT + 1)

        @block.gpsimd
        def _(pool):
            nc.gpsimd.memset(m.V[:, :, :, HD:HD + 1], 1.0)

            def step(pair, odd):
                if not exists(pair, odd, 0):
                    return
                a = tile_at(pair, 0, odd)
                pool.wait_ge(tile_in[a.slot], 32 * a.turn + 32)
                pool.wait_ge(qk_biased, a.count + 1)
                if exists(pair, odd, -2):
                    pool.wait_ge(rot_made, a.count - 1)
                pairs = lambda t: t.rearrange("p c (n two) -> p c n two", two=2)
                for c in range(2):
                    for e in range(2):
                        mm = nc.gpsimd.tensor_tensor(
                            crossed[:, a.slot, c].rearrange("p (h n two) -> p h n two", two=2, h=NH)[:, :, :, e],
                            qkb[:, a.slot, c].rearrange("p (h n two) -> p h n two", two=2, h=NH)[:, :, :, 1 - e],
                            tab[:, a.slot, c, 1].rearrange("p (n two) -> p n two", two=2)[:, :, e].unsqueeze(1).broadcast_to([P, NH, HD // 2]), ALU.mult)
                mm.then_inc(crossed_made, 1)
                pool.wait_ge(crossed_made, a.count + 1)
                pool.wait_ge(turned_made, a.count + 1)
                if exists(pair, odd, -2):
                    pool.wait_ge(parts_made, a.count - 1)
                nc.gpsimd.tensor_tensor(rot[:, a.slot], turned[:, a.slot], crossed[:, a.slot], ALU.add).then_inc(rot_made, 1)
            stepped(pool, step, -1, NT + 1)


Q_PARTS = [0, 0, 0, 1, 1, 2]
K_PARTS = [0, 1, 2, 0, 1, 0]
SROWS = len(Q_PARTS) * HD
MROWS = SROWS + 3
PAIRS = [(g, j) for g in range(NG) for j in range(0, GT * (g + 1), 2)]
CHUNKS = [(t, c) for t in range(NT) for c in range(t // GT + 1)]
LEAD, TRAIL = 5, 5
FILL = [[] for _ in PAIRS]
for _i in range(len(CHUNKS)):
    FILL[LEAD + _i * (len(PAIRS) - LEAD - TRAIL) // len(CHUNKS)].append(_i)
TURN = len(PAIRS) - 3
FREE_ST, FREE_PROBS, FREE_O = 2, 4, 2
S_ITEMS = len(CHUNKS) + 1


def causal_attention(nc, m, sem):
    with ExitStack() as ctx:
        def sb(name, shape, dt=F32):
            return ctx.enter_context(nc.sbuf_tensor(name, shape, dt))

        def ps(name, shape, dt=F32):
            return ctx.enter_context(nc.psum_tensor(name, shape, dt))

        names = "s_made s_read st_made exp_made pv_done o_read v_in max_made split_made maxT_copied max_in max_row_in rows_set".split()
        (s_made, s_read, st_made, exp_made, pv_done, o_read, v_in, max_made, split_made, maxT_copied, max_in, max_row_in,
         rows_set) = (ctx.enter_context(nc.semaphore("d_" + n)) for n in names)
        stack_in = [ctx.enter_context(nc.semaphore(f"d_stack_in{i}")) for i in range(2)]

        q = sb("d_q", [P, 2, S], BF16)
        k = sb("d_k", [P, 2, S], BF16)
        probs = sb("d_probs", [P, 4, 2, GW])
        vh = sb("d_v", [P, 2, NT, HD + 1])
        chunk_max = sb("d_chunk_max", [P, NT, NG])
        neg_max = sb("d_neg_max", [P, NT])
        max_rest = sb("d_max_rest", [P, NT])
        max_parts = sb("d_max_parts", [P, 3, NT], BF16)
        maxT = sb("d_maxT", [3 * NT, P], BF16)
        st = ps("d_st", [P, 2, 2, GW])
        s_ps = ps("d_s", [P, 2, GW])
        o_ps = ps("d_o", [P, 2, 512])

        block = ctx.enter_context(nc.Block())

        def heads(eng, body):
            with eng.Fori(0, NH // 2 - 1) as pair:
                for b in range(2):
                    body(2 * pair + b, b, True)
            body(NH - 2, 0, True)
            body(NH - 1, 1, False)

        @block.sync
        def _(sp):
            def load(h, b):
                for n, part in enumerate(Q_PARTS):
                    nc.sync.dma_start(q[n * HD:(n + 1) * HD, b], m.parts_dram[part, bass.ds(h * HD, HD)]).then_inc(stack_in[b], 16)
                for n, part in enumerate(K_PARTS):
                    nc.sync.dma_start(k[n * HD:(n + 1) * HD, b], m.parts_dram[3 + part, bass.ds(h * HD, HD)]).then_inc(stack_in[b], 16)

            def max_rows(h, b):
                sp.wait_ge(maxT_copied, h + 1)
                nc.sync.dma_start(m.max_dram.rearrange("a (t c) -> (a t) c", c=P), maxT[:]).then_inc(max_row_in, 16)
                sp.wait_ge(max_row_in, 16 * h + 16)
                nc.sync.dma_start(q[SROWS:MROWS, b], m.max_dram).then_inc(max_in, 16)
            load(0, 0)
            load(1, 1)
            max_rows(0, 0)

            def body(h, b, more):
                if more:
                    max_rows(h + 1, 1 - b)
                if more and not (isinstance(h, int) and h + 2 >= NH):
                    sp.wait_ge(pv_done, FREE_PROBS + len(PAIRS) * (h + 1))
                    load(h + 2, b)
            heads(sp, body)

        @block.tensor
        def _(pe):
            def chunk(h, b, i):
                t, c = CHUNKS[i]
                w = min(GW, (t + 1) * P - c * GW)
                n = S_ITEMS * b + i
                slot = n % 2
                if i == 0:
                    pe.wait_ge(stack_in[b], 192 * (h // 2 if isinstance(h, int) else m.half(h, b)) + 192)
                if not (isinstance(h, int) and h == 0 and i < 2):
                    pe.wait_ge(s_read, S_ITEMS * h + i - 1)
                last = c == t // GT
                mm = nc.tensor.matmul(s_ps[:, slot, 0:w], q[0:SROWS, b, t * P:(t + 1) * P], k[0:SROWS, b, c * GW:c * GW + w],
                                      start=True, stop=not last)
                if last:
                    mm = nc.tensor.matmul(s_ps[:, slot, w - P:w], m.identb[:], m.cmask[:, 2], start=False, stop=True)
                mm.then_inc(s_made, 1)

            def turn_maxima(h, b):
                slot = (S_ITEMS * b + len(CHUNKS)) % 2
                pe.wait_ge(s_read, S_ITEMS * h + len(CHUNKS) - 1)
                pe.wait_ge(split_made, h + 1)
                nc.tensor.transpose(s_ps[0:3 * NT, slot, 0:P // 2].bitcast(BF16), max_parts[:].rearrange("p a t -> p (a t)"),
                                    m.identb[:]).then_inc(s_made, 1)

            def scores(h, b, n):
                g, j0 = PAIRS[n]
                col = P * max(0, j0 - GT * g)
                if n == 0:
                    pe.wait_ge(max_in, 16 * h + 16)
                pe.wait_ge(exp_made, FREE_ST + len(PAIRS) * h + n - 1)
                for j in range(2):
                    diagonal = j0 >= GT * g
                    mm = nc.tensor.matmul(st[:, n % 2, j, col:GW], k[0:MROWS, b, (j0 + j) * P:(j0 + j + 1) * P],
                                          q[0:MROWS, b, g * GW + col:(g + 1) * GW], start=True, stop=not diagonal)
                    if diagonal:
                        mm = nc.tensor.matmul(st[:, n % 2, j, col:col + P * (j + 1)], m.identb[:],
                                              m.cmask[:, 1 - j:2].rearrange("p a i -> p (a i)"), start=False, stop=True)
                mm.then_inc(st_made, 1)

            def sum_values(h, b, n):
                g, j0 = PAIRS[n]
                pe.wait_ge(exp_made, FREE_ST + len(PAIRS) * h + n + 1)
                if n == 0:
                    pe.wait_ge(v_in, h + 1)
                if j0 == 0:
                    pe.wait_ge(o_read, FREE_O + NG * h + g - 1)
                for j in range(j0, j0 + 2):
                    for t in range(max(j, GT * g), GT * (g + 1)):
                        i = t % GT
                        mm = nc.tensor.matmul(o_ps[:, g % 2, i * (HD + 1):(i + 1) * (HD + 1)], probs[:, n % 4, j - j0, i * P:(i + 1) * P],
                                              vh[:, b, j], start=(j == 0 and i == 0), stop=(j == t), skip_group_check=True)
                mm.then_inc(pv_done, 1)

            pe.sem_inc(pv_done, FREE_PROBS)
            pe.wait_ge(rows_set, 2)
            for i in range(len(CHUNKS)):
                chunk(0, 0, i)
            turn_maxima(0, 0)

            def body(h, b, more):
                scores(h, b, 0)
                for n in range(len(PAIRS)):
                    if n + 1 < len(PAIRS):
                        scores(h, b, n + 1)
                    if more:
                        for i in FILL[n]:
                            chunk(h + 1, 1 - b, i)
                        if n == TURN:
                            turn_maxima(h + 1, 1 - b)
                    sum_values(h, b, n)
            heads(pe, body)

        @block.scalar
        def _(act):
            act.sem_inc(exp_made, FREE_ST)

            def body(h, b, more):
                for n, (g, j0) in enumerate(PAIRS):
                    col = P * max(0, j0 - GT * g)
                    act.wait_ge(st_made, len(PAIRS) * h + n + 1)
                    act.wait_ge(pv_done, FREE_PROBS + len(PAIRS) * h + n - 3)
                    nc.scalar.activation(probs[:, n % 4, :, col:GW], st[:, n % 2, :, col:GW], ACT.Exp).then_inc(exp_made, 1)
            heads(act, body)

        @block.vector
        def _(dve):
            def chunk_maxima(h, b, i):
                t, c = CHUNKS[i]
                w = min(GW, (t + 1) * P - c * GW)
                dve.wait_ge(s_made, S_ITEMS * h + i + 1)
                nc.vector.tensor_reduce(chunk_max[:, t, c:c + 1], s_ps[:, (S_ITEMS * b + i) % 2, 0:w], AX.X, ALU.max).then_inc(s_read, 1)

            def split_maxima(h):
                dve.wait_ge(s_read, S_ITEMS * h + len(CHUNKS))
                nc.vector.tensor_reduce(neg_max[:], chunk_max[:], AX.X, ALU.max, negate=True).then_inc(max_made, 1)
                dve.wait_ge(max_made, 4 * h + 1)
                nc.vector.tensor_copy(max_parts[:, 0], neg_max[:]).then_inc(max_made, 1)
                dve.wait_ge(max_made, 4 * h + 2)
                nc.vector.tensor_tensor(max_rest[:], neg_max[:], max_parts[:, 0], ALU.subtract).then_inc(max_made, 1)
                dve.wait_ge(max_made, 4 * h + 3)
                nc.vector.tensor_copy(max_parts[:, 1], max_rest[:]).then_inc(max_made, 1)
                dve.wait_ge(max_made, 4 * h + 4)
                nc.vector.tensor_tensor(max_parts[:, 2], max_rest[:], max_parts[:, 1], ALU.subtract).then_inc(split_made, 1)

            def copy_turned(h, b):
                dve.wait_ge(s_made, S_ITEMS * h + S_ITEMS)
                slot = (S_ITEMS * b + len(CHUNKS)) % 2
                if not (isinstance(h, int) and h == 0):
                    dve.wait_ge(max_row_in, 16 * h)
                nc.vector.tensor_copy(maxT[:], s_ps[0:3 * NT, slot, 0:P // 2].bitcast(BF16)).then_inc(s_read, 1)
                dve.wait_ge(s_read, S_ITEMS * h + S_ITEMS)
                dve.sem_inc(maxT_copied, 1)

            def read_sums(h, g):
                pass_gate(dve, sem, pv_done, FREE_PROBS + len(PAIRS) * h + PAIRS.index((g, GT * (g + 1) - 2)) + 1)
                nc.vector.tensor_copy(m.O[:, GT * g:GT * (g + 1), h], o_ps[:, g % 2, 0:GT * (HD + 1)].rearrange("p (t d) -> p t d", t=GT)).then_inc(o_read, 1)

            dve.sem_inc(o_read, FREE_O)
            nc.vector.memset(k[SROWS:MROWS], 1.0).then_inc(rows_set, 1)
            nc.vector.memset(chunk_max[:], -3e38).then_inc(rows_set, 1)
            dve.wait_ge(rows_set, 2)
            for i in range(len(CHUNKS)):
                chunk_maxima(0, 0, i)
            split_maxima(0)
            copy_turned(0, 0)

            def body(h, b, more):
                for n in range(len(PAIRS)):
                    if more:
                        for i in FILL[n]:
                            chunk_maxima(h + 1, 1 - b, i)
                        if FILL[n] and FILL[n][-1] == len(CHUNKS) - 1:
                            split_maxima(h + 1)
                        if n == TURN:
                            copy_turned(h + 1, 1 - b)
                    g, j0 = PAIRS[n - 1]
                    if n and j0 == GT * (g + 1) - 2:
                        read_sums(h, g)
                read_sums(h, NG - 1)
            heads(dve, body)

        @block.gpsimd
        def _(pool):
            nc.gpsimd.tensor_copy(vh[:, 0], m.V[:, :, 0]).then_inc(v_in, 1)

            def body(h, b, more):
                if more:
                    pass_gate(pool, sem, pv_done, FREE_PROBS + len(PAIRS) * h)
                    nc.gpsimd.tensor_copy(vh[:, 1 - b], m.V[:, :, h + 1]).then_inc(v_in, 1)
            heads(pool, body)


def project_out(nc, m, sem):
    X = m.X
    with ExitStack() as ctx:
        def sb(name, shape, dt=F32):
            return ctx.enter_context(nc.sbuf_tensor(name, shape, dt))

        def ps(name, shape, dt=F32):
            return ctx.enter_context(nc.psum_tensor(name, shape, dt))

        names = "e_w_in recip_made o_made oT_made oT_copied y_made base_made joined".split()
        w_in, recip_made, o_made, oT_made, oT_copied, y_made, base_made, joined = (ctx.enter_context(nc.semaphore("e_" + n)) for n in names)
        mid_in, late_out = ([ctx.enter_context(nc.semaphore(f"e_{n}{i}")) for i in range(2)] for n in ("mid_in", "late_out"))
        w = sb("e_w", [P, KC, D])
        bias = sb("e_bias", [P, D])
        recip = sb("e_recip", [P, 2, NH])
        o = sb("e_o", [P, 2, D])
        oT = sb("e_oT", [P, 2, KC, P])
        mid = sb("e_mid", [P, 2, D])
        base = sb("e_base", [P, 2, D])
        late = sb("e_late", [P, 2, D])
        oT_ps = ps("e_oT_ps", [P, 2, 512])
        y_ps = ps("e_y_ps", [P, 2, 512])
        block = ctx.enter_context(nc.Block())

        @block.sync
        def _(sp):
            nc.sync.dma_start(w[:], m.cwo_dram).then_inc(w_in, 16)
            nc.sync.dma_start(bias[:], m.cbo_dram.partition_broadcast(P)).then_inc(w_in, 16)

            def load(pair, odd):
                a = tile_at(pair, 0, odd)
                if exists(pair, odd, -2):
                    sp.wait_ge(base_made, a.count - 1)
                nc.sync.dma_start(mid[:, a.slot], m.mid_dram[bass.ts(a.place, P)]).then_inc(mid_in[a.slot], 16)
            for s in range(2):
                load(s // 2, s % 2)
            with sp.Fori(1, NT // 2) as pair:
                for odd in range(2):
                    load(pair, odd)

        @block.tensor
        def _(pe):
            def step(pair, odd):
                if exists(pair, odd, 0):
                    a = tile_at(pair, 0, odd)
                    pe.wait_ge(o_made, a.count + 1)
                    if exists(pair, odd, -2):
                        pe.wait_ge(oT_copied, a.count - 1)
                    for c in range(KC):
                        mm = nc.tensor.transpose(oT_ps[:, a.slot, c * P:(c + 1) * P], o[:, a.slot, c * P:(c + 1) * P], m.ident[:])
                    mm.then_inc(oT_made, 1)
                if exists(pair, odd, -1):
                    a = tile_at(pair, 0, odd, -1)
                    pe.wait_ge(oT_copied, a.count + 1)
                    if exists(pair, odd, -3):
                        pe.wait_ge(joined, a.count - 1)
                    else:
                        pe.wait_ge(w_in, 32)
                    for c in range(KC):
                        mm = nc.tensor.matmul(y_ps[:, a.slot, 0:D], oT[:, a.slot, c], w[:, c], start=(c == 0), stop=(c == KC - 1))
                    mm.then_inc(y_made, 1)
            stepped(pe, step, 0, NT)

        @block.scalar
        def _(act):
            def step(pair, odd):
                if exists(pair, odd, 0):
                    a = tile_at(pair, 0, odd)
                    act.wait_ge(oT_made, a.count + 1)
                    if exists(pair, odd, -2):
                        act.wait_ge(y_made, a.count - 1)
                    nc.scalar.copy(oT[:, a.slot], oT_ps[:, a.slot, 0:D].rearrange("p (c t) -> p c t", t=P)).then_inc(oT_copied, 1)
                if exists(pair, odd, -1):
                    a = tile_at(pair, 0, odd, -1)
                    act.wait_ge(joined, a.count + 1)
                    nc.scalar.dma_start(m.late_dram[bass.ts(a.place, P)], late[:, a.slot]).then_inc(late_out[a.slot], 16)
            stepped(act, step, 0, NT)
            for slot in range(2):
                act.wait_ge(late_out[slot], 16 * (NT // 2))

        @block.vector
        def _(dve):
            def step(pair, odd):
                if exists(pair, odd, 0):
                    a = tile_at(pair, 0, odd)
                    nc.vector.reciprocal(recip[:, a.slot], m.O[:, a.place, :, HD]).then_inc(recip_made, 1)
                    pass_gate(dve, sem, recip_made, a.count + 1)
                    if exists(pair, odd, -2):
                        pass_gate(dve, sem, oT_made, a.count - 1)
                    nc.vector.tensor_tensor(o[:, a.slot].rearrange("p (h d) -> p h d", d=HD), m.O[:, a.place, :, 0:HD],
                                            recip[:, a.slot].unsqueeze(2).broadcast_to([P, NH, HD]), ALU.mult).then_inc(o_made, 1)
                if exists(pair, odd, -1):
                    a = tile_at(pair, 0, odd, -1)
                    dve.wait_ge(base_made, a.count + 1)
                    if exists(pair, odd, -3):
                        dve.wait_ge(late_out[a.slot], 16 * a.turn)
                    dve.wait_ge(y_made, a.count + 1)
                    nc.vector.tensor_tensor(late[:, a.slot], base[:, a.slot], y_ps[:, a.slot, 0:D], ALU.add).then_inc(joined, 1)
                    pass_gate(dve, sem, joined, a.count + 1)
                    nc.vector.tensor_copy(X[:, a.place], late[:, a.slot])
            stepped(dve, step, 0, NT)

        @block.gpsimd
        def _(pool):
            pool.wait_ge(w_in, 32)

            def step(pair, odd):
                if exists(pair, odd, 0):
                    a = tile_at(pair, 0, odd)
                    pool.wait_ge(mid_in[a.slot], 16 * a.turn + 16)
                    if exists(pair, odd, -2):
                        pool.wait_ge(joined, a.count - 1)
                    nc.gpsimd.tensor_tensor(base[:, a.slot], mid[:, a.slot], bias[:], ALU.add).then_inc(base_made, 1)
            stepped(pool, step, 0, NT)


ATTENTION_SEMS = """h_in:2 rope_in:2 w_attn_in rope_made hT_made hT_copied qkT_made qkT_copied pT_made pT_copied
    scores_made masked nbias_made probs_made rsum_made o_summed o_made oT_made oT_copied out_made x_added
    qk_made v_made v_copied squared qk_read ssq_made ssq_kept rnorm_made k_turned qk_rotated window_cleared""".split()
MLP_SEMS = """mh_in w_mlp_in stats_made mv_made eps_added rstd_made ln_applied mhT_made mhT_copied ag_made gelu_made
    u_made y_made xb_made mx_added""".split()


class Memory:
    pass


def window_masks():
    i, j = np.arange(P)[:, None], np.arange(P)[None, :]
    own = np.where(j > i, NEG, 0.0)
    past = np.where(j < i, NEG, 0.0)
    even, odd = np.concatenate([own, past], 1), np.concatenate([past, own], 1)
    first = np.concatenate([own, np.full((P, P), NEG)], 1)
    return np.stack([even, odd, first], 1).astype(np.float32)


def window_tables():
    half = np.arange(0, WD, 2, dtype=np.float32)
    inv = (np.float32(1.0) / np.float32(10000.0) ** (half / np.float32(WD))).astype(np.float32)
    t = np.arange(S, dtype=np.float32)
    freqs = t[:, None] * inv[None, :]
    base = (half + np.float32(0.4 * WD)) / np.float32(1.4 * WD)
    power = (t - np.float32(S // 2)) / np.float32(P // 2)
    scale = base[None, :].astype(np.float64) ** power[:, None].astype(np.float64)
    two = lambda a: np.concatenate([a, a], -1)
    cos, sin = two(np.cos(freqs.astype(np.float64))), np.sin(freqs.astype(np.float64))
    sin = np.concatenate([-sin, sin], -1)
    scale = two(scale)
    tables = np.stack([8.0 * cos * scale, 8.0 * sin * scale, cos / scale, sin / scale], 1)
    return np.ascontiguousarray(tables.reshape(NT, P, 4, WD).astype(np.float32))


def build(nc, a, out, stage=99):
    with ExitStack() as ctx:
        m, made = Memory(), {}

        def sb(name, shape, dt=F32):
            return ctx.enter_context(nc.sbuf_tensor(name, shape, dt))

        for name in ATTENTION_SEMS + MLP_SEMS + ["consts_in", "gates_passed"]:
            name, _, n = name.partition(":")
            each = [ctx.enter_context(nc.semaphore(name + (str(i) if n else ""))) for i in range(int(n or 1))]
            made[name] = each if n else each[0]
        sem = namedtuple("Semaphores", made)(**made)

        m.X = sb("X", [P, NT, D])
        m.ident = sb("ident", [P, P])
        m.identb = sb("identb", [P, P], BF16)
        m.cmask = sb("cmask", [P, 3, P], BF16)
        m.masks = sb("masks", [P, 3, 2 * P])
        m.mask_first = m.masks[:, 2]
        m.zeros = sb("zeros", [1, P])
        m.minus_half = sb("minus_half", [P, 2 * WH])
        m.wqkv = sb("wqkv", [P, KC, 3 * INNER])
        m.wo = sb("wo", [P, INNER // P, D])
        m.scales = sb("scales", [P, 4, WD])
        m.w1 = sb("w1", [P, KC, 2 * HID])
        m.w2 = sb("w2", [P, NC, D])
        m.b1 = sb("b1", [P, 2, NC])
        m.ln = sb("ln", [P, 2, KC])
        m.b2 = sb("b2", [P, D])

        m.wqkv_dram = a["wqkv"].rearrange("l (c p) n -> l p c n", p=P)
        m.wo_dram = a["wo"].rearrange("l (c p) n -> l p c n", p=P)
        m.scales_dram = a["scales"]
        m.rope_dram = a["rope"]
        m.cwqkv_dram = a["cwqkv"].rearrange("(c p) n -> p c n", p=P)
        m.cwo_dram = a["cwo"].rearrange("(c p) n -> p c n", p=P)
        m.cbias_dram, m.cbo_dram, m.crope_dram = a["cbias"], a["cbo"], a["crope"]
        m.mid_dram = nc.dram_tensor("mid_dram", [S, D], F32).ap()
        m.late_dram = nc.dram_tensor("late_dram", [S, D], F32).ap()
        m.max_dram = nc.dram_tensor("max_dram", [3, S], BF16).ap()
        m.parts_dram = nc.dram_tensor("parts_dram", [6, D, S], BF16).ap()

        full = HID // P * P
        def mlp_weights(l):
            loads = [(m.w1[:], a["w1"].rearrange("l (c p) n -> l p c n", p=P)[l]),
                     (m.w2[:, 0:NC - 1], a["w2"][:, 0:full].rearrange("l (c p) n -> l p c n", p=P)[l]),
                     (m.w2[0:HID - full, NC - 1], a["w2"][l, full:HID]),
                     (m.ln[:], a["ln"][l]),
                     (m.b1[:], a["b1"][l]),
                     (m.b2[:], a["b2"][l].partition_broadcast(P))]
            return loads
        m.mlp_weights = mlp_weights
        m.half = lambda h, b: (h - b) // 2
        m.w_mlp_count = lambda before: before * (16 * 6 // NG) + 96
        m.w_attn_count = lambda before: before * (48 // (NT // 2)) + 48

        with nc.Block() as block:
            @block.sync
            def _(sp):
                nc.sync.dma_start(m.ident[:], a["ident"]).then_inc(sem.consts_in, 16)
                nc.sync.dma_start(m.masks[:], a["masks"]).then_inc(sem.consts_in, 16)
                nc.sync.dma_start(m.identb[:], a["identb"]).then_inc(sem.consts_in, 16)
                nc.sync.dma_start(m.cmask[:], a["cmask"]).then_inc(sem.consts_in, 16)
                sp.wait_ge(sem.consts_in, 64)

            @block.gpsimd
            def _(pool):
                nc.gpsimd.memset(m.zeros[:], 0.0)
                nc.gpsimd.memset(m.minus_half[:], -0.5)

        def stack(call):
            with nc.Fori(0, DEPTH) as layer:
                m.layer = layer
                m.tag = f"_s{call}"
                window_attention(nc, m, sem, (call * DEPTH + layer) * (NT // 2))
                mlp(nc, m, sem, (call * DEPTH + layer) * NG)

        m.tag = "_in"
        rejoin(nc, m, sem, a["x"], None, None, True)
        stack(0)
        m.tag = "_mid"
        rejoin(nc, m, sem, a["x"], 0.5, m.mid_dram, True)
        with nc.sbuf_tensor("V", [P, NT, NH, HD + 1], F32) as m.V:
            project_heads(nc, m, sem)
            with nc.sbuf_tensor("O", [P, NT, NH, HD + 1], F32) as m.O:
                causal_attention(nc, m, sem)
                project_out(nc, m, sem)
        m.tag = "_late"
        rejoin(nc, m, sem, None, None, None, True)
        stack(1)
        m.tag = "_out"
        rejoin(nc, m, sem, m.late_dram, 0.5, out, False)


def causal_tables():
    dim = np.arange(HD // 2, dtype=np.float32)
    div = np.exp((np.float32(2.0) * dim / np.float32(HD) * np.float32(np.log(10000.0))).astype(np.float32)).astype(np.float32)
    theta = (np.arange(S, dtype=np.float32)[:, None] / div[None, :]).astype(np.float32).astype(np.float64)
    cos = np.repeat(np.cos(theta), 2, -1)
    sin = np.stack([-np.sin(theta), np.sin(theta)], -1).reshape(S, HD)
    both = np.stack([cos, sin], 1)
    tables = np.stack([both * HD ** -0.5, both], 1)
    return np.ascontiguousarray(tables.reshape(NT, P, 2, 2, HD).astype(np.float32))


def causal_masks():
    i, j = np.arange(P)[:, None], np.arange(P)[None, :]
    masks = np.stack([np.full((P, P), NEG), np.where(i > j, NEG, 0.0), np.where(j > i, NEG, 0.0)], 1)
    return np.ascontiguousarray(masks.astype(mybir.dt.np(BF16)))


def arrays(i):
    f = lambda n: np.ascontiguousarray(i["L0_" + n])
    swap = lambda s: np.concatenate([s[:, WD // 2:], s[:, :WD // 2]], 1)
    qs, ks = f("ffn_q_scale"), f("ffn_k_scale")
    b1 = np.zeros((DEPTH, 2, NC * P), np.float32)
    b1[:, :, :HID] = f("ffn_b1").reshape(DEPTH, 2, HID)
    b1 = np.ascontiguousarray(b1.reshape(DEPTH, 2, NC, P).transpose(0, 3, 1, 2))
    ln = np.stack([f("ffn_ln_g"), f("ffn_ln_b")], 1).reshape(DEPTH, 2, KC, P)
    return {
        "x": f("attn_x").reshape(S, D),
        "wqkv": f("ffn_wqkv"), "wo": f("ffn_wo"), "scales": np.ascontiguousarray(np.stack([qs, swap(qs), ks, swap(ks)], 1)),
        "w1": f("ffn_w1"), "b1": b1, "w2": f("ffn_w2"), "b2": f("ffn_b2"), "ln": np.ascontiguousarray(ln.transpose(0, 3, 1, 2)),
        "cwqkv": np.ascontiguousarray(np.concatenate([f("attn_wq").T, f("attn_wk").T, f("attn_wv").T], 1)),
        "cbias": np.concatenate([f("attn_bq"), f("attn_bk"), f("attn_bv")]), "cwo": np.ascontiguousarray(f("attn_wo").T), "cbo": f("attn_bo"),
        "crope": causal_tables(), "cmask": causal_masks(), "identb": np.eye(P, dtype=mybir.dt.np(BF16)),
        "rope": window_tables(), "masks": window_masks(), "ident": np.eye(P, dtype=np.float32),
    }


def kernel(**inputs):
    import concourse.bacc as bacc
    from concourse.bass_utils import run_bass_kernel_spmd

    nc = bacc.Bacc("TRN2", target_bir_lowering=False, num_devices=1)
    laid_out = arrays({name: np.asarray(v) for name, v in inputs.items()})
    tensors = {name: nc.dram_tensor(f"in_{name}_dram", v.shape, mybir.dt.from_np(v.dtype), kind="ExternalInput").ap()
               for name, v in laid_out.items()}
    out = nc.dram_tensor("out_dram", [S, D], F32, kind="ExternalOutput").ap()
    build(nc, tensors, out)
    result = run_bass_kernel_spmd(nc, [{f"in_{name}_dram": v for name, v in laid_out.items()}], core_ids=[0])
    return result.results[0]["out_dram"].reshape(1, S, D)
```

```python
from collections import namedtuple
from contextlib import ExitStack

import numpy as np
import concourse.bass as bass
from concourse import mybir

F32 = mybir.dt.float32
BF16 = mybir.dt.bfloat16
ALU = mybir.AluOpType
ACT = mybir.ActivationFunctionType
AX = mybir.AxisListType

P = 128
D = 256
KC = D // P
S = 4096
NT = S // P
DEPTH = 2
WH = 8
WD = 64
INNER = WH * WD
HID = int(D * 4 * 2 / 3)
NC = -(-HID // P)
NH = 16
HD = D // NH
GT = 4
NG = NT // GT
GW = GT * P
NEG = -1e30
EPS = 1e-5

Tile = namedtuple("Tile", "place count slot turn")


def tile_at(pair, before, odd, ahead=0):
    p, slot = pair + (odd + ahead) // 2, (odd + ahead) % 2
    return Tile(2 * p + slot, 2 * (p + before) + slot, slot, p + before)


def exists(pair, odd, ahead):
    return not isinstance(pair, int) or 0 <= 2 * pair + odd + ahead < NT


def pass_gate(eng, sem, semaphore, value):
    eng.wait_ge(semaphore, value)
    eng.sem_inc(sem.gates_passed, 1)


def stepped(eng, step, first, last):
    for s in range(first, 2):
        step(s // 2, s % 2)
    with eng.Fori(1, NT // 2 - 1) as pair:
        for odd in range(2):
            step(pair, odd)
    for s in range(NT - 2, last + 1):
        step(s // 2, s % 2)


def window_attention(nc, m, sem, before):
    with ExitStack() as ctx:
        def sb(name, shape, dt=F32):
            return ctx.enter_context(nc.sbuf_tensor(name + m.tag, shape, dt))

        def ps(name, shape, dt=F32):
            return ctx.enter_context(nc.psum_tensor(name + m.tag, shape, dt))

        X, h = m.X, sb("h", [P, 2, D])
        hT = sb("hT", [P, 2, KC, P])
        rope_raw = sb("rope_raw", [P, 2, 4, WD])
        rope = sb("rope", [P, 2, 4, WD])
        squares = sb("squares", [P, 2, INNER])
        ssq = sb("ssq", [P, 2, 2 * WH])
        rnorm = sb("rnorm", [P, 2, 2 * WH])
        turned = sb("turned", [P, 2, INNER])
        crossed = sb("crossed", [P, 2, INNER])
        qk = sb("qk", [P, 2, INNER])
        qT = sb("qT", [P, WH // 2, 2, P])
        kT = sb("kT", [P, WH // 2, 2, P])
        v = sb("v", [P, 2, INNER])
        scores = sb("scores", [P, WH, 2 * P])
        smax = sb("smax", [P, 2, WH])
        nbias = sb("nbias", [P, 2, WH])
        probs = sb("probs", [P, 2, WH, 2 * P])
        psum_row = sb("psum_row", [P, 2, WH])
        rsum = sb("rsum", [P, 2, WH])
        probsT = sb("probsT", [P, WH, 2, P])
        oT = sb("oT", [P, INNER // P, P])

        qkv_ps = ps("qkv_ps", [P, 3, INNER])
        o_ps = ps("o_ps", [P, INNER // P, P])
        ring = ps("ring", [P, 4, INNER])
        QT, KT, HT = 0, 1, 2
        PT = [3, 0, 1, 2]
        SC = [3, 0, 1, 2]
        OUT = 3

        block = ctx.enter_context(nc.Block())

        @block.sync
        def _(sp):
            nc.sync.dma_start(m.wqkv[:], m.wqkv_dram[m.layer]).then_inc(sem.w_attn_in, 16)
            nc.sync.dma_start(m.scales[:], m.scales_dram[m.layer].partition_broadcast(P)).then_inc(sem.w_attn_in, 16)
            nc.sync.dma_start(m.wo[:], m.wo_dram[m.layer]).then_inc(sem.w_attn_in, 16)

            def load(pair, odd):
                a = tile_at(pair, before, odd)
                if exists(pair, odd, -2):
                    sp.wait_ge(sem.hT_made, a.count - 1)
                    sp.wait_ge(sem.rope_made, a.count - 1)
                nc.sync.dma_start(h[:, a.slot, 0:P], X[:, a.place, 0:P]).then_inc(sem.h_in[a.slot], 16)
                nc.sync.dma_start(h[1:P, a.slot, P:D], X[0:P - 1, a.place, P:D]).then_inc(sem.h_in[a.slot], 16)
                last = m.zeros[0:1, 0:P] if not exists(pair, odd, -1) else X[P - 1:P, a.place - 1, P:D]
                nc.sync.dma_start(h[0:1, a.slot, P:D], last).then_inc(sem.h_in[a.slot], 16)
                nc.sync.dma_start(rope_raw[:, a.slot], m.rope_dram[a.place]).then_inc(sem.rope_in[a.slot], 16)
            for s in range(2):
                load(s // 2, s % 2)
            with sp.Fori(1, NT // 2) as pair:
                for odd in range(2):
                    load(pair, odd)
            for dst, src in m.mlp_weights(m.layer):
                nc.sync.dma_start(dst, src).then_inc(sem.w_mlp_in, 16)

        @block.tensor
        def _(pe):
            def step(pair, odd):
                cur, nxt, nxt2, prv = (tile_at(pair, before, odd, k) for k in (0, 1, 2, -1))
                is_cur, is_nxt, is_nxt2, is_prv = (exists(pair, odd, k) for k in (0, 1, 2, -1))
                is_prv2 = exists(pair, odd, -2)
                if is_cur:
                    pe.wait_ge(sem.qk_rotated, cur.count + 1)
                    for c, slot in ((0, QT), (1, KT)):
                        if is_prv:
                            pe.wait_ge(sem.masked, WH * prv.count + 4 + 2 * c)
                        for j in range(WH // 2):
                            mm = nc.tensor.transpose(ring[:, slot, j * P:(j + 1) * P], qk[:, c, j * P:(j + 1) * P], m.ident[:])
                        mm.then_inc(sem.qkT_made, 1)
                if is_nxt2:
                    pe.wait_ge(sem.h_in[nxt2.slot], 48 * nxt2.turn + 48)
                    if is_prv:
                        pe.wait_ge(sem.masked, WH * prv.count + 8)
                    elif is_nxt:
                        pe.wait_ge(sem.hT_copied, nxt.count + 1)
                    for c in range(KC):
                        mm = nc.tensor.transpose(ring[:, HT, c * P:(c + 1) * P], h[:, nxt2.slot, c * P:(c + 1) * P], m.ident[:])
                    mm.then_inc(sem.hT_made, 1)
                if is_prv:
                    for n in range(WH // 2):
                        pe.wait_ge(sem.probs_normal, WH * prv.count + 2 * n + 2)
                        if n == 0 and is_prv2:
                            pe.wait_ge(sem.x_added, prv.count)
                        if n in (1, 2) and is_cur:
                            pe.wait_ge(sem.qkT_copied, 3 * cur.count + n + 1)
                        if n == 3 and is_nxt2:
                            pe.wait_ge(sem.hT_copied, nxt2.count + 1)
                        for i in range(2):
                            for b in range(2):
                                mm = nc.tensor.transpose(ring[:, PT[n], (2 * i + b) * P:(2 * i + b + 1) * P],
                                                         probs[:, prv.slot, 2 * n + i, b * P:(b + 1) * P], m.ident[:])
                        mm.then_inc(sem.pT_made, 1)
                if is_cur:
                    pe.wait_ge(sem.qkT_copied, 3 * cur.count + 3)
                    if not is_prv:
                        pe.wait_ge(sem.window_cleared, before // (NT // 2) * 4 + 4)
                        pe.wait_ge(sem.hT_copied, nxt2.count + 1)
                    for n in range(WH // 2):
                        if is_prv:
                            pe.wait_ge(sem.pT_copied, 4 * prv.count + n + 1)
                        for i in range(2):
                            mm = nc.tensor.matmul(ring[:, SC[n], i * 2 * P:(i + 1) * 2 * P], qT[:, n, i],
                                                  kT[:, n].rearrange("p b t -> p (b t)"), start=True, stop=True)
                        mm.then_inc(sem.scores_made, 1)
                if is_prv:
                    pe.wait_ge(sem.pT_copied, 4 * prv.count + 4)
                    pe.wait_ge(sem.v_copied, prv.count + 1)
                    if is_prv2:
                        pe.wait_ge(sem.oT_copied, prv.count)
                    for n in range(WH // 2):
                        for b in range(2):
                            for i in range(2):
                                mm = nc.tensor.matmul(o_ps[i * WD:(i + 1) * WD, n], v[:, b, (2 * n + i) * WD:(2 * n + i + 1) * WD],
                                                      probsT[:, 2 * n + i, b], start=(b == 0), stop=(b == 1))
                    mm.then_inc(sem.o_summed, 1)
                if is_nxt2:
                    pe.wait_ge(sem.hT_copied, nxt2.count + 1)
                    if not is_nxt:
                        pe.wait_ge(sem.w_attn_in, m.w_attn_count(before))
                    else:
                        pe.wait_ge(sem.qk_read, nxt.count + 1)
                    for j in range(2):
                        for c in range(KC):
                            mm = nc.tensor.matmul(qkv_ps[:, j], hT[:, nxt2.slot, c], m.wqkv[:, c, j * INNER:(j + 1) * INNER],
                                                  start=(c == 0), stop=(c == KC - 1))
                    mm.then_inc(sem.qk_made, 1)
                if is_prv:
                    pe.wait_ge(sem.oT_copied, prv.count + 1)
                    if is_cur:
                        pe.wait_ge(sem.masked, WH * cur.count + 2)
                    for j in range(INNER // P):
                        mm = nc.tensor.matmul(ring[:, OUT, 0:D], oT[:, j], m.wo[:, j], start=(j == 0), stop=(j == INNER // P - 1))
                    mm.then_inc(sem.out_made, 1)
                if is_nxt:
                    if is_cur:
                        pe.wait_ge(sem.v_copied, cur.count + 1)
                    for c in range(KC):
                        mm = nc.tensor.matmul(qkv_ps[:, 2], hT[:, nxt.slot, c], m.wqkv[:, c, 2 * INNER:3 * INNER],
                                              start=(c == 0), stop=(c == KC - 1))
                    mm.then_inc(sem.v_made, 1)
            stepped(pe, step, -2, NT)

        @block.scalar
        def _(act):
            def step(pair, odd):
                cur, nxt, nxt2, prv = (tile_at(pair, before, odd, k) for k in (0, 1, 2, -1))
                is_cur, is_nxt, is_nxt2, is_prv = (exists(pair, odd, k) for k in (0, 1, 2, -1))
                if is_cur:
                    act.wait_ge(sem.qkT_made, 2 * cur.count + 1)
                    for i in range(2):
                        rows = slice(i * WD, (i + 1) * WD)
                        nc.scalar.copy(qT[rows, :, i], ring[rows, QT].rearrange("p (j t) -> p j t", t=P)).then_inc(sem.qkT_copied, 1)
                    act.wait_ge(sem.qkT_made, 2 * cur.count + 2)
                    nc.scalar.copy(kT[:, :, cur.slot], ring[:, KT].rearrange("p (j t) -> p j t", t=P)).then_inc(sem.qkT_copied, 1)
                if is_nxt2:
                    act.wait_ge(sem.hT_made, nxt2.count + 1)
                    nc.scalar.copy(hT[:, nxt2.slot], ring[:, HT, 0:D].rearrange("p (c t) -> p c t", t=P)).then_inc(sem.hT_copied, 1)
                if is_prv:
                    for n in range(WH // 2):
                        act.wait_ge(sem.pT_made, 4 * prv.count + n + 1)
                        nc.scalar.copy(probsT[:, 2 * n:2 * n + 2], ring[:, PT[n]].rearrange("p (i b t) -> p i b t", i=2, b=2)).then_inc(sem.pT_copied, 1)
                if is_cur:
                    for head in range(WH):
                        if head % 4 == 0:
                            act.wait_ge(sem.nbias_made, 2 * cur.count + head // 4 + 1)
                        nc.scalar.activation(probs[:, cur.slot, head], scores[:, head], ACT.Exp,
                                             bias=nbias[:, cur.slot, head:head + 1], scale=rnorm[:, cur.slot, head:head + 1],
                                             accum_out=psum_row[:, cur.slot, head:head + 1]).then_inc(sem.probs_made, 1)
                if is_nxt2:
                    act.wait_ge(sem.qk_made, nxt2.count + 1)
                    if is_nxt:
                        act.wait_ge(sem.ssq_made, nxt.count + 1)
                    for j in range(2):
                        nc.scalar.activation(squares[:, j], qkv_ps[:, j], ACT.Square).then_inc(sem.squared, 1)
            stepped(act, step, -2, NT)

        @block.vector
        def _(dve):
            def step(pair, odd):
                cur, nxt, nxt2, prv = (tile_at(pair, before, odd, k) for k in (0, 1, 2, -1))
                is_cur, is_nxt, is_nxt2, is_prv = (exists(pair, odd, k) for k in (0, 1, 2, -1))
                if is_cur:
                    mask = m.mask_first if not is_prv else m.masks[:, cur.slot]
                    for head in range(WH):
                        n, i = head // 2, head % 2
                        if i == 0:
                            pass_gate(dve, sem, sem.scores_made, 4 * cur.count + n + 1)
                        nc.vector.tensor_tensor_reduce(out=scores[:, head], in0=ring[:, SC[n], i * 2 * P:(i + 1) * 2 * P], in1=mask,
                                                       scale=1.0, scalar=-3e38, op0=ALU.add, op1=ALU.max,
                                                       accum_out=smax[:, cur.slot, head:head + 1]).then_inc(sem.masked, 1)
                        if head % 4 == 3:
                            k = 4 * (head // 4)
                            dve.wait_ge(sem.masked, WH * cur.count + head + 1)
                            nc.vector.scalar_tensor_tensor(out=nbias[:, cur.slot, k:k + 4], in0=smax[:, cur.slot, k:k + 4], scalar=-1.0,
                                                           in1=rnorm[:, cur.slot, k:k + 4], op0=ALU.mult, op1=ALU.mult).then_inc(sem.nbias_made, 1)
                if is_prv:
                    dve.wait_ge(sem.o_summed, prv.count + 1)
                    nc.vector.tensor_copy(oT[:], o_ps[:]).then_inc(sem.oT_copied, 1)
                if is_cur:
                    dve.wait_ge(sem.v_made, cur.count + 1)
                    nc.vector.tensor_copy(v[:, cur.slot], qkv_ps[:, 2]).then_inc(sem.v_copied, 1)
                    for half in range(2):
                        k = 4 * half
                        dve.wait_ge(sem.probs_made, WH * cur.count + k + 4)
                        nc.vector.reciprocal(rsum[:, cur.slot, k:k + 4], psum_row[:, cur.slot, k:k + 4]).then_inc(sem.rsum_made, 1)
                        dve.wait_ge(sem.rsum_made, 2 * cur.count + half + 1)
                        for head in range(k, k + 4):
                            nc.vector.tensor_scalar(probs[:, cur.slot, head], probs[:, cur.slot, head],
                                                    rsum[:, cur.slot, head:head + 1], None, ALU.mult).then_inc(sem.probs_normal, 1)
                if is_nxt2:
                    dve.wait_ge(sem.squared, 2 * nxt2.count + 2)
                    dve.wait_ge(sem.rope_made, nxt2.count + 1)
                    if is_nxt:
                        dve.wait_ge(sem.qk_rotated, nxt.count + 1)
                    raw = qkv_ps[:, 0:2].rearrange("p c (h d) -> p c h d", d=WD)
                    tab = rope[:, nxt2.slot].rearrange("p (c f) d -> p c f d", f=2)
                    nc.vector.tensor_tensor(turned[:].rearrange("p c (h d) -> p c h d", d=WD), raw,
                                            tab[:, :, 0].unsqueeze(2).broadcast_to([P, 2, WH, WD]), ALU.mult)
                    cr = crossed[:].rearrange("p c (h d) -> p c h d", d=WD)
                    H = WD // 2
                    nc.vector.tensor_tensor(cr[:, :, :, 0:H], raw[:, :, :, H:WD],
                                            tab[:, :, 1, 0:H].unsqueeze(2).broadcast_to([P, 2, WH, H]), ALU.mult)
                    nc.vector.tensor_tensor(cr[:, :, :, H:WD], raw[:, :, :, 0:H],
                                            tab[:, :, 1, H:WD].unsqueeze(2).broadcast_to([P, 2, WH, H]), ALU.mult).then_inc(sem.qk_read, 1)
                    nc.vector.tensor_reduce(ssq[:, nxt2.slot], squares[:].rearrange("p c (h d) -> p (c h) d", d=WD), AX.X, ALU.add).then_inc(sem.ssq_made, 1)
                if is_prv:
                    dve.wait_ge(sem.out_made, prv.count + 1)
                    nc.vector.tensor_tensor(X[:, prv.place], X[:, prv.place], ring[:, OUT, 0:D], ALU.add).then_inc(sem.x_added, 1)
            for i in range(2):
                nc.vector.memset(qT[i * WD:(i + 1) * WD, :, 1 - i], 0.0).then_inc(sem.window_cleared, 1)
            stepped(dve, step, -2, NT)

        @block.gpsimd
        def _(pool):
            def scale_tables(pair, odd, ahead):
                a = tile_at(pair, before, odd, ahead)
                pool.wait_ge(sem.rope_in[a.slot], 16 * a.turn + 16)
                if exists(pair, odd, ahead - 2):
                    pool.wait_ge(sem.qk_read, a.count - 1)
                nc.gpsimd.tensor_tensor(rope[:, a.slot], rope_raw[:, a.slot], m.scales[:], ALU.mult).then_inc(sem.rope_made, 1)

            def step(pair, odd):
                cur, last, last2 = (tile_at(pair, before, odd, -k) for k in (0, 1, 2))
                if exists(pair, odd, 1):
                    if not exists(pair, odd, 0):
                        pool.wait_ge(sem.w_attn_in, m.w_attn_count(before))
                    scale_tables(pair, odd, 1)
                if not exists(pair, odd, 0):
                    return
                pass_gate(pool, sem, sem.ssq_made, cur.count + 1)
                nc.gpsimd.tensor_scalar(ssq[:, cur.slot], ssq[:, cur.slot], 1e-24, None, ALU.max).then_inc(sem.ssq_kept, 1)
                pool.wait_ge(sem.ssq_kept, cur.count + 1)
                if exists(pair, odd, -2):
                    pool.wait_ge(sem.probs_made, WH * last2.count + WH)
                nc.gpsimd.tensor_tensor(rnorm[:, cur.slot], ssq[:, cur.slot], m.minus_half[:, 0:2 * WH], ALU.pow).then_inc(sem.rnorm_made, 1)
                nc.gpsimd.tensor_tensor(turned[:, 1], turned[:, 1], crossed[:, 1], ALU.add).then_inc(sem.k_turned, 1)
                if exists(pair, odd, -1):
                    pool.wait_ge(sem.qkT_made, 2 * last.count + 2)
                nc.gpsimd.tensor_tensor(qk[:, 0], turned[:, 0], crossed[:, 0], ALU.add)
                pool.wait_ge(sem.rnorm_made, cur.count + 1)
                pool.wait_ge(sem.k_turned, cur.count + 1)
                nc.gpsimd.tensor_tensor(qk[:, 1].rearrange("p (h d) -> p h d", d=WD), turned[:, 1].rearrange("p (h d) -> p h d", d=WD),
                                        rnorm[:, cur.slot, WH:2 * WH].unsqueeze(2).broadcast_to([P, WH, WD]), ALU.mult).then_inc(sem.qk_rotated, 1)

            nc.gpsimd.memset(kT[:, :, 1], 0.0).then_inc(sem.window_cleared, 1)
            nc.gpsimd.memset(v[:, 1], 0.0).then_inc(sem.window_cleared, 1)
            stepped(pool, step, -1, NT - 1)


def mlp(nc, m, sem, before):
    widths = [min(P, HID - c * P) for c in range(NC)]
    with ExitStack() as ctx:
        def sb(name, shape, dt=F32):
            return ctx.enter_context(nc.sbuf_tensor(name + m.tag, shape, dt))

        def ps(name, shape, dt=F32):
            return ctx.enter_context(nc.psum_tensor(name + m.tag, shape, dt))

        X, h = m.X, sb("mh", [P, GT, D])
        stats = sb("stats", [P, GT, nc.vector.BN_STATS_DIM])
        mv = sb("mv", [P, GT, 2])
        shifted_var = sb("shifted_var", [P, GT])
        rstd = sb("rstd", [P, GT])
        hn = sb("hn", [P, GT, D])
        hT = sb("mhT", [P, KC, GW])
        gate = sb("gate", [P, 2, GW])
        u = sb("u", [P, NC, GW])
        xb = sb("xb", [P, GT, D])
        turn_ps = ps("turn_ps", [P, 2, 4, P])
        ag_ps = ps("ag_ps", [P, 2, 2, GW])
        y_ps = ps("y_ps", [P, 2, 512])

        block = ctx.enter_context(nc.Block())

        def groups(eng, body):
            with eng.Fori(0, NG - 1) as g:
                body(g, before + g, True)
            body(NG - 1, before + NG - 1, False)

        @block.sync
        def _(sp):
            def load(g, count, first):
                if not first:
                    sp.wait_ge(sem.ln_applied, GT * count)
                nc.sync.dma_start(h[:, :, 0:P], X[:, bass.ds(g * GT, GT), 0:P]).then_inc(sem.mh_in, 16)
                nc.sync.dma_start(h[1:P, :, P:D], X[0:P - 1, bass.ds(g * GT, GT), P:D]).then_inc(sem.mh_in, 16)
                before_group = m.zeros[0:1, 0:P] if first else X[P - 1:P, g * GT - 1, P:D]
                nc.sync.dma_start(h[0:1, 0, P:D], before_group).then_inc(sem.mh_in, 16)
                nc.sync.dma_start(h[0:1, 1:GT, P:D], X[P - 1:P, bass.ds(g * GT, GT - 1), P:D]).then_inc(sem.mh_in, 16)
            load(0, before, True)
            with sp.Fori(1, NG) as g:
                load(g, before + g, False)

        @block.tensor
        def _(pe):
            def turn(count):
                for t in range(GT):
                    pe.wait_ge(sem.ln_applied, GT * count + t + 1)
                    if t >= 2:
                        pe.wait_ge(sem.mhT_copied, GT * count + t - 1)
                    for c in range(KC):
                        mm = nc.tensor.transpose(turn_ps[:, t % 2, c], hn[:, t, c * P:(c + 1) * P], m.ident[:])
                    mm.then_inc(sem.mhT_made, 1)

            pe.wait_ge(sem.w_mlp_in, m.w_mlp_count(before))
            turn(before)

            def body(g, count, more):
                pe.wait_ge(sem.mhT_copied, GT * count + GT)
                for c, w in enumerate(widths):
                    if c >= 2:
                        pe.wait_ge(sem.u_made, NC * count + c - 1)
                    for half in range(2):
                        for k in range(KC):
                            mm = nc.tensor.matmul(ag_ps[0:w, c % 2, half], m.w1[:, k, half * HID + c * P:half * HID + c * P + w],
                                                  hT[:, k], start=(k == 0), stop=(k == KC - 1))
                    mm.then_inc(sem.ag_made, 1)
                if more:
                    turn(count + 1)
                for t in range(GT):
                    if t == 0:
                        pe.wait_ge(sem.u_made, NC * count + NC)
                    if t >= 2:
                        pe.wait_ge(sem.mx_added, GT * count + t - 1)
                    for c, w in enumerate(widths):
                        mm = nc.tensor.matmul(y_ps[:, t % 2, 0:D], u[0:w, c, t * P:(t + 1) * P], m.w2[0:w, c],
                                              start=(c == 0), stop=(c == NC - 1))
                    mm.then_inc(sem.y_made, 1)
            groups(pe, body)

        @block.scalar
        def _(act):
            act.wait_ge(sem.w_mlp_in, m.w_mlp_count(before))

            def body(g, count, more):
                for c, w in enumerate(widths):
                    act.wait_ge(sem.ag_made, NC * count + c + 1)
                    act.wait_ge(sem.u_made, NC * count + c - 1 if c >= 2 else NC * count)
                    nc.scalar.activation(gate[0:w, c % 2], ag_ps[0:w, c % 2, 1], ACT.Gelu, bias=m.b1[0:w, 1, c:c + 1],
                                         scale=1.0).then_inc(sem.gelu_made, 1)
            groups(act, body)

        @block.vector
        def _(dve):
            def layernorm(count):
                dve.wait_ge(sem.mh_in, 64 * count + 64)
                for t in range(GT):
                    nc.vector.bn_stats(stats[:, t], h[:, t]).then_inc(sem.stats_made, 1)
                for t in range(GT):
                    pass_gate(dve, sem, sem.stats_made, GT * count + t + 1)
                    nc.vector.bn_aggr(mv[:, t], stats[:, t]).then_inc(sem.mv_made, 1)
                dve.wait_ge(sem.rstd_made, count + 1)
                for t in range(GT):
                    nc.vector.tensor_scalar(hn[:, t], h[:, t], mv[:, t, 0:1], rstd[:, t:t + 1], ALU.subtract, ALU.mult).then_inc(sem.ln_applied, 1)

            def hidden(c, w, count):
                dve.wait_ge(sem.gelu_made, NC * count + c + 1)
                nc.vector.scalar_tensor_tensor(out=u[0:w, c], in0=ag_ps[0:w, c % 2, 0], scalar=m.b1[0:w, 0, c:c + 1],
                                               in1=gate[0:w, c % 2], op0=ALU.add, op1=ALU.mult).then_inc(sem.u_made, 1)

            def copy_turned(t, count):
                dve.wait_ge(sem.mhT_made, GT * count + t + 1)
                for k in range(KC):
                    mm = nc.vector.tensor_scalar(hT[:, k, t * P:(t + 1) * P], turn_ps[:, t % 2, k],
                                                 m.ln[:, 0, k:k + 1], m.ln[:, 1, k:k + 1], ALU.mult, ALU.add)
                mm.then_inc(sem.mhT_copied, 1)

            dve.wait_ge(sem.w_mlp_in, m.w_mlp_count(before))
            layernorm(before)
            for t in range(GT):
                copy_turned(t, before)

            def body(g, count, more):
                for c, w in enumerate(widths):
                    if c == 2 and more:
                        layernorm(count + 1)
                    if c == 0 and not isinstance(count, int) or c == 0 and count > before:
                        dve.wait_ge(sem.y_made, GT * count)
                    hidden(c, w, count)
                if more:
                    for t in range(GT):
                        copy_turned(t, count + 1)
                for t in range(GT):
                    dve.wait_ge(sem.y_made, GT * count + t + 1)
                    if t == 0:
                        dve.wait_ge(sem.xb_made, count + 1)
                    nc.vector.tensor_tensor(X[:, g * GT + t], xb[:, t], y_ps[:, t % 2, 0:D], ALU.add).then_inc(sem.mx_added, 1)
            groups(dve, body)

        @block.gpsimd
        def _(pool):
            def rstds(count):
                pass_gate(pool, sem, sem.mv_made, GT * count + GT)
                nc.gpsimd.tensor_scalar(shifted_var[:], mv[:, :, 1], EPS, None, ALU.add).then_inc(sem.eps_added, 1)
                pool.wait_ge(sem.eps_added, count + 1)
                nc.gpsimd.tensor_tensor(rstd[:], shifted_var[:], m.minus_half[:, 0:GT], ALU.pow).then_inc(sem.rstd_made, 1)
            pool.wait_ge(sem.w_mlp_in, m.w_mlp_count(before))
            rstds(before)

            def body(g, count, more):
                if not isinstance(count, int) or count > before:
                    pool.wait_ge(sem.mx_added, GT * count)
                nc.gpsimd.tensor_tensor(xb[:], X[:, bass.ds(g * GT, GT)], m.b2[:].unsqueeze(1).broadcast_to([P, GT, D]), ALU.add).then_inc(sem.xb_made, 1)
                if more:
                    rstds(count + 1)
            groups(pool, body)


CT = 8
NQ = NT // CT


def rejoin(nc, m, sem, base, scale, store, normalise):
    X = m.X
    with ExitStack() as ctx:
        def sb(name, shape, dt=F32):
            return ctx.enter_context(nc.sbuf_tensor(name + m.tag, shape, dt))

        part = sb("part", [P, 2, CT, D])
        stats = sb("jstats", [P, CT, nc.vector.BN_STATS_DIM])
        mv = sb("jmv", [P, CT, 2])
        shifted_var = sb("jvar", [P, CT])
        rstd = sb("jrstd", [P, CT])
        base_in = [ctx.enter_context(nc.semaphore(f"base_in{n}" + m.tag)) for n in range(NQ)]
        stored = [ctx.enter_context(nc.semaphore(f"stored{n}" + m.tag)) for n in range(NQ)]
        joined, stats_made, mv_made, eps_added, rstd_made = (
            ctx.enter_context(nc.semaphore(n + m.tag)) for n in ("joined", "jstats_made", "jmv_made", "jeps", "jrstd_made"))

        def chunk(dram, q):
            return dram.rearrange("(t p) d -> p t d", p=P)[:, q * CT:(q + 1) * CT]

        block = ctx.enter_context(nc.Block())

        @block.sync
        def _(sp):
            for q in range(NQ if base is not None else 0):
                if scale is None:
                    nc.sync.dma_start(X[:, q * CT:(q + 1) * CT], chunk(base, q)).then_inc(base_in[q], 16)
                    continue
                if q >= 2:
                    sp.wait_ge(joined, q - 1)
                nc.sync.dma_start(part[:, q % 2], chunk(base, q)).then_inc(base_in[q], 16)

        @block.scalar
        def _(act):
            if store is not None:
                for q in range(NQ):
                    act.wait_ge(joined, q + 1)
                    nc.scalar.dma_start(chunk(store, q), X[:, q * CT:(q + 1) * CT]).then_inc(stored[q], 16)
                for q in range(NQ):
                    act.wait_ge(stored[q], 16)

        @block.vector
        def _(dve):
            if scale is not None:
                for q in range(NQ):
                    dve.wait_ge(base_in[q], 16)
                    x = X[:, q * CT:(q + 1) * CT].rearrange("p t d -> p (t d)")
                    nc.vector.scalar_tensor_tensor(out=x, in0=x, scalar=scale, in1=part[:, q % 2].rearrange("p t d -> p (t d)"),
                                                   op0=ALU.mult, op1=ALU.add).then_inc(joined, 1)
            if normalise:
                for q in range(NQ):
                    if scale is None and base is not None:
                        dve.wait_ge(base_in[q], 16)
                    elif scale is not None:
                        dve.wait_ge(joined, q + 1)
                    if store is not None:
                        dve.wait_ge(stored[q], 16)
                    for t in range(CT):
                        nc.vector.bn_stats(stats[:, t], X[:, q * CT + t]).then_inc(stats_made, 1)
                    for t in range(CT):
                        dve.wait_ge(stats_made, CT * q + t + 1)
                        nc.vector.bn_aggr(mv[:, t], stats[:, t]).then_inc(mv_made, 1)
                    dve.wait_ge(rstd_made, q + 1)
                    for t in range(CT):
                        nc.vector.tensor_scalar(X[:, q * CT + t], X[:, q * CT + t], mv[:, t, 0:1], rstd[:, t:t + 1],
                                                ALU.subtract, ALU.mult)

        @block.gpsimd
        def _(pool):
            if normalise:
                for q in range(NQ):
                    pool.wait_ge(mv_made, CT * (q + 1))
                    nc.gpsimd.tensor_scalar(shifted_var[:], mv[:, :, 1], EPS, None, ALU.add).then_inc(eps_added, 1)
                    pool.wait_ge(eps_added, q + 1)
                    nc.gpsimd.tensor_tensor(rstd[:], shifted_var[:], m.minus_half[:, 0:CT], ALU.pow).then_inc(rstd_made, 1)


def project_heads(nc, m, sem):
    X = m.X
    with ExitStack() as ctx:
        def sb(name, shape, dt=F32):
            return ctx.enter_context(nc.sbuf_tensor(name, shape, dt))

        def ps(name, shape, dt=F32):
            return ctx.enter_context(nc.psum_tensor(name, shape, dt))

        names = """c_w_in c_xT_made c_xT_copied qk_summed v_summed v_biased qk_biased turned_made crossed_made rot_made high_made
            rest_made mid_made parts_made partsT_made partsT_copied""".split()
        (w_in, xT_made, xT_copied, qk_summed, v_summed, v_biased, qk_biased, turned_made, crossed_made, rot_made, high_made,
         rest_made, mid_made, parts_made, partsT_made, partsT_copied) = (ctx.enter_context(nc.semaphore(n)) for n in names)
        tile_in = [ctx.enter_context(nc.semaphore(f"c_tile_in{i}")) for i in range(2)]
        parts_out = [ctx.enter_context(nc.semaphore(f"c_parts_out{i}")) for i in range(2)]

        w = sb("c_w", [P, KC, 3 * D])
        bias = sb("c_bias", [P, 3 * D])
        x = sb("c_x", [P, 2, D])
        tab = sb("c_tab", [P, 2, 2, 2, HD])
        xT = sb("c_xT", [P, 2, KC, P])
        qkb = sb("c_qkb", [P, 2, 2, D])
        turned = sb("c_turned", [P, 2, 2, D])
        crossed = sb("c_crossed", [P, 2, 2, D])
        rot = sb("c_rot", [P, 2, 2, D])
        rest = sb("c_rest", [P, 2, 2, D])
        parts = sb("c_parts", [P, 2, 2, 3, D], BF16)
        partsT = sb("c_partsT", [P, 2, 12, P], BF16)
        xT_ps = ps("c_xT_ps", [P, 512])
        qk_ps = ps("c_qk_ps", [P, 2 * D])
        v_ps = ps("c_v_ps", [P, 512])
        partsT_ps = ps("c_partsT_ps", [P, 2, 8, P], BF16)

        block = ctx.enter_context(nc.Block())

        @block.sync
        def _(sp):
            nc.sync.dma_start(w[:], m.cwqkv_dram).then_inc(w_in, 16)
            nc.sync.dma_start(bias[:], m.cbias_dram.partition_broadcast(P)).then_inc(w_in, 16)

            def load(pair, odd):
                a = tile_at(pair, 0, odd)
                if exists(pair, odd, -2):
                    sp.wait_ge(xT_made, a.count - 1)
                    sp.wait_ge(crossed_made, a.count - 1)
                    sp.wait_ge(turned_made, a.count - 1)
                nc.sync.dma_start(x[:, a.slot], X[:, a.place]).then_inc(tile_in[a.slot], 16)
                nc.sync.dma_start(tab[:, a.slot], m.crope_dram[a.place]).then_inc(tile_in[a.slot], 16)

            def store(pair, odd):
                a = tile_at(pair, 0, odd)
                sp.wait_ge(partsT_copied, 2 * a.count + 2)
                nc.sync.dma_start(m.parts_dram.rearrange("a (b p) s -> p (a b) s", p=P)[:, :, bass.ts(a.place, P)],
                                  partsT[:, a.slot]).then_inc(parts_out[a.slot], 16)
            for s in range(4):
                load(s // 2, s % 2)
            with sp.Fori(2, NT // 2) as pair:
                for odd in range(2):
                    load(pair, odd)
                    store(pair - 2, odd)
            for s in range(NT - 4, NT):
                store(s // 2, s % 2)
            for slot in range(2):
                sp.wait_ge(parts_out[slot], 16 * (NT // 2))

        @block.tensor
        def _(pe):
            def step(pair, odd):
                if exists(pair, odd, 1):
                    a = tile_at(pair, 0, odd, 1)
                    pe.wait_ge(tile_in[a.slot], 32 * a.turn + 32)
                    if exists(pair, odd, 0):
                        pe.wait_ge(xT_copied, a.count)
                    for c in range(KC):
                        mm = nc.tensor.transpose(xT_ps[:, c * P:(c + 1) * P], x[:, a.slot, c * P:(c + 1) * P], m.ident[:])
                    mm.then_inc(xT_made, 1)
                if exists(pair, odd, 0):
                    a = tile_at(pair, 0, odd)
                    pe.wait_ge(xT_copied, a.count + 1)
                    if exists(pair, odd, -1):
                        pe.wait_ge(qk_biased, a.count)
                        pe.wait_ge(v_biased, a.count)
                    else:
                        pe.wait_ge(w_in, 32)
                    for c in range(KC):
                        mm = nc.tensor.matmul(qk_ps[:], xT[:, a.slot, c], w[:, c, 0:2 * D], start=(c == 0), stop=(c == KC - 1))
                    mm.then_inc(qk_summed, 1)
                    for c in range(KC):
                        mm = nc.tensor.matmul(v_ps[:, 0:D], xT[:, a.slot, c], w[:, c, 2 * D:3 * D], start=(c == 0), stop=(c == KC - 1))
                    mm.then_inc(v_summed, 1)
                if exists(pair, odd, -2):
                    a = tile_at(pair, 0, odd, -2)
                    pe.wait_ge(parts_made, a.count + 1)
                    for qk in range(2):
                        if exists(pair, odd, -3):
                            pe.wait_ge(partsT_copied, 2 * a.count)
                        for n in range(6):
                            mm = nc.tensor.transpose(partsT_ps[:, qk, n], parts[:, a.slot, qk, n // 2, (n % 2) * P:(n % 2 + 1) * P], m.identb[:])
                        mm.then_inc(partsT_made, 1)
            stepped(pe, step, -1, NT + 1)

        @block.scalar
        def _(act):
            def step(pair, odd):
                if exists(pair, odd, 1):
                    a = tile_at(pair, 0, odd, 1)
                    act.wait_ge(xT_made, a.count + 1)
                    nc.scalar.copy(xT[:, a.slot], xT_ps[:, 0:D].rearrange("p (c t) -> p c t", t=P)).then_inc(xT_copied, 1)
                if exists(pair, odd, -1):
                    a = tile_at(pair, 0, odd, -1)
                    act.wait_ge(rot_made, a.count + 1)
                    if exists(pair, odd, -3):
                        act.wait_ge(partsT_made, 2 * a.count - 2)
                    nc.scalar.copy(parts[:, a.slot, :, 0], rot[:, a.slot]).then_inc(high_made, 1)
                    act.wait_ge(rest_made, a.count + 1)
                    nc.scalar.copy(parts[:, a.slot, :, 1], rest[:, a.slot]).then_inc(mid_made, 1)
                if exists(pair, odd, -2):
                    a = tile_at(pair, 0, odd, -2)
                    if exists(pair, odd, -4):
                        act.wait_ge(parts_out[a.slot], 16 * a.turn)
                    for qk in range(2):
                        act.wait_ge(partsT_made, 2 * a.count + 1 + qk)
                        nc.scalar.copy(partsT[:, a.slot, 6 * qk:6 * qk + 6], partsT_ps[:, qk, 0:6]).then_inc(partsT_copied, 1)
            stepped(act, step, -1, NT + 1)

        @block.vector
        def _(dve):
            dve.wait_ge(w_in, 32)

            def step(pair, odd):
                if exists(pair, odd, 0):
                    a = tile_at(pair, 0, odd)
                    dve.wait_ge(qk_summed, a.count + 1)
                    if exists(pair, odd, -2):
                        dve.wait_ge(crossed_made, a.count - 1)
                    nc.vector.tensor_tensor(qkb[:, a.slot].rearrange("p c n -> p (c n)"), qk_ps[:], bias[:, 0:2 * D], ALU.add).then_inc(qk_biased, 1)
                    pass_gate(dve, sem, v_summed, a.count + 1)
                    nc.vector.tensor_tensor(m.V[:, a.place, :, 0:HD], v_ps[:, 0:D].rearrange("p (h d) -> p h d", d=HD),
                                            bias[:, 2 * D:3 * D].rearrange("p (h d) -> p h d", d=HD), ALU.add).then_inc(v_biased, 1)
                    if exists(pair, odd, -2):
                        dve.wait_ge(rot_made, a.count - 1)
                    dve.wait_ge(tile_in[a.slot], 32 * a.turn + 32)
                    dve.wait_ge(qk_biased, a.count + 1)
                    nc.vector.tensor_tensor(turned[:, a.slot].rearrange("p c (h d) -> p c h d", d=HD),
                                            qkb[:, a.slot].rearrange("p c (h d) -> p c h d", d=HD),
                                            tab[:, a.slot, :, 0].unsqueeze(2).broadcast_to([P, 2, NH, HD]), ALU.mult).then_inc(turned_made, 1)
                if exists(pair, odd, -1):
                    a = tile_at(pair, 0, odd, -1)
                    dve.wait_ge(high_made, a.count + 1)
                    nc.vector.tensor_tensor(rest[:, a.slot], rot[:, a.slot], parts[:, a.slot, :, 0], ALU.subtract).then_inc(rest_made, 1)
                    dve.wait_ge(mid_made, a.count + 1)
                    nc.vector.tensor_tensor(parts[:, a.slot, :, 2], rest[:, a.slot], parts[:, a.slot, :, 1], ALU.subtract).then_inc(parts_made, 1)
            stepped(dve, step, -1, NT + 1)

        @block.gpsimd
        def _(pool):
            nc.gpsimd.memset(m.V[:, :, :, HD:HD + 1], 1.0)

            def step(pair, odd):
                if not exists(pair, odd, 0):
                    return
                a = tile_at(pair, 0, odd)
                pool.wait_ge(tile_in[a.slot], 32 * a.turn + 32)
                pool.wait_ge(qk_biased, a.count + 1)
                if exists(pair, odd, -2):
                    pool.wait_ge(rot_made, a.count - 1)
                pairs = lambda t: t.rearrange("p c (n two) -> p c n two", two=2)
                for c in range(2):
                    for e in range(2):
                        mm = nc.gpsimd.tensor_tensor(
                            crossed[:, a.slot, c].rearrange("p (h n two) -> p h n two", two=2, h=NH)[:, :, :, e],
                            qkb[:, a.slot, c].rearrange("p (h n two) -> p h n two", two=2, h=NH)[:, :, :, 1 - e],
                            tab[:, a.slot, c, 1].rearrange("p (n two) -> p n two", two=2)[:, :, e].unsqueeze(1).broadcast_to([P, NH, HD // 2]), ALU.mult)
                mm.then_inc(crossed_made, 1)
                pool.wait_ge(crossed_made, a.count + 1)
                pool.wait_ge(turned_made, a.count + 1)
                if exists(pair, odd, -2):
                    pool.wait_ge(parts_made, a.count - 1)
                nc.gpsimd.tensor_tensor(rot[:, a.slot], turned[:, a.slot], crossed[:, a.slot], ALU.add).then_inc(rot_made, 1)
            stepped(pool, step, -1, NT + 1)


Q_PARTS = [0, 0, 0, 1, 1, 2]
K_PARTS = [0, 1, 2, 0, 1, 0]
SROWS = len(Q_PARTS) * HD
MROWS = SROWS + 3
PAIRS = [(g, j) for g in range(NG) for j in range(0, GT * (g + 1), 2)]
NQUAD = len(PAIRS) // 2
GROUP_END = {(g + 1) * (g + 2) // 2 - 1: g for g in range(NG)}
CHUNKS = [(t, c) for t in range(NT) for c in range(t // GT + 1)]
LEAD, TRAIL = 3, 7


def quad_items():
    items = [[] for _ in range(NQUAD)]
    for i in range(len(CHUNKS)):
        items[LEAD + i * (NQUAD - LEAD - TRAIL) // len(CHUNKS)].append(("chunk", i))
    items[NQUAD - TRAIL + 1].append(("maxima", 0))
    for quad, g in GROUP_END.items():
        if g < NG - 1:
            items[quad + 1].append(("sums", g))
    return items


ITEMS = quad_items()
FIRST_ITEMS = [("chunk", i) for i in range(len(CHUNKS))] + [("maxima", 0)]
HEAD_ITEMS = [item for quad in ITEMS for item in quad] + [("sums", NG - 1)]
LAST_ITEMS = [item for item in HEAD_ITEMS if item[0] == "sums"]
FREE_ST, FREE_PROBS, FREE_O = 2, 4, 2


def item_count(h, item, more):
    if isinstance(h, int) and h < 0:
        return FIRST_ITEMS.index(item)
    return len(FIRST_ITEMS) + len(HEAD_ITEMS) * h + (HEAD_ITEMS if more else LAST_ITEMS).index(item)


def item_slot(h, b, item, more):
    return item_count(h if isinstance(h, int) and h < 0 else b, item, more) % 2


def causal_attention(nc, m, sem):
    with ExitStack() as ctx:
        def sb(name, shape, dt=F32):
            return ctx.enter_context(nc.sbuf_tensor(name, shape, dt))

        def ps(name, shape, dt=F32):
            return ctx.enter_context(nc.psum_tensor(name, shape, dt))

        names = "s_made s_read st_made exp_made pv_done o_read v_cleared v_in max_made split_made maxT_copied max_in max_row_in rows_set".split()
        (s_made, s_read, st_made, exp_made, pv_done, o_read, v_cleared, v_in, max_made, split_made, maxT_copied, max_in, max_row_in,
         rows_set) = (ctx.enter_context(nc.semaphore("d_" + n)) for n in names)
        stack_in = [ctx.enter_context(nc.semaphore(f"d_stack_in{i}")) for i in range(2)]

        q = sb("d_q", [P, 2, S], BF16)
        k = sb("d_k", [P, 2, S], BF16)
        probs = sb("d_probs", [P, 4, 2, GW])
        vh = sb("d_v", [P, 2, NT, 32])
        no_v = sb("d_no_v", [P, 32], BF16)
        sums = sb("d_sums", [P, 2, GW])
        chunk_max = sb("d_chunk_max", [P, NT, NG])
        neg_max = sb("d_neg_max", [P, NT])
        max_rest = sb("d_max_rest", [P, NT])
        max_parts = sb("d_max_parts", [P, 3, NT], BF16)
        maxT = sb("d_maxT", [3 * NT, P], BF16)
        st = ps("d_st", [P, 2, 2, GW])
        s_ps = ps("d_s", [P, 2, GW])
        o_ps = ps("d_o", [P, 2, 512])

        block = ctx.enter_context(nc.Block())

        def heads(eng, body):
            with eng.Fori(0, NH // 2 - 1) as pair:
                for b in range(2):
                    body(2 * pair + b, b, True)
            body(NH - 2, 0, True)
            body(NH - 1, 1, False)

        @block.sync
        def _(sp):
            def load(h, b):
                for n, part in enumerate(Q_PARTS):
                    nc.sync.dma_start(q[n * HD:(n + 1) * HD, b], m.parts_dram[part, bass.ds(h * HD, HD)]).then_inc(stack_in[b], 16)
                for n, part in enumerate(K_PARTS):
                    nc.sync.dma_start(k[n * HD:(n + 1) * HD, b], m.parts_dram[3 + part, bass.ds(h * HD, HD)]).then_inc(stack_in[b], 16)

            def max_rows(h, b):
                sp.wait_ge(maxT_copied, h + 1)
                nc.sync.dma_start(m.max_dram.rearrange("a (t c) -> (a t) c", c=P), maxT[:]).then_inc(max_row_in, 16)
                sp.wait_ge(max_row_in, 16 * h + 16)
                nc.sync.dma_start(q[SROWS:MROWS, b], m.max_dram).then_inc(max_in, 16)
            load(0, 0)
            load(1, 1)
            max_rows(0, 0)

            def body(h, b, more):
                if more:
                    max_rows(h + 1, 1 - b)
                if more and not (isinstance(h, int) and h + 2 >= NH):
                    sp.wait_ge(exp_made, FREE_ST + len(PAIRS) * (h + 1))
                    load(h + 2, b)
            heads(sp, body)

        @block.tensor
        def _(pe):
            def chunk(h, b, i, slot):
                t, c = CHUNKS[i]
                w = min(GW, (t + 1) * P - c * GW)
                if i == 0:
                    pe.wait_ge(stack_in[b], 192 * ((h - b) // 2) + 192)
                last = c == t // GT
                mm = nc.tensor.matmul(s_ps[:, slot, 0:w], q[0:SROWS, b, t * P:(t + 1) * P], k[0:SROWS, b, c * GW:c * GW + w],
                                      start=True, stop=not last)
                if last:
                    mm = nc.tensor.matmul(s_ps[:, slot, w - P:w], m.identb[:], m.cmask[:, 2], start=False, stop=True)
                mm.then_inc(s_made, 1)

            def item(h, b, which, more):
                n, slot = item_count(h, which, more), item_slot(h, b, which, more)
                if not (isinstance(n, int) and n < 2):
                    pe.wait_ge(s_read, n - 1)
                kind, i = which
                if kind == "chunk":
                    chunk(h + 1, 1 - b, i, slot)
                elif kind == "maxima":
                    pe.wait_ge(split_made, h + 2)
                    nc.tensor.transpose(s_ps[0:3 * NT, slot, 0:P // 2].bitcast(BF16), max_parts[:].rearrange("p a t -> p (a t)"),
                                        m.identb[:]).then_inc(s_made, 1)
                else:
                    pe.wait_ge(o_read, FREE_O + NG * h + i + 1)
                    for t in range(GT):
                        mm = nc.tensor.transpose(s_ps[:, slot, t * P:(t + 1) * P], sums[:, i % 2, t * P:(t + 1) * P], m.ident[:])
                    mm.then_inc(s_made, 1)

            def scores(h, b, n):
                g, j0 = PAIRS[n]
                col = P * max(0, j0 - GT * g)
                if n == 0:
                    pe.wait_ge(max_in, 16 * h + 16)
                pe.wait_ge(exp_made, FREE_ST + len(PAIRS) * h + n - 1)
                for j in range(2):
                    diagonal = j0 >= GT * g
                    mm = nc.tensor.matmul(st[:, n % 2, j, col:GW], k[0:MROWS, b, (j0 + j) * P:(j0 + j + 1) * P],
                                          q[0:MROWS, b, g * GW + col:(g + 1) * GW], start=True, stop=not diagonal)
                    if diagonal:
                        mm = nc.tensor.matmul(st[:, n % 2, j, col:col + P * (j + 1)], m.identb[:],
                                              m.cmask[:, 1 - j:2].rearrange("p a i -> p (a i)"), start=False, stop=True)
                mm.then_inc(st_made, 1)

            def sum_values(h, b, quad):
                g, j0 = PAIRS[2 * quad]
                pe.wait_ge(exp_made, FREE_ST + len(PAIRS) * h + 2 * quad + 2)
                if quad == 0:
                    pe.wait_ge(v_in, h + 1)
                if j0 == 0:
                    pe.wait_ge(o_read, FREE_O + NG * h + g - 1)
                if g == 0:
                    for c in range(4):
                        nc.tensor.matmul(o_ps[32 * c:32 * c + 32, g % 2], no_v[0:SROWS], k[0:SROWS, b, 0:GW],
                                         start=True, stop=False, skip_group_check=True)
                for c in range(4):
                    col = P * c if j0 == GT * g else 0
                    mm = nc.tensor.matmul(o_ps[32 * c:32 * c + 32, g % 2, col:GW], vh[:, b, j0 + c],
                                          probs[:, (2 * quad + c // 2) % 4, c % 2, col:GW],
                                          start=(j0 == 0 and g > 0), stop=(j0 == GT * g), skip_group_check=True)
                mm.then_inc(pv_done, 2)

            pe.sem_inc(pv_done, FREE_PROBS)
            pe.wait_ge(rows_set, 3)
            for which in FIRST_ITEMS:
                item(-1, 1, which, True)
            for n in range(2):
                scores(0, 0, n)

            def body(h, b, more):
                for quad in range(NQUAD):
                    items = [i for i in ITEMS[quad] if more or i[0] == "sums"]
                    third = -(-len(items) // 3)
                    for which in items[:third]:
                        item(h, b, which, more)
                    for j in range(2):
                        if quad + 1 < NQUAD:
                            scores(h, b, 2 * quad + 2 + j)
                        elif more:
                            scores(h + 1, 1 - b, j)
                        for which in items[third * (j + 1):third * (j + 2)]:
                            item(h, b, which, more)
                    sum_values(h, b, quad)
                item(h, b, ("sums", NG - 1), more)
            heads(pe, body)

        @block.scalar
        def _(act):
            act.sem_inc(exp_made, FREE_ST)
            act.sem_inc(o_read, FREE_O)

            def copy_sums(h, g):
                quad = (g + 1) * (g + 2) // 2 - 1
                act.wait_ge(pv_done, FREE_PROBS + len(PAIRS) * h + 2 * quad + 2)
                nc.scalar.copy(sums[:, g % 2], o_ps[:, g % 2]).then_inc(o_read, 1)

            def body(h, b, more):
                for n, (g, j0) in enumerate(PAIRS):
                    col = P * max(0, j0 - GT * g)
                    act.wait_ge(st_made, len(PAIRS) * h + n + 1)
                    act.wait_ge(pv_done, FREE_PROBS + len(PAIRS) * h + n - 3)
                    nc.scalar.activation(probs[:, n % 4, :, col:GW], st[:, n % 2, :, col:GW], ACT.Exp).then_inc(exp_made, 1)
                    if n % 2 and n // 2 - 1 in GROUP_END:
                        copy_sums(h, GROUP_END[n // 2 - 1])
                copy_sums(h, NG - 1)
            heads(act, body)

        @block.vector
        def _(dve):
            def split_maxima(h):
                nc.vector.tensor_reduce(neg_max[:], chunk_max[:], AX.X, ALU.max, negate=True).then_inc(max_made, 1)
                dve.wait_ge(max_made, 4 * h + 1)
                nc.vector.tensor_copy(max_parts[:, 0], neg_max[:]).then_inc(max_made, 1)
                dve.wait_ge(max_made, 4 * h + 2)
                nc.vector.tensor_tensor(max_rest[:], neg_max[:], max_parts[:, 0], ALU.subtract).then_inc(max_made, 1)
                dve.wait_ge(max_made, 4 * h + 3)
                nc.vector.tensor_copy(max_parts[:, 1], max_rest[:]).then_inc(max_made, 1)
                dve.wait_ge(max_made, 4 * h + 4)
                nc.vector.tensor_tensor(max_parts[:, 2], max_rest[:], max_parts[:, 1], ALU.subtract).then_inc(split_made, 1)

            def item(h, b, which, more):
                n, slot = item_count(h, which, more), item_slot(h, b, which, more)
                kind, i = which
                if kind == "chunk":
                    t, c = CHUNKS[i]
                    w = min(GW, (t + 1) * P - c * GW)
                    dve.wait_ge(s_made, n + 1)
                    nc.vector.tensor_reduce(chunk_max[:, t, c:c + 1], s_ps[:, slot, 0:w], AX.X, ALU.max).then_inc(s_read, 1)
                    if i == len(CHUNKS) - 1:
                        dve.wait_ge(s_read, n + 1)
                        split_maxima(h + 1)
                elif kind == "maxima":
                    dve.wait_ge(s_made, n + 1)
                    if not (isinstance(h, int) and h < 0):
                        dve.wait_ge(max_row_in, 16 * (h + 1))
                    nc.vector.tensor_copy(maxT[:], s_ps[0:3 * NT, slot, 0:P // 2].bitcast(BF16)).then_inc(s_read, 1)
                    dve.wait_ge(s_read, n + 1)
                    dve.sem_inc(maxT_copied, 1)
                else:
                    pass_gate(dve, sem, s_made, n + 1)
                    nc.vector.tensor_reduce(m.O[:, GT * i:GT * (i + 1), h],
                                            s_ps[:, slot].rearrange("p (t c d) -> p t d c", t=GT, c=4)[:, :, 0:HD + 1],
                                            AX.X, ALU.add).then_inc(s_read, 1)

            nc.vector.memset(k[SROWS:MROWS], 1.0).then_inc(rows_set, 1)
            nc.vector.memset(no_v[:], 0.0).then_inc(rows_set, 1)
            nc.vector.memset(chunk_max[:], -3e38).then_inc(rows_set, 1)
            dve.wait_ge(rows_set, 3)
            for which in FIRST_ITEMS:
                item(-1, 1, which, True)

            def body(h, b, more):
                for which in HEAD_ITEMS if more else LAST_ITEMS:
                    item(h, b, which, more)
            heads(dve, body)

        @block.gpsimd
        def _(pool):
            nc.gpsimd.memset(vh[:], 0.0).then_inc(v_cleared, 1)
            pool.wait_ge(v_cleared, 1)
            nc.gpsimd.tensor_copy(vh[:, 0, :, 0:HD + 1], m.V[:, :, 0]).then_inc(v_in, 1)

            def body(h, b, more):
                if more:
                    pass_gate(pool, sem, pv_done, FREE_PROBS + len(PAIRS) * h)
                    nc.gpsimd.tensor_copy(vh[:, 1 - b, :, 0:HD + 1], m.V[:, :, h + 1]).then_inc(v_in, 1)
            heads(pool, body)


def project_out(nc, m, sem):
    X = m.X
    with ExitStack() as ctx:
        def sb(name, shape, dt=F32):
            return ctx.enter_context(nc.sbuf_tensor(name, shape, dt))

        def ps(name, shape, dt=F32):
            return ctx.enter_context(nc.psum_tensor(name, shape, dt))

        names = "e_w_in recip_made o_made oT_made oT_copied y_made base_made joined".split()
        w_in, recip_made, o_made, oT_made, oT_copied, y_made, base_made, joined = (ctx.enter_context(nc.semaphore("e_" + n)) for n in names)
        mid_in, late_out = ([ctx.enter_context(nc.semaphore(f"e_{n}{i}")) for i in range(2)] for n in ("mid_in", "late_out"))
        w = sb("e_w", [P, KC, D])
        bias = sb("e_bias", [P, D])
        recip = sb("e_recip", [P, 2, NH])
        o = sb("e_o", [P, 2, D])
        oT = sb("e_oT", [P, 2, KC, P])
        mid = sb("e_mid", [P, 2, D])
        base = sb("e_base", [P, 2, D])
        late = sb("e_late", [P, 2, D])
        oT_ps = ps("e_oT_ps", [P, 2, 512])
        y_ps = ps("e_y_ps", [P, 2, 512])
        block = ctx.enter_context(nc.Block())

        @block.sync
        def _(sp):
            nc.sync.dma_start(w[:], m.cwo_dram).then_inc(w_in, 16)
            nc.sync.dma_start(bias[:], m.cbo_dram.partition_broadcast(P)).then_inc(w_in, 16)

            def load(pair, odd):
                a = tile_at(pair, 0, odd)
                if exists(pair, odd, -2):
                    sp.wait_ge(base_made, a.count - 1)
                nc.sync.dma_start(mid[:, a.slot], m.mid_dram[bass.ts(a.place, P)]).then_inc(mid_in[a.slot], 16)
            for s in range(2):
                load(s // 2, s % 2)
            with sp.Fori(1, NT // 2) as pair:
                for odd in range(2):
                    load(pair, odd)

        @block.tensor
        def _(pe):
            def step(pair, odd):
                if exists(pair, odd, 0):
                    a = tile_at(pair, 0, odd)
                    pe.wait_ge(o_made, a.count + 1)
                    if exists(pair, odd, -2):
                        pe.wait_ge(oT_copied, a.count - 1)
                    for c in range(KC):
                        mm = nc.tensor.transpose(oT_ps[:, a.slot, c * P:(c + 1) * P], o[:, a.slot, c * P:(c + 1) * P], m.ident[:])
                    mm.then_inc(oT_made, 1)
                if exists(pair, odd, -1):
                    a = tile_at(pair, 0, odd, -1)
                    pe.wait_ge(oT_copied, a.count + 1)
                    if exists(pair, odd, -3):
                        pe.wait_ge(joined, a.count - 1)
                    else:
                        pe.wait_ge(w_in, 32)
                    for c in range(KC):
                        mm = nc.tensor.matmul(y_ps[:, a.slot, 0:D], oT[:, a.slot, c], w[:, c], start=(c == 0), stop=(c == KC - 1))
                    mm.then_inc(y_made, 1)
            stepped(pe, step, 0, NT)

        @block.scalar
        def _(act):
            def step(pair, odd):
                if exists(pair, odd, 0):
                    a = tile_at(pair, 0, odd)
                    act.wait_ge(oT_made, a.count + 1)
                    if exists(pair, odd, -2):
                        act.wait_ge(y_made, a.count - 1)
                    nc.scalar.copy(oT[:, a.slot], oT_ps[:, a.slot, 0:D].rearrange("p (c t) -> p c t", t=P)).then_inc(oT_copied, 1)
                if exists(pair, odd, -1):
                    a = tile_at(pair, 0, odd, -1)
                    act.wait_ge(joined, a.count + 1)
                    nc.scalar.dma_start(m.late_dram[bass.ts(a.place, P)], late[:, a.slot]).then_inc(late_out[a.slot], 16)
            stepped(act, step, 0, NT)
            for slot in range(2):
                act.wait_ge(late_out[slot], 16 * (NT // 2))

        @block.vector
        def _(dve):
            def step(pair, odd):
                if exists(pair, odd, 0):
                    a = tile_at(pair, 0, odd)
                    nc.vector.reciprocal(recip[:, a.slot], m.O[:, a.place, :, HD]).then_inc(recip_made, 1)
                    pass_gate(dve, sem, recip_made, a.count + 1)
                    if exists(pair, odd, -2):
                        pass_gate(dve, sem, oT_made, a.count - 1)
                    nc.vector.tensor_tensor(o[:, a.slot].rearrange("p (h d) -> p h d", d=HD), m.O[:, a.place, :, 0:HD],
                                            recip[:, a.slot].unsqueeze(2).broadcast_to([P, NH, HD]), ALU.mult).then_inc(o_made, 1)
                if exists(pair, odd, -1):
                    a = tile_at(pair, 0, odd, -1)
                    dve.wait_ge(base_made, a.count + 1)
                    if exists(pair, odd, -3):
                        dve.wait_ge(late_out[a.slot], 16 * a.turn)
                    dve.wait_ge(y_made, a.count + 1)
                    nc.vector.tensor_tensor(late[:, a.slot], base[:, a.slot], y_ps[:, a.slot, 0:D], ALU.add).then_inc(joined, 1)
                    pass_gate(dve, sem, joined, a.count + 1)
                    nc.vector.tensor_copy(X[:, a.place], late[:, a.slot])
            stepped(dve, step, 0, NT)

        @block.gpsimd
        def _(pool):
            pool.wait_ge(w_in, 32)

            def step(pair, odd):
                if exists(pair, odd, 0):
                    a = tile_at(pair, 0, odd)
                    pool.wait_ge(mid_in[a.slot], 16 * a.turn + 16)
                    if exists(pair, odd, -2):
                        pool.wait_ge(joined, a.count - 1)
                    nc.gpsimd.tensor_tensor(base[:, a.slot], mid[:, a.slot], bias[:], ALU.add).then_inc(base_made, 1)
            stepped(pool, step, 0, NT)


ATTENTION_SEMS = """h_in:2 rope_in:2 w_attn_in rope_made hT_made hT_copied qkT_made qkT_copied pT_made pT_copied
    scores_made masked nbias_made probs_made rsum_made probs_normal o_summed oT_copied out_made x_added
    qk_made v_made v_copied squared qk_read ssq_made ssq_kept rnorm_made k_turned qk_rotated window_cleared""".split()
MLP_SEMS = """mh_in w_mlp_in stats_made mv_made eps_added rstd_made ln_applied mhT_made mhT_copied ag_made gelu_made
    u_made y_made xb_made mx_added""".split()


class Memory:
    pass


def window_masks():
    i, j = np.arange(P)[:, None], np.arange(P)[None, :]
    own = np.where(j > i, NEG, 0.0)
    past = np.where(j < i, NEG, 0.0)
    even, odd = np.concatenate([own, past], 1), np.concatenate([past, own], 1)
    first = np.concatenate([own, np.full((P, P), NEG)], 1)
    return np.stack([even, odd, first], 1).astype(np.float32)


def window_tables():
    half = np.arange(0, WD, 2, dtype=np.float32)
    inv = (np.float32(1.0) / np.float32(10000.0) ** (half / np.float32(WD))).astype(np.float32)
    t = np.arange(S, dtype=np.float32)
    freqs = t[:, None] * inv[None, :]
    base = (half + np.float32(0.4 * WD)) / np.float32(1.4 * WD)
    power = (t - np.float32(S // 2)) / np.float32(P // 2)
    scale = base[None, :].astype(np.float64) ** power[:, None].astype(np.float64)
    two = lambda a: np.concatenate([a, a], -1)
    cos, sin = two(np.cos(freqs.astype(np.float64))), np.sin(freqs.astype(np.float64))
    sin = np.concatenate([-sin, sin], -1)
    scale = two(scale)
    tables = np.stack([8.0 * cos * scale, 8.0 * sin * scale, cos / scale, sin / scale], 1)
    return np.ascontiguousarray(tables.reshape(NT, P, 4, WD).astype(np.float32))


def build(nc, a, out, stage=99):
    with ExitStack() as ctx:
        m, made = Memory(), {}

        def sb(name, shape, dt=F32):
            return ctx.enter_context(nc.sbuf_tensor(name, shape, dt))

        for name in ATTENTION_SEMS + MLP_SEMS + ["consts_in", "gates_passed"]:
            name, _, n = name.partition(":")
            each = [ctx.enter_context(nc.semaphore(name + (str(i) if n else ""))) for i in range(int(n or 1))]
            made[name] = each if n else each[0]
        sem = namedtuple("Semaphores", made)(**made)

        m.X = sb("X", [P, NT, D])
        m.ident = sb("ident", [P, P])
        m.identb = sb("identb", [P, P], BF16)
        m.cmask = sb("cmask", [P, 3, P], BF16)
        m.masks = sb("masks", [P, 3, 2 * P])
        m.mask_first = m.masks[:, 2]
        m.zeros = sb("zeros", [1, P])
        m.minus_half = sb("minus_half", [P, 2 * WH])
        m.wqkv = sb("wqkv", [P, KC, 3 * INNER])
        m.wo = sb("wo", [P, INNER // P, D])
        m.scales = sb("scales", [P, 4, WD])
        m.w1 = sb("w1", [P, KC, 2 * HID])
        m.w2 = sb("w2", [P, NC, D])
        m.b1 = sb("b1", [P, 2, NC])
        m.ln = sb("ln", [P, 2, KC])
        m.b2 = sb("b2", [P, D])

        m.wqkv_dram = a["wqkv"].rearrange("l (c p) n -> l p c n", p=P)
        m.wo_dram = a["wo"].rearrange("l (c p) n -> l p c n", p=P)
        m.scales_dram = a["scales"]
        m.rope_dram = a["rope"]
        m.cwqkv_dram = a["cwqkv"].rearrange("(c p) n -> p c n", p=P)
        m.cwo_dram = a["cwo"].rearrange("(c p) n -> p c n", p=P)
        m.cbias_dram, m.cbo_dram, m.crope_dram = a["cbias"], a["cbo"], a["crope"]
        m.mid_dram = nc.dram_tensor("mid_dram", [S, D], F32).ap()
        m.late_dram = nc.dram_tensor("late_dram", [S, D], F32).ap()
        m.max_dram = nc.dram_tensor("max_dram", [3, S], BF16).ap()
        m.parts_dram = nc.dram_tensor("parts_dram", [6, D, S], BF16).ap()

        full = HID // P * P
        def mlp_weights(l):
            loads = [(m.w1[:], a["w1"].rearrange("l (c p) n -> l p c n", p=P)[l]),
                     (m.w2[:, 0:NC - 1], a["w2"][:, 0:full].rearrange("l (c p) n -> l p c n", p=P)[l]),
                     (m.w2[0:HID - full, NC - 1], a["w2"][l, full:HID]),
                     (m.ln[:], a["ln"][l]),
                     (m.b1[:], a["b1"][l]),
                     (m.b2[:], a["b2"][l].partition_broadcast(P))]
            return loads
        m.mlp_weights = mlp_weights
        m.half = lambda h, b: (h - b) // 2
        m.w_mlp_count = lambda before: before * (16 * 6 // NG) + 96
        m.w_attn_count = lambda before: before * (48 // (NT // 2)) + 48

        with nc.Block() as block:
            @block.sync
            def _(sp):
                nc.sync.dma_start(m.ident[:], a["ident"]).then_inc(sem.consts_in, 16)
                nc.sync.dma_start(m.masks[:], a["masks"]).then_inc(sem.consts_in, 16)
                nc.sync.dma_start(m.identb[:], a["identb"]).then_inc(sem.consts_in, 16)
                nc.sync.dma_start(m.cmask[:], a["cmask"]).then_inc(sem.consts_in, 16)
                sp.wait_ge(sem.consts_in, 64)

            @block.gpsimd
            def _(pool):
                nc.gpsimd.memset(m.zeros[:], 0.0)
                nc.gpsimd.memset(m.minus_half[:], -0.5)

        def stack(call):
            with nc.Fori(0, DEPTH) as layer:
                m.layer = layer
                m.tag = f"_s{call}"
                window_attention(nc, m, sem, (call * DEPTH + layer) * (NT // 2))
                mlp(nc, m, sem, (call * DEPTH + layer) * NG)

        m.tag = "_in"
        rejoin(nc, m, sem, a["x"], None, None, True)
        stack(0)
        m.tag = "_mid"
        rejoin(nc, m, sem, a["x"], 0.5, m.mid_dram, True)
        with nc.sbuf_tensor("V", [P, NT, NH, HD + 1], F32) as m.V:
            project_heads(nc, m, sem)
            with nc.sbuf_tensor("O", [P, NT, NH, HD + 1], F32) as m.O:
                causal_attention(nc, m, sem)
                project_out(nc, m, sem)
        m.tag = "_late"
        rejoin(nc, m, sem, None, None, None, True)
        stack(1)
        m.tag = "_out"
        rejoin(nc, m, sem, m.late_dram, 0.5, out, False)


def causal_tables():
    dim = np.arange(HD // 2, dtype=np.float32)
    div = np.exp((np.float32(2.0) * dim / np.float32(HD) * np.float32(np.log(10000.0))).astype(np.float32)).astype(np.float32)
    theta = (np.arange(S, dtype=np.float32)[:, None] / div[None, :]).astype(np.float32).astype(np.float64)
    cos = np.repeat(np.cos(theta), 2, -1)
    sin = np.stack([-np.sin(theta), np.sin(theta)], -1).reshape(S, HD)
    both = np.stack([cos, sin], 1)
    tables = np.stack([both * HD ** -0.5, both], 1)
    return np.ascontiguousarray(tables.reshape(NT, P, 2, 2, HD).astype(np.float32))


def causal_masks():
    i, j = np.arange(P)[:, None], np.arange(P)[None, :]
    masks = np.stack([np.full((P, P), NEG), np.where(i > j, NEG, 0.0), np.where(j > i, NEG, 0.0)], 1)
    return np.ascontiguousarray(masks.astype(mybir.dt.np(BF16)))


def arrays(i):
    f = lambda n: np.ascontiguousarray(i["L0_" + n])
    swap = lambda s: np.concatenate([s[:, WD // 2:], s[:, :WD // 2]], 1)
    qs, ks = f("ffn_q_scale"), f("ffn_k_scale")
    b1 = np.zeros((DEPTH, 2, NC * P), np.float32)
    b1[:, :, :HID] = f("ffn_b1").reshape(DEPTH, 2, HID)
    b1 = np.ascontiguousarray(b1.reshape(DEPTH, 2, NC, P).transpose(0, 3, 1, 2))
    ln = np.stack([f("ffn_ln_g"), f("ffn_ln_b")], 1).reshape(DEPTH, 2, KC, P)
    return {
        "x": f("attn_x").reshape(S, D),
        "wqkv": f("ffn_wqkv"), "wo": f("ffn_wo"), "scales": np.ascontiguousarray(np.stack([qs, swap(qs), ks, swap(ks)], 1)),
        "w1": f("ffn_w1"), "b1": b1, "w2": f("ffn_w2"), "b2": f("ffn_b2"), "ln": np.ascontiguousarray(ln.transpose(0, 3, 1, 2)),
        "cwqkv": np.ascontiguousarray(np.concatenate([f("attn_wq").T, f("attn_wk").T, f("attn_wv").T], 1)),
        "cbias": np.concatenate([f("attn_bq"), f("attn_bk"), f("attn_bv")]), "cwo": np.ascontiguousarray(f("attn_wo").T), "cbo": f("attn_bo"),
        "crope": causal_tables(), "cmask": causal_masks(), "identb": np.eye(P, dtype=mybir.dt.np(BF16)),
        "rope": window_tables(), "masks": window_masks(), "ident": np.eye(P, dtype=np.float32),
    }


def kernel(**inputs):
    import concourse.bacc as bacc
    from concourse.bass_utils import run_bass_kernel_spmd

    nc = bacc.Bacc("TRN2", target_bir_lowering=False, num_devices=1)
    laid_out = arrays({name: np.asarray(v) for name, v in inputs.items()})
    tensors = {name: nc.dram_tensor(f"in_{name}_dram", v.shape, mybir.dt.from_np(v.dtype), kind="ExternalInput").ap()
               for name, v in laid_out.items()}
    out = nc.dram_tensor("out_dram", [S, D], F32, kind="ExternalOutput").ap()
    build(nc, tensors, out)
    result = run_bass_kernel_spmd(nc, [{f"in_{name}_dram": v for name, v in laid_out.items()}], core_ids=[0])
    return result.results[0]["out_dram"].reshape(1, S, D)
```

```python
from collections import namedtuple
from contextlib import ExitStack

import numpy as np
import concourse.bass as bass
from concourse import mybir

F32 = mybir.dt.float32
F32R = mybir.dt.float32r
BF16 = mybir.dt.bfloat16
ALU = mybir.AluOpType
ACT = mybir.ActivationFunctionType
AX = mybir.AxisListType

P = 128
D = 256
KC = D // P
S = 4096
NT = S // P
DEPTH = 2
assert DEPTH == 2
WH = 8
WD = 64
INNER = WH * WD
HID = int(D * 4 * 2 / 3)
NC = -(-HID // P)
CW = -(-HID // NC)
NH = 16
HD = D // NH
SPLIT_PRODUCTS = [(0, 0), (0, 1), (1, 0)]
GT = 4
NG = NT // GT
GW = GT * P
NEG = -1e30
EPS = 1e-5

Tile = namedtuple("Tile", "place count slot turn")


def tile_at(pair, before, odd, ahead=0):
    p, slot = pair + (odd + ahead) // 2, (odd + ahead) % 2
    return Tile(2 * p + slot, 2 * (p + before) + slot, slot, p + before)


def exists(pair, odd, ahead):
    return not isinstance(pair, int) or 0 <= 2 * pair + odd + ahead < NT


def pass_gate(eng, sem, semaphore, value):
    eng.wait_ge(semaphore, value)
    eng.sem_inc(sem.gates_passed, 1)


def stepped(eng, step, first, last, peeled=1):
    for s in range(first, 2 * peeled):
        step(s // 2, s % 2)
    with eng.Fori(peeled, NT // 2 - 1) as pair:
        for odd in range(2):
            step(pair, odd)
    for s in range(NT - 2, last + 1):
        step(s // 2, s % 2)


def load_shifted(nc, m, sem, g):
    X, h, first = m.X, m.mlp_h, isinstance(g, int)
    nc.sync.dma_start(h[:, :, 0:P], X[:, bass.ds(g * GT, GT), 0:P]).then_inc(sem.mh_in, 16)
    nc.sync.dma_start(h[1:P, :, P:D], X[0:P - 1, bass.ds(g * GT, GT), P:D]).then_inc(sem.mh_in, 16)
    before_group = m.zeros[0:1, 0:P] if first else X[P - 1:P, g * GT - 1, P:D]
    nc.sync.dma_start(h[0:1, 0, P:D], before_group).then_inc(sem.mh_in, 16)
    nc.sync.dma_start(h[0:1, 1:GT, P:D], X[P - 1:P, bass.ds(g * GT, GT - 1), P:D]).then_inc(sem.mh_in, 16)


def token_statistics(nc, m, sem, dve, count):
    dve.wait_ge(sem.mh_in, 64 * count + 64)
    for t in range(GT):
        nc.vector.bn_stats(m.mlp_stats[:, t], m.mlp_h[:, t]).then_inc(sem.stats_made, 1)
    for t in range(GT):
        pass_gate(dve, sem, sem.stats_made, GT * count + t + 1)
        nc.vector.bn_aggr(m.mlp_mv[:, t], m.mlp_stats[:, t]).then_inc(sem.mv_made, 1)


def token_rstds(nc, m, sem, pool, count):
    pass_gate(pool, sem, sem.mv_made, GT * count + GT)
    nc.gpsimd.tensor_scalar(m.mlp_var[:], m.mlp_mv[:, :, 1], EPS, None, ALU.add).then_inc(sem.eps_added, 1)
    pool.wait_ge(sem.eps_added, count + 1)
    nc.gpsimd.tensor_tensor(m.mlp_rstd[:], m.mlp_var[:], m.minus_half[:, 0:GT], ALU.pow).then_inc(sem.rstd_made, 1)


def layernorm_tokens(nc, m, sem, dve, count):
    dve.wait_ge(sem.rstd_made, count + 1)
    for t in range(GT):
        nc.vector.tensor_scalar(m.mlp_hn[:, t], m.mlp_h[:, t], m.mlp_mv[:, t, 0:1], m.mlp_rstd[:, t:t + 1],
                                ALU.subtract, ALU.mult).then_inc(sem.ln_applied, 1)


def window_attention(nc, m, sem, before):
    with ExitStack() as ctx:
        def sb(name, shape, dt=F32):
            return ctx.enter_context(nc.sbuf_tensor(name + m.tag, shape, dt))

        def ps(name, shape, dt=F32):
            return ctx.enter_context(nc.psum_tensor(name + m.tag, shape, dt))

        X, h = m.X, sb("h", [P, 2, D])
        hT = [sb("hT" + n, [P, 2, KC, P], F32R) for n in ("_high", "_low")]
        w = [sb("wqkv" + n, [P, KC, 3 * INNER], F32R) for n in ("_high", "_low")]
        rope_raw = sb("rope_raw", [P, 2, 4, WD])
        rope = sb("rope", [P, 2, 4, WD])
        squares = sb("squares", [P, 2, INNER])
        ssq = sb("ssq", [P, 2, 2 * WH])
        rnorm = sb("rnorm", [P, 2, 2 * WH])
        turned = sb("turned", [P, 2, INNER])
        crossed = sb("crossed", [P, 2, INNER])
        qk = sb("qk", [P, 2, INNER])
        qT = sb("qT", [P, WH // 2, 2, P])
        kT = sb("kT", [P, WH // 2, 2, P])
        v = sb("v", [P, 2, INNER])
        scores = sb("scores", [P, WH, 2 * P])
        smax = sb("smax", [P, 2, WH])
        nbias = sb("nbias", [P, 2, WH])
        probs = sb("probs", [P, 2, WH, 2 * P])
        psum_row = sb("psum_row", [P, 2, WH])
        rsum = sb("rsum", [P, 2, WH])
        probsT = sb("probsT", [P, WH, 2, P])
        oT = sb("oT", [P, INNER // P, P])

        qkv_ps = ps("qkv_ps", [P, 3, INNER])
        o_ps = ps("o_ps", [P, INNER // P, P])
        ring = ps("ring", [P, 4, INNER])
        QT, KT, HT = 0, 1, 2
        PT = [3, 0, 1, 2]
        SC = [3, 0, 1, 2]
        OUT = 3

        layers = before // (NT // 2)
        groups = layers * NG
        W1_PIECES = [(k, slice(half * HID, (half + 1) * HID)) for k in range(KC) for half in range(2)]
        W_PIECES = [(c, cols) for cols in (slice(0, 2 * INNER), slice(2 * INNER, 3 * INNER)) for c in range(KC)]

        block = ctx.enter_context(nc.Block())

        @block.sync
        def _(sp):
            def load(pair, odd):
                a = tile_at(pair, before, odd)
                if exists(pair, odd, -2):
                    sp.wait_ge(sem.hT_made, a.count - 1)
                    sp.wait_ge(sem.rope_made, a.count - 1)
                nc.sync.dma_start(h[:, a.slot, 0:P], X[:, a.place, 0:P]).then_inc(sem.h_in[a.slot], 16)
                nc.sync.dma_start(h[1:P, a.slot, P:D], X[0:P - 1, a.place, P:D]).then_inc(sem.h_in[a.slot], 16)
                last = m.zeros[0:1, 0:P] if not exists(pair, odd, -1) else X[P - 1:P, a.place - 1, P:D]
                nc.sync.dma_start(h[0:1, a.slot, P:D], last).then_inc(sem.h_in[a.slot], 16)
                nc.sync.dma_start(rope_raw[:, a.slot], m.rope_dram[a.place]).then_inc(sem.rope_in[a.slot], 16)
            for s in range(2):
                load(s // 2, s % 2)
            with sp.Fori(1, NT // 2) as pair:
                for odd in range(2):
                    load(pair, odd)
            for dst, src in m.mlp_weights(m.layer):
                nc.sync.dma_start(dst, src).then_inc(sem.w_mlp_in, 16)
            sp.wait_ge(sem.x_added, 2 * before + GT)
            load_shifted(nc, m, sem, 0)

        @block.tensor
        def _(pe):
            def split_product(j, slot):
                for n, (c, high_or_low) in enumerate((c, parts) for c in range(KC) for parts in SPLIT_PRODUCTS):
                    mm = nc.tensor.matmul(qkv_ps[:, j], hT[high_or_low[0]][:, slot, c], w[high_or_low[1]][:, c, j * INNER:(j + 1) * INNER],
                                          start=(n == 0), stop=(n == KC * len(SPLIT_PRODUCTS) - 1))
                return mm

            def step(pair, odd):
                cur, nxt, nxt2, prv = (tile_at(pair, before, odd, k) for k in (0, 1, 2, -1))
                is_cur, is_nxt, is_nxt2, is_prv = (exists(pair, odd, k) for k in (0, 1, 2, -1))
                is_prv2 = exists(pair, odd, -2)
                if is_cur:
                    pe.wait_ge(sem.qk_rotated, cur.count + 1)
                    for c, slot in ((0, QT), (1, KT)):
                        if is_prv:
                            pe.wait_ge(sem.masked, WH * prv.count + 4 + 2 * c)
                        for j in range(WH // 2):
                            mm = nc.tensor.transpose(ring[:, slot, j * P:(j + 1) * P], qk[:, c, j * P:(j + 1) * P], m.ident[:])
                        mm.then_inc(sem.qkT_made, 1)
                if is_nxt2:
                    pe.wait_ge(sem.h_in[nxt2.slot], 48 * nxt2.turn + 48)
                    if is_prv:
                        pe.wait_ge(sem.masked, WH * prv.count + 8)
                    elif is_nxt:
                        pe.wait_ge(sem.hT_split, nxt.count + 1)
                    for c in range(KC):
                        mm = nc.tensor.transpose(ring[:, HT, c * P:(c + 1) * P], h[:, nxt2.slot, c * P:(c + 1) * P], m.ident[:])
                    mm.then_inc(sem.hT_made, 1)
                if is_prv:
                    for n in range(WH // 2):
                        pe.wait_ge(sem.probs_normal, WH * prv.count + 2 * n + 2)
                        if n == 0 and is_prv2:
                            pe.wait_ge(sem.x_added, prv.count)
                        if n in (1, 2) and is_cur:
                            pe.wait_ge(sem.qkT_copied, 3 * cur.count + n + 1)
                        if n == 3 and is_nxt2:
                            pe.wait_ge(sem.hT_split, nxt2.count + 1)
                        for i in range(2):
                            for b in range(2):
                                mm = nc.tensor.transpose(ring[:, PT[n], (2 * i + b) * P:(2 * i + b + 1) * P],
                                                         probs[:, prv.slot, 2 * n + i, b * P:(b + 1) * P], m.ident[:])
                        mm.then_inc(sem.pT_made, 1)
                if is_cur:
                    pe.wait_ge(sem.qkT_copied, 3 * cur.count + 3)
                    if not is_prv:
                        pe.wait_ge(sem.window_cleared, before // (NT // 2) * 4 + 4)
                        pe.wait_ge(sem.hT_split, nxt2.count + 1)
                    for n in range(WH // 2):
                        if is_prv:
                            pe.wait_ge(sem.pT_copied, 4 * prv.count + n + 1)
                        for i in range(2):
                            mm = nc.tensor.matmul(ring[:, SC[n], i * 2 * P:(i + 1) * 2 * P], qT[:, n, i],
                                                  kT[:, n].rearrange("p b t -> p (b t)"), start=True, stop=True)
                        mm.then_inc(sem.scores_made, 1)
                if is_prv:
                    pe.wait_ge(sem.pT_copied, 4 * prv.count + 4)
                    pe.wait_ge(sem.v_copied, prv.count + 1)
                    if is_prv2:
                        pe.wait_ge(sem.oT_copied, prv.count)
                    for n in range(WH // 2):
                        for b in range(2):
                            for i in range(2):
                                mm = nc.tensor.matmul(o_ps[i * WD:(i + 1) * WD, n], v[:, b, (2 * n + i) * WD:(2 * n + i + 1) * WD],
                                                      probsT[:, 2 * n + i, b], start=(b == 0), stop=(b == 1))
                    mm.then_inc(sem.o_summed, 1)
                if is_nxt2:
                    pe.wait_ge(sem.hT_split, nxt2.count + 1)
                    if not is_nxt:
                        pe.wait_ge(sem.w_split, 4 * layers + 2)
                    else:
                        pe.wait_ge(sem.qk_read, nxt.count + 1)
                    for j in range(2):
                        mm = split_product(j, nxt2.slot)
                    mm.then_inc(sem.qk_made, 1)
                if is_prv:
                    pe.wait_ge(sem.oT_copied, prv.count + 1)
                    if is_cur:
                        pe.wait_ge(sem.masked, WH * cur.count + 2)
                    for j in range(INNER // P):
                        mm = nc.tensor.matmul(ring[:, OUT, 0:D], oT[:, j], m.wo[:, j], start=(j == 0), stop=(j == INNER // P - 1))
                    mm.then_inc(sem.out_made, 1)
                if is_nxt:
                    if is_cur:
                        pe.wait_ge(sem.v_copied, cur.count + 1)
                    else:
                        pe.wait_ge(sem.w_split, 4 * layers + 4)
                    split_product(2, nxt.slot).then_inc(sem.v_made, 1)
            stepped(pe, step, -2, NT)

        @block.scalar
        def _(act):
            def step(pair, odd):
                cur, nxt, nxt2, prv = (tile_at(pair, before, odd, k) for k in (0, 1, 2, -1))
                is_cur, is_nxt, is_nxt2, is_prv = (exists(pair, odd, k) for k in (0, 1, 2, -1))
                if isinstance(pair, int) and 2 * pair + odd == NT - 1:
                    act.wait_ge(sem.w_mlp_in, m.w_mlp_count(groups))
                    for n, (k, cols) in enumerate(W1_PIECES):
                        nc.scalar.copy(m.w1_parts[0][:, k, cols], m.w1[:, k, cols]).then_inc(sem.w1_high_made, 1)
                if is_cur:
                    act.wait_ge(sem.qkT_made, 2 * cur.count + 1)
                    for i in range(2):
                        rows = slice(i * WD, (i + 1) * WD)
                        nc.scalar.copy(qT[rows, :, i], ring[rows, QT].rearrange("p (j t) -> p j t", t=P)).then_inc(sem.qkT_copied, 1)
                    act.wait_ge(sem.qkT_made, 2 * cur.count + 2)
                    nc.scalar.copy(kT[:, :, cur.slot], ring[:, KT].rearrange("p (j t) -> p j t", t=P)).then_inc(sem.qkT_copied, 1)
                if is_nxt2:
                    act.wait_ge(sem.hT_made, nxt2.count + 1)
                    nc.scalar.copy(hT[0][:, nxt2.slot], ring[:, HT, 0:D].rearrange("p (c t) -> p c t", t=P)).then_inc(sem.hT_copied, 1)
                if is_prv:
                    for n in range(WH // 2):
                        act.wait_ge(sem.pT_made, 4 * prv.count + n + 1)
                        nc.scalar.copy(probsT[:, 2 * n:2 * n + 2], ring[:, PT[n]].rearrange("p (i b t) -> p i b t", i=2, b=2)).then_inc(sem.pT_copied, 1)
                if is_cur:
                    for head in range(WH):
                        if head % 4 == 0:
                            act.wait_ge(sem.nbias_made, 2 * cur.count + head // 4 + 1)
                        nc.scalar.activation(probs[:, cur.slot, head], scores[:, head], ACT.Exp,
                                             bias=nbias[:, cur.slot, head:head + 1], scale=rnorm[:, cur.slot, head:head + 1],
                                             accum_out=psum_row[:, cur.slot, head:head + 1]).then_inc(sem.probs_made, 1)
                if is_nxt2:
                    act.wait_ge(sem.qk_made, nxt2.count + 1)
                    if is_nxt:
                        act.wait_ge(sem.ssq_made, nxt.count + 1)
                    for j in range(2):
                        nc.scalar.activation(squares[:, j], qkv_ps[:, j], ACT.Square).then_inc(sem.squared, 1)
            act.wait_ge(sem.w_attn_in, m.w_attn_count(before))
            for c, cols in W_PIECES:
                nc.scalar.copy(w[0][:, c, cols], m.wqkv[:, c, cols]).then_inc(sem.w_high_made, 1)
            stepped(act, step, -2, NT)

        @block.vector
        def _(dve):
            def step(pair, odd):
                cur, nxt, nxt2, prv = (tile_at(pair, before, odd, k) for k in (0, 1, 2, -1))
                is_cur, is_nxt, is_nxt2, is_prv = (exists(pair, odd, k) for k in (0, 1, 2, -1))
                if isinstance(pair, int) and 2 * pair + odd == NT - 1:
                    token_statistics(nc, m, sem, dve, groups)
                if isinstance(pair, int) and 2 * pair + odd == NT:
                    layernorm_tokens(nc, m, sem, dve, groups)
                if is_nxt2:
                    dve.wait_ge(sem.hT_copied, nxt2.count + 1)
                    nc.vector.tensor_tensor(hT[1][:, nxt2.slot], ring[:, HT, 0:D].rearrange("p (c t) -> p c t", t=P),
                                            hT[0][:, nxt2.slot].bitcast(F32), ALU.subtract).then_inc(sem.hT_split, 1)
                if is_cur:
                    mask = m.mask_first if not is_prv else m.masks[:, cur.slot]
                    for head in range(WH):
                        n, i = head // 2, head % 2
                        if i == 0:
                            pass_gate(dve, sem, sem.scores_made, 4 * cur.count + n + 1)
                        nc.vector.tensor_tensor_reduce(out=scores[:, head], in0=ring[:, SC[n], i * 2 * P:(i + 1) * 2 * P], in1=mask,
                                                       scale=1.0, scalar=-3e38, op0=ALU.add, op1=ALU.max,
                                                       accum_out=smax[:, cur.slot, head:head + 1]).then_inc(sem.masked, 1)
                        if head % 4 == 3:
                            k = 4 * (head // 4)
                            dve.wait_ge(sem.masked, WH * cur.count + head + 1)
                            nc.vector.scalar_tensor_tensor(out=nbias[:, cur.slot, k:k + 4], in0=smax[:, cur.slot, k:k + 4], scalar=-1.0,
                                                           in1=rnorm[:, cur.slot, k:k + 4], op0=ALU.mult, op1=ALU.mult).then_inc(sem.nbias_made, 1)
                if is_prv:
                    dve.wait_ge(sem.o_summed, prv.count + 1)
                    nc.vector.tensor_copy(oT[:], o_ps[:]).then_inc(sem.oT_copied, 1)
                if is_cur:
                    dve.wait_ge(sem.v_made, cur.count + 1)
                    nc.vector.tensor_copy(v[:, cur.slot], qkv_ps[:, 2]).then_inc(sem.v_copied, 1)
                    for half in range(2):
                        k = 4 * half
                        dve.wait_ge(sem.probs_made, WH * cur.count + k + 4)
                        nc.vector.reciprocal(rsum[:, cur.slot, k:k + 4], psum_row[:, cur.slot, k:k + 4]).then_inc(sem.rsum_made, 1)
                        dve.wait_ge(sem.rsum_made, 2 * cur.count + half + 1)
                        for head in range(k, k + 4):
                            nc.vector.tensor_scalar(probs[:, cur.slot, head], probs[:, cur.slot, head],
                                                    rsum[:, cur.slot, head:head + 1], None, ALU.mult).then_inc(sem.probs_normal, 1)
                if is_nxt2:
                    dve.wait_ge(sem.squared, 2 * nxt2.count + 2)
                    dve.wait_ge(sem.rope_made, nxt2.count + 1)
                    if is_nxt:
                        dve.wait_ge(sem.qk_rotated, nxt.count + 1)
                    raw = qkv_ps[:, 0:2].rearrange("p c (h d) -> p c h d", d=WD)
                    tab = rope[:, nxt2.slot].rearrange("p (c f) d -> p c f d", f=2)
                    nc.vector.tensor_tensor(turned[:].rearrange("p c (h d) -> p c h d", d=WD), raw,
                                            tab[:, :, 0].unsqueeze(2).broadcast_to([P, 2, WH, WD]), ALU.mult)
                    cr = crossed[:].rearrange("p c (h d) -> p c h d", d=WD)
                    H = WD // 2
                    nc.vector.tensor_tensor(cr[:, :, :, 0:H], raw[:, :, :, H:WD],
                                            tab[:, :, 1, 0:H].unsqueeze(2).broadcast_to([P, 2, WH, H]), ALU.mult)
                    nc.vector.tensor_tensor(cr[:, :, :, H:WD], raw[:, :, :, 0:H],
                                            tab[:, :, 1, H:WD].unsqueeze(2).broadcast_to([P, 2, WH, H]), ALU.mult).then_inc(sem.qk_read, 1)
                if is_prv:
                    dve.wait_ge(sem.out_made, prv.count + 1)
                    nc.vector.tensor_tensor(X[:, prv.place], X[:, prv.place], ring[:, OUT, 0:D], ALU.add).then_inc(sem.x_added, 1)
                if is_nxt2:
                    nc.vector.tensor_reduce(ssq[:, nxt2.slot], squares[:].rearrange("p c (h d) -> p (c h) d", d=WD), AX.X, ALU.add).then_inc(sem.ssq_made, 1)
            for i in range(2):
                nc.vector.memset(qT[i * WD:(i + 1) * WD, :, 1 - i], 0.0).then_inc(sem.window_cleared, 1)
            for n, (c, cols) in enumerate(W_PIECES):
                dve.wait_ge(sem.w_high_made, 4 * layers + n + 1)
                nc.vector.tensor_tensor(w[1][:, c, cols], m.wqkv[:, c, cols], w[0][:, c, cols].bitcast(F32), ALU.subtract).then_inc(sem.w_split, 1)
            stepped(dve, step, -2, NT)

        @block.gpsimd
        def _(pool):
            def scale_tables(pair, odd, ahead):
                a = tile_at(pair, before, odd, ahead)
                pool.wait_ge(sem.rope_in[a.slot], 16 * a.turn + 16)
                if exists(pair, odd, ahead - 2):
                    pool.wait_ge(sem.qk_read, a.count - 1)
                nc.gpsimd.tensor_tensor(rope[:, a.slot], rope_raw[:, a.slot], m.scales[:], ALU.mult).then_inc(sem.rope_made, 1)

            def step(pair, odd):
                cur, last, last2 = (tile_at(pair, before, odd, -k) for k in (0, 1, 2))
                if exists(pair, odd, 1):
                    if not exists(pair, odd, 0):
                        pool.wait_ge(sem.w_attn_in, m.w_attn_count(before))
                    scale_tables(pair, odd, 1)
                if not exists(pair, odd, 0):
                    return
                pass_gate(pool, sem, sem.ssq_made, cur.count + 1)
                nc.gpsimd.tensor_scalar(ssq[:, cur.slot], ssq[:, cur.slot], 1e-24, None, ALU.max).then_inc(sem.ssq_kept, 1)
                pool.wait_ge(sem.ssq_kept, cur.count + 1)
                if exists(pair, odd, -2):
                    pool.wait_ge(sem.probs_made, WH * last2.count + WH)
                nc.gpsimd.tensor_tensor(rnorm[:, cur.slot], ssq[:, cur.slot], m.minus_half[:, 0:2 * WH], ALU.pow).then_inc(sem.rnorm_made, 1)
                nc.gpsimd.tensor_tensor(turned[:, 1], turned[:, 1], crossed[:, 1], ALU.add).then_inc(sem.k_turned, 1)
                if exists(pair, odd, -1):
                    pool.wait_ge(sem.qkT_made, 2 * last.count + 2)
                nc.gpsimd.tensor_tensor(qk[:, 0], turned[:, 0], crossed[:, 0], ALU.add)
                pool.wait_ge(sem.rnorm_made, cur.count + 1)
                pool.wait_ge(sem.k_turned, cur.count + 1)
                nc.gpsimd.tensor_tensor(qk[:, 1].rearrange("p (h d) -> p h d", d=WD), turned[:, 1].rearrange("p (h d) -> p h d", d=WD),
                                        rnorm[:, cur.slot, WH:2 * WH].unsqueeze(2).broadcast_to([P, WH, WD]), ALU.mult).then_inc(sem.qk_rotated, 1)

            nc.gpsimd.memset(kT[:, :, 1], 0.0).then_inc(sem.window_cleared, 1)
            nc.gpsimd.memset(v[:, 1], 0.0).then_inc(sem.window_cleared, 1)
            stepped(pool, step, -1, NT - 1)
            token_rstds(nc, m, sem, pool, groups)
            for n, (k, cols) in enumerate(W1_PIECES):
                pool.wait_ge(sem.w1_high_made, len(W1_PIECES) * layers + n + 1)
                nc.gpsimd.tensor_tensor(m.w1_parts[1][:, k, cols], m.w1[:, k, cols], m.w1_parts[0][:, k, cols].bitcast(F32), ALU.subtract)


def mlp(nc, m, sem, before):
    widths = [min(CW, HID - c * CW) for c in range(NC)]
    with ExitStack() as ctx:
        def sb(name, shape, dt=F32):
            return ctx.enter_context(nc.sbuf_tensor(name + m.tag, shape, dt))

        def ps(name, shape, dt=F32):
            return ctx.enter_context(nc.psum_tensor(name + m.tag, shape, dt))

        X, hn = m.X, m.mlp_hn
        hT = sb("mhT", [P, KC, GW])
        hT_parts = [sb("mhT" + n, [P, KC, GW], F32R) for n in ("_high", "_low")]
        w1 = m.w1_parts
        gate = sb("gate", [P, 2, GW])
        u = sb("u", [P, NC, GW])
        xb = sb("xb", [P, GT, D])
        turn_ps = ps("turn_ps", [P, GT // 2, KC, 2, P])
        ag_ps = ps("ag_ps", [P, 2, 2, GW])
        y_ps = ps("y_ps", [P, 2, 512])

        block = ctx.enter_context(nc.Block())

        def groups(eng, body):
            body(0, before, False, True)
            with eng.Fori(1, NG - 1) as g:
                body(g, before + g, True, True)
            body(NG - 1, before + NG - 1, True, False)

        @block.sync
        def _(sp):
            for dst, src in m.attention_weights(DEPTH - 1 - m.layer):
                nc.sync.dma_start(dst, src).then_inc(sem.w_attn_in, 16)
            with sp.Fori(1, NG) as g:
                sp.wait_ge(sem.ln_applied, GT * (before + g))
                load_shifted(nc, m, sem, g)

        @block.tensor
        def _(pe):
            def turn(count):
                for t in range(GT):
                    pe.wait_ge(sem.ln_applied, GT * count + t + 1)
                    for c in range(KC):
                        mm = nc.tensor.transpose(turn_ps[:, t // 2, c, t % 2], hn[:, t, c * P:(c + 1) * P], m.ident[:])
                    mm.then_inc(sem.mhT_made, 1)

            pe.wait_ge(sem.w_mlp_in, m.w_mlp_count(before))
            turn(before)

            def body(g, count, earlier, more):
                pe.wait_ge(sem.mhT_split, 2 * count + 2)
                for c, w in enumerate(widths):
                    if c >= 2:
                        pe.wait_ge(sem.u_made, NC * count + c - 1)
                    for half in range(2):
                        cols = slice(half * HID + c * CW, half * HID + c * CW + w)
                        for n, (k, parts) in enumerate((k, parts) for k in range(KC) for parts in SPLIT_PRODUCTS):
                            mm = nc.tensor.matmul(ag_ps[0:w, c % 2, half], w1[parts[0]][:, k, cols], hT_parts[parts[1]][:, k],
                                                  start=(n == 0), stop=(n == KC * len(SPLIT_PRODUCTS) - 1))
                    mm.then_inc(sem.ag_made, 1)
                if more:
                    turn(count + 1)
                for t in range(GT):
                    if t == 0:
                        pe.wait_ge(sem.u_made, NC * count + NC)
                    if t >= 2:
                        pe.wait_ge(sem.mx_added, GT * count + t - 1)
                    for c, w in enumerate(widths):
                        mm = nc.tensor.matmul(y_ps[:, t % 2, 0:D], u[0:w, c, t * P:(t + 1) * P], m.w2[0:w, c],
                                              start=(c == 0), stop=(c == NC - 1))
                    mm.then_inc(sem.y_made, 1)
            groups(pe, body)

        @block.scalar
        def _(act):
            def high_parts(half, count):
                cols = slice(half * GW // 2, (half + 1) * GW // 2)
                act.wait_ge(sem.mhT_copied, 2 * count + half + 1)
                nc.scalar.copy(hT_parts[0][:, :, cols], hT[:, :, cols]).then_inc(sem.mhT_high_made, 1)

            act.wait_ge(sem.w_mlp_in, m.w_mlp_count(before))
            for half in range(2):
                high_parts(half, before)

            def body(g, count, earlier, more):
                for c, w in enumerate(widths):
                    act.wait_ge(sem.ag_made, NC * count + c + 1)
                    if c >= 2 or earlier:
                        act.wait_ge(sem.u_made, NC * count + c - 1)
                    nc.scalar.activation(gate[0:w, c % 2], ag_ps[0:w, c % 2, 1], ACT.Gelu, bias=m.b1[0:w, 1, c:c + 1],
                                         scale=1.0).then_inc(sem.gelu_made, 1)
                if more:
                    for half in range(2):
                        high_parts(half, count + 1)
            groups(act, body)

        @block.vector
        def _(dve):
            def hidden(c, w, count):
                dve.wait_ge(sem.gelu_made, NC * count + c + 1)
                nc.vector.scalar_tensor_tensor(out=u[0:w, c], in0=ag_ps[0:w, c % 2, 0], scalar=m.b1[0:w, 0, c:c + 1],
                                               in1=gate[0:w, c % 2], op0=ALU.add, op1=ALU.mult).then_inc(sem.u_made, 1)

            def copy_turned(half, count):
                dve.wait_ge(sem.mhT_made, GT * count + 2 * half + 2)
                for k in range(KC):
                    mm = nc.vector.tensor_scalar(hT[:, k, half * GW // 2:(half + 1) * GW // 2], turn_ps[:, half, k].rearrange("p t c -> p (t c)"),
                                                 m.ln[:, 0, k:k + 1], m.ln[:, 1, k:k + 1], ALU.mult, ALU.add)
                mm.then_inc(sem.mhT_copied, 1)

            def low_parts(half, count):
                cols = slice(half * GW // 2, (half + 1) * GW // 2)
                dve.wait_ge(sem.mhT_high_made, 2 * count + half + 1)
                nc.vector.tensor_tensor(hT_parts[1][:, :, cols], hT[:, :, cols],
                                        hT_parts[0][:, :, cols].bitcast(F32), ALU.subtract).then_inc(sem.mhT_split, 1)

            def turned_parts(count):
                copy_turned(0, count)
                copy_turned(1, count)
                low_parts(0, count)
                low_parts(1, count)

            dve.wait_ge(sem.w_mlp_in, m.w_mlp_count(before))
            turned_parts(before)

            def body(g, count, earlier, more):
                for c, w in enumerate(widths):
                    if c == 2 and more:
                        token_statistics(nc, m, sem, dve, count + 1)
                    if c == 4 and more:
                        layernorm_tokens(nc, m, sem, dve, count + 1)
                    if c == 0 and earlier:
                        dve.wait_ge(sem.y_made, GT * count)
                    hidden(c, w, count)
                if more:
                    turned_parts(count + 1)
                for t in range(GT):
                    dve.wait_ge(sem.y_made, GT * count + t + 1)
                    if t == 0:
                        dve.wait_ge(sem.xb_made, count + 1)
                    nc.vector.tensor_tensor(X[:, g * GT + t], xb[:, t], y_ps[:, t % 2, 0:D], ALU.add).then_inc(sem.mx_added, 1)
            groups(dve, body)

        @block.gpsimd
        def _(pool):
            pass_gate(pool, sem, sem.w_mlp_in, m.w_mlp_count(before))

            def body(g, count, earlier, more):
                if earlier:
                    pool.wait_ge(sem.mx_added, GT * count)
                nc.gpsimd.tensor_tensor(xb[:], X[:, bass.ds(g * GT, GT)], m.b2[:].unsqueeze(1).broadcast_to([P, GT, D]), ALU.add).then_inc(sem.xb_made, 1)
                if more:
                    token_rstds(nc, m, sem, pool, count + 1)
            groups(pool, body)


CT = 4
NQ = NT // CT


def chunk_of(dram, q):
    return dram.rearrange("(t p) d -> p t d", p=P)[:, q * CT:(q + 1) * CT]


def normalise_input(nc, m, sem):
    X = m.X
    with ExitStack() as ctx:
        stats, mv, shifted_var, rstd, shift = (ctx.enter_context(nc.sbuf_tensor("n_" + n, [P, NT, width], F32)) for n, width in
            (("stats", nc.vector.BN_STATS_DIM), ("mv", 2), ("shifted_var", 1), ("rstd", 1), ("shift", 1)))
        x_in = [ctx.enter_context(nc.semaphore(f"n_x_in{q}")) for q in range(NQ)]
        stats_made, mv_made, eps_added, rstd_made, scaled, shift_made = (ctx.enter_context(nc.semaphore("n_" + n)) for n in
            "stats_made mv_made eps_added rstd_made scaled shift_made".split())

        block = ctx.enter_context(nc.Block())

        @block.sync
        def _(sp):
            for q in range(NQ):
                nc.sync.dma_start(X[:, q * CT:(q + 1) * CT], chunk_of(m.x_dram, q)).then_inc(x_in[q], 16)
            for dst, src in m.attention_weights(0):
                nc.sync.dma_start(dst, src).then_inc(sem.w_attn_in, 16)

        @block.vector
        def _(dve):
            for q in range(NQ):
                dve.wait_ge(x_in[q], 16)
                for t in range(q * CT, (q + 1) * CT):
                    nc.vector.bn_stats(stats[:, t], X[:, t]).then_inc(stats_made, 1)
                for t in range(q * CT, (q + 1) * CT):
                    dve.wait_ge(stats_made, t + 1)
                    nc.vector.bn_aggr(mv[:, t], stats[:, t]).then_inc(mv_made, 1)

        @block.gpsimd
        def _(pool):
            for q in range(NQ):
                chunk = slice(q * CT, (q + 1) * CT)
                pool.wait_ge(mv_made, CT * (q + 1))
                nc.gpsimd.tensor_scalar(shifted_var[:, chunk, 0], mv[:, chunk, 1], EPS, None, ALU.add).then_inc(eps_added, 1)
                pool.wait_ge(eps_added, q + 1)
                nc.gpsimd.tensor_tensor(rstd[:, chunk, 0], shifted_var[:, chunk, 0], m.minus_half[:, 0:CT], ALU.pow).then_inc(rstd_made, 1)
                pool.wait_ge(rstd_made, q + 1)
                nc.gpsimd.tensor_tensor(shift[:, chunk, 0], mv[:, chunk, 0], rstd[:, chunk, 0], ALU.mult).then_inc(scaled, 1)
                pool.wait_ge(scaled, q + 1)
                nc.gpsimd.tensor_scalar(shift[:, chunk, 0], shift[:, chunk, 0], -1.0, None, ALU.mult).then_inc(shift_made, 1)

        @block.scalar
        def _(act):
            for q in range(NQ):
                act.wait_ge(shift_made, q + 1)
                for t in range(q * CT, (q + 1) * CT):
                    nc.scalar.activation(X[:, t], X[:, t], ACT.Identity, bias=shift[:, t], scale=rstd[:, t])


def join_output(nc, m, out):
    X = m.X
    with ExitStack() as ctx:
        late = ctx.enter_context(nc.sbuf_tensor("j_late", [P, NT, D], F32))
        late_in = [ctx.enter_context(nc.semaphore(f"j_late_in{q}")) for q in range(NQ)]
        joined, stored = (ctx.enter_context(nc.semaphore("j_" + n)) for n in ("joined", "stored"))

        block = ctx.enter_context(nc.Block())

        @block.sync
        def _(sp):
            for q in range(NQ):
                nc.sync.dma_start(late[:, q * CT:(q + 1) * CT], chunk_of(m.late_dram, q)).then_inc(late_in[q], 16)

        @block.vector
        def _(dve):
            for q in range(NQ):
                dve.wait_ge(late_in[q], 16)
                x = X[:, q * CT:(q + 1) * CT].rearrange("p t d -> p (t d)")
                nc.vector.scalar_tensor_tensor(out=x, in0=x, scalar=0.5, in1=late[:, q * CT:(q + 1) * CT].rearrange("p t d -> p (t d)"),
                                               op0=ALU.mult, op1=ALU.add).then_inc(joined, 1)

        @block.scalar
        def _(act):
            for q in range(NQ):
                act.wait_ge(joined, q + 1)
                nc.scalar.dma_start(chunk_of(out, q), X[:, q * CT:(q + 1) * CT]).then_inc(stored, 16)
            act.wait_ge(stored, 16 * NQ)


def project_heads(nc, m, sem):
    X = m.X
    with ExitStack() as ctx:
        def sb(name, shape, dt=F32):
            return ctx.enter_context(nc.sbuf_tensor(name, shape, dt))

        def ps(name, shape, dt=F32):
            return ctx.enter_context(nc.psum_tensor(name, shape, dt))

        names = """c_w_in c_xT_made c_xT_copied qk_summed v_summed v_biased qk_biased turned_made crossed_made rot_made high_made
            rest_made mid_made parts_made partsT_made partsT_copied""".split()
        (w_in, xT_made, xT_copied, qk_summed, v_summed, v_biased, qk_biased, turned_made, crossed_made, rot_made, high_made,
         rest_made, mid_made, parts_made, partsT_made, partsT_copied) = (ctx.enter_context(nc.semaphore(n)) for n in names)
        base_in = [ctx.enter_context(nc.semaphore(f"c_base_in{i}")) for i in range(2)]
        mid_out = [ctx.enter_context(nc.semaphore(f"c_mid_out{i}")) for i in range(2)]
        joined, stats_made, mv_made, eps_added, rstd_made, shift_made, ln_applied = (ctx.enter_context(nc.semaphore("c_" + n)) for n in
            "joined stats_made mv_made eps_added rstd_made shift_made ln_applied".split())
        tab_in = [ctx.enter_context(nc.semaphore(f"c_tab_in{i}")) for i in range(2)]
        parts_out = [ctx.enter_context(nc.semaphore(f"c_parts_out{i}")) for i in range(2)]

        w = sb("c_w", [P, KC, 3 * D])
        bias = sb("c_bias", [P, 3 * D])
        base = sb("c_base", [P, 2, D])
        mid = sb("c_mid", [P, 2, D])
        stats = sb("c_stats", [P, 2, nc.vector.BN_STATS_DIM])
        mv = sb("c_mv", [P, 2, 2])
        shifted_var = sb("c_shifted_var", [P, 2, 1])
        rstd = sb("c_rstd", [P, 2, 1])
        shift = sb("c_shift", [P, 2, 1])
        x = sb("c_x", [P, 2, D])
        tab = sb("c_tab", [P, 2, 2, 2, HD])
        xT = sb("c_xT", [P, 2, KC, P])
        qkb = sb("c_qkb", [P, 2, 2, D])
        turned = sb("c_turned", [P, 2, 2, D])
        crossed = sb("c_crossed", [P, 2, 2, D])
        rot = sb("c_rot", [P, 2, 2, D])
        rest = sb("c_rest", [P, 2, 2, D])
        parts = sb("c_parts", [P, 2, 2, 3, D], BF16)
        partsT = sb("c_partsT", [P, 2, 12, P], BF16)
        xT_ps = ps("c_xT_ps", [P, 512])
        qk_ps = ps("c_qk_ps", [P, 2, 2 * D])
        v_ps = ps("c_v_ps", [P, 512])
        partsT_ps = ps("c_partsT_ps", [P, 2, 8, P], BF16)

        block = ctx.enter_context(nc.Block())

        @block.sync
        def _(sp):
            nc.sync.dma_start(w[:], m.cwqkv_dram).then_inc(w_in, 16)
            nc.sync.dma_start(bias[:], m.cbias_dram.partition_broadcast(P)).then_inc(w_in, 16)

            def load(pair, odd):
                if exists(pair, odd, -1):
                    a = tile_at(pair, 0, odd, -1)
                    sp.wait_ge(joined, a.count + 1)
                    nc.sync.dma_start(m.mid_dram[bass.ts(a.place, P)], mid[:, a.slot]).then_inc(mid_out[a.slot], 16)
                if exists(pair, odd, 1):
                    a = tile_at(pair, 0, odd, 1)
                    nc.sync.dma_start(base[:, a.slot], m.x_dram[bass.ts(a.place, P)]).then_inc(base_in[a.slot], 16)
                if exists(pair, odd, 0):
                    a = tile_at(pair, 0, odd)
                    if exists(pair, odd, -2):
                        sp.wait_ge(crossed_made, a.count - 1)
                        sp.wait_ge(turned_made, a.count - 1)
                    nc.sync.dma_start(tab[:, a.slot], m.crope_dram[a.place]).then_inc(tab_in[a.slot], 16)
            stepped(sp, load, -1, NT)
            for slot in range(2):
                sp.wait_ge(mid_out[slot], 16 * (NT // 2))
                sp.wait_ge(parts_out[slot], 16 * (NT // 2))

        @block.tensor
        def _(pe):
            def step(pair, odd):
                if exists(pair, odd, 0):
                    a = tile_at(pair, 0, odd)
                    pe.wait_ge(xT_copied, a.count + 1)
                    if exists(pair, odd, -2):
                        pe.wait_ge(qk_biased, a.count - 1)
                    elif not exists(pair, odd, -1):
                        pe.wait_ge(w_in, 32)
                    for c in range(KC):
                        mm = nc.tensor.matmul(qk_ps[:, a.slot], xT[:, a.slot, c], w[:, c, 0:2 * D], start=(c == 0), stop=(c == KC - 1))
                    mm.then_inc(qk_summed, 1)
                if exists(pair, odd, 1):
                    a = tile_at(pair, 0, odd, 1)
                    pe.wait_ge(ln_applied, a.count + 1)
                    if exists(pair, odd, 0):
                        pe.wait_ge(xT_copied, a.count)
                    for c in range(KC):
                        mm = nc.tensor.transpose(xT_ps[:, c * P:(c + 1) * P], x[:, a.slot, c * P:(c + 1) * P], m.ident[:])
                    mm.then_inc(xT_made, 1)
                if exists(pair, odd, -3):
                    a = tile_at(pair, 0, odd, -3)
                    pe.wait_ge(parts_made, a.count + 1)
                    for qk in range(2):
                        if exists(pair, odd, -4):
                            pe.wait_ge(partsT_copied, 2 * a.count - 1 + qk)
                        for n in range(6):
                            mm = nc.tensor.transpose(partsT_ps[:, qk, n], parts[:, a.slot, qk, n // 2, (n % 2) * P:(n % 2 + 1) * P], m.identb[:])
                        mm.then_inc(partsT_made, 1)
                if exists(pair, odd, 0):
                    a = tile_at(pair, 0, odd)
                    if exists(pair, odd, -1):
                        pe.wait_ge(v_biased, a.count)
                    for c in range(KC):
                        mm = nc.tensor.matmul(v_ps[:, 0:D], xT[:, a.slot, c], w[:, c, 2 * D:3 * D], start=(c == 0), stop=(c == KC - 1))
                    mm.then_inc(v_summed, 1)
            stepped(pe, step, -1, NT + 2, 2)

        @block.scalar
        def _(act):
            def step(pair, odd):
                if exists(pair, odd, -2):
                    a = tile_at(pair, 0, odd, -2)
                    act.wait_ge(rest_made, a.count + 1)
                    nc.scalar.copy(parts[:, a.slot, :, 1], rest[:, a.slot]).then_inc(mid_made, 1)
                if exists(pair, odd, 1):
                    a = tile_at(pair, 0, odd, 1)
                    act.wait_ge(xT_made, a.count + 1)
                    nc.scalar.copy(xT[:, a.slot], xT_ps[:, 0:D].rearrange("p (c t) -> p c t", t=P)).then_inc(xT_copied, 1)
                if exists(pair, odd, -3):
                    a = tile_at(pair, 0, odd, -3)
                    if exists(pair, odd, -5):
                        act.wait_ge(parts_out[a.slot], 16 * a.turn)
                    for qk in range(2):
                        act.wait_ge(partsT_made, 2 * a.count + 1 + qk)
                        nc.scalar.copy(partsT[:, a.slot, 6 * qk:6 * qk + 6], partsT_ps[:, qk, 0:6]).then_inc(partsT_copied, 1)
                    act.wait_ge(partsT_copied, 2 * a.count + 2)
                    nc.scalar.dma_start(m.parts_dram.rearrange("a (b p) s -> p (a b) s", p=P)[:, :, bass.ts(a.place, P)],
                                        partsT[:, a.slot]).then_inc(parts_out[a.slot], 16)
                if exists(pair, odd, -1):
                    a = tile_at(pair, 0, odd, -1)
                    act.wait_ge(rot_made, a.count + 1)
                    if exists(pair, odd, -3):
                        act.wait_ge(partsT_made, 2 * a.count - 2)
                    nc.scalar.copy(parts[:, a.slot, :, 0], rot[:, a.slot]).then_inc(high_made, 1)
                if exists(pair, odd, 2):
                    a = tile_at(pair, 0, odd, 2)
                    if exists(pair, odd, 0):
                        act.wait_ge(xT_made, a.count - 1)
                    act.wait_ge(shift_made, a.count + 1)
                    nc.scalar.activation(x[:, a.slot], mid[:, a.slot], ACT.Identity, bias=shift[:, a.slot], scale=rstd[:, a.slot]).then_inc(ln_applied, 1)
            stepped(act, step, -2, NT + 2, 3)

        @block.vector
        def _(dve):
            def step(pair, odd):
                if exists(pair, odd, 2):
                    a = tile_at(pair, 0, odd, 2)
                    if exists(pair, odd, 0):
                        dve.wait_ge(mid_out[a.slot], 16 * a.turn)
                        dve.wait_ge(ln_applied, a.count - 1)
                    dve.wait_ge(base_in[a.slot], 16 * a.turn + 16)
                    nc.vector.scalar_tensor_tensor(out=mid[:, a.slot], in0=X[:, a.place], scalar=0.5, in1=base[:, a.slot],
                                                   op0=ALU.mult, op1=ALU.add).then_inc(joined, 1)
                    pass_gate(dve, sem, joined, a.count + 1)
                    nc.vector.bn_stats(stats[:, a.slot], mid[:, a.slot]).then_inc(stats_made, 1)
                    pass_gate(dve, sem, stats_made, a.count + 1)
                    nc.vector.bn_aggr(mv[:, a.slot], stats[:, a.slot]).then_inc(mv_made, 1)
                if exists(pair, odd, 0) and not exists(pair, odd, -1):
                    dve.wait_ge(w_in, 32)
                if exists(pair, odd, -2):
                    a = tile_at(pair, 0, odd, -2)
                    dve.wait_ge(high_made, a.count + 1)
                    nc.vector.tensor_tensor(rest[:, a.slot], rot[:, a.slot], parts[:, a.slot, :, 0], ALU.subtract).then_inc(rest_made, 1)
                if exists(pair, odd, 0):
                    a = tile_at(pair, 0, odd)
                    dve.wait_ge(qk_summed, a.count + 1)
                    if exists(pair, odd, -2):
                        dve.wait_ge(crossed_made, a.count - 1)
                    nc.vector.tensor_tensor(qkb[:, a.slot].rearrange("p c n -> p (c n)"), qk_ps[:, a.slot], bias[:, 0:2 * D], ALU.add).then_inc(qk_biased, 1)
                    if exists(pair, odd, -2):
                        dve.wait_ge(rot_made, a.count - 1)
                    dve.wait_ge(tab_in[a.slot], 16 * a.turn + 16)
                    dve.wait_ge(qk_biased, a.count + 1)
                    nc.vector.tensor_tensor(turned[:, a.slot].rearrange("p c (h d) -> p c h d", d=HD),
                                            qkb[:, a.slot].rearrange("p c (h d) -> p c h d", d=HD),
                                            tab[:, a.slot, :, 0].unsqueeze(2).broadcast_to([P, 2, NH, HD]), ALU.mult).then_inc(turned_made, 1)
                if exists(pair, odd, -2):
                    a = tile_at(pair, 0, odd, -2)
                    dve.wait_ge(mid_made, a.count + 1)
                    nc.vector.tensor_tensor(parts[:, a.slot, :, 2], rest[:, a.slot], parts[:, a.slot, :, 1], ALU.subtract).then_inc(parts_made, 1)
                if exists(pair, odd, 0):
                    a = tile_at(pair, 0, odd)
                    pass_gate(dve, sem, v_summed, a.count + 1)
                    nc.vector.tensor_tensor(m.V[:, a.place, :, 0:HD], v_ps[:, 0:D].rearrange("p (h d) -> p h d", d=HD),
                                            bias[:, 2 * D:3 * D].rearrange("p (h d) -> p h d", d=HD), ALU.add).then_inc(v_biased, 1)
            stepped(dve, step, -2, NT + 1)

        @block.gpsimd
        def _(pool):
            nc.gpsimd.memset(m.V[:, :, :, HD:HD + 1], 1.0)

            def step(pair, odd):
                if exists(pair, odd, 2):
                    a = tile_at(pair, 0, odd, 2)
                    pass_gate(pool, sem, mv_made, a.count + 1)
                    nc.gpsimd.tensor_scalar(shifted_var[:, a.slot], mv[:, a.slot, 1:2], EPS, None, ALU.add).then_inc(eps_added, 1)
                    if exists(pair, odd, 0):
                        pool.wait_ge(ln_applied, a.count - 1)
                    pool.wait_ge(eps_added, a.count + 1)
                    nc.gpsimd.tensor_tensor(rstd[:, a.slot], shifted_var[:, a.slot], m.minus_half[:, 0:1], ALU.pow).then_inc(rstd_made, 1)
                    pass_gate(pool, sem, rstd_made, a.count + 1)
                    nc.gpsimd.tensor_scalar(shift[:, a.slot], mv[:, a.slot, 0:1], rstd[:, a.slot], -1.0, ALU.mult, ALU.mult).then_inc(shift_made, 1)
                if not exists(pair, odd, 0):
                    return
                a = tile_at(pair, 0, odd)
                pool.wait_ge(tab_in[a.slot], 16 * a.turn + 16)
                pool.wait_ge(qk_biased, a.count + 1)
                if exists(pair, odd, -2):
                    pool.wait_ge(rot_made, a.count - 1)
                for c in range(2):
                    for e in range(2):
                        mm = nc.gpsimd.tensor_tensor(
                            crossed[:, a.slot, c].rearrange("p (h n two) -> p h n two", two=2, h=NH)[:, :, :, e],
                            qkb[:, a.slot, c].rearrange("p (h n two) -> p h n two", two=2, h=NH)[:, :, :, 1 - e],
                            tab[:, a.slot, c, 1].rearrange("p (n two) -> p n two", two=2)[:, :, e].unsqueeze(1).broadcast_to([P, NH, HD // 2]), ALU.mult)
                mm.then_inc(crossed_made, 1)
                pool.wait_ge(crossed_made, a.count + 1)
                pool.wait_ge(turned_made, a.count + 1)
                if exists(pair, odd, -2):
                    pool.wait_ge(parts_made, a.count - 1)
                nc.gpsimd.tensor_tensor(rot[:, a.slot], turned[:, a.slot], crossed[:, a.slot], ALU.add).then_inc(rot_made, 1)
            stepped(pool, step, -2, NT + 1)


Q_PARTS = [0, 0, 0, 1, 1, 2]
K_PARTS = [0, 1, 2, 0, 1, 0]
SROWS = len(Q_PARTS) * HD
MROWS = SROWS + 3
PAIRS = [(g, j) for g in range(NG) for j in range(0, GT * (g + 1), 2)]
NQUAD = len(PAIRS) // 2
GROUP_END = {(g + 1) * (g + 2) // 2 - 1: g for g in range(NG)}
CHUNKS = [(t, c) for t in range(NT) for c in range(t // GT + 1)]
LEAD, TRAIL = 2, 5


def quad_items():
    items = [[] for _ in range(NQUAD)]
    for i in range(len(CHUNKS)):
        items[LEAD + i * (NQUAD - LEAD - TRAIL) // len(CHUNKS)].append(("chunk", i))
    items[NQUAD - TRAIL + 1].append(("maxima", 0))
    for quad, g in GROUP_END.items():
        if g < NG - 1:
            items[quad + 1].append(("sums", g))
    return items


ITEMS = quad_items()
FIRST_ITEMS = [("chunk", i) for i in range(len(CHUNKS))] + [("maxima", 0)]
HEAD_ITEMS = [item for quad in ITEMS for item in quad] + [("sums", NG - 1)]
LAST_ITEMS = [item for item in HEAD_ITEMS if item[0] == "sums"]
FREE_ST, FREE_PROBS, FREE_O = 2, 4, 1
ITEM_BANKS = 3
assert len(HEAD_ITEMS) % ITEM_BANKS == 0


def item_count(h, item, more):
    if isinstance(h, int) and h < 0:
        return FIRST_ITEMS.index(item)
    return len(FIRST_ITEMS) + len(HEAD_ITEMS) * h + (HEAD_ITEMS if more else LAST_ITEMS).index(item)


def item_slot(h, b, item, more):
    return item_count(h if isinstance(h, int) and h < 0 else b, item, more) % ITEM_BANKS


def causal_attention(nc, m, sem):
    with ExitStack() as ctx:
        def sb(name, shape, dt=F32):
            return ctx.enter_context(nc.sbuf_tensor(name, shape, dt))

        def ps(name, shape, dt=F32):
            return ctx.enter_context(nc.psum_tensor(name, shape, dt))

        names = "s_made s_read st_made exp_made pv_done o_read v_cleared v_in max_made split_made maxT_copied max_in max_row_in rows_set".split()
        (s_made, s_read, st_made, exp_made, pv_done, o_read, v_cleared, v_in, max_made, split_made, maxT_copied, max_in, max_row_in,
         rows_set) = (ctx.enter_context(nc.semaphore("d_" + n)) for n in names)
        stack_in = [ctx.enter_context(nc.semaphore(f"d_stack_in{i}")) for i in range(2)]

        q = sb("d_q", [P, 2, S], BF16)
        k = sb("d_k", [P, 2, S], BF16)
        probs = sb("d_probs", [P, 4, 2, GW])
        vh = sb("d_v", [P, 2, NT, 32])
        no_v = sb("d_no_v", [P, 32], BF16)
        sums = sb("d_sums", [P, 2, GW])
        chunk_max = sb("d_chunk_max", [P, NT, NG])
        neg_max = sb("d_neg_max", [P, NT])
        max_rest = sb("d_max_rest", [P, NT])
        max_parts = sb("d_max_parts", [P, 3, NT], BF16)
        maxT = sb("d_maxT", [3 * NT, P], BF16)
        st = ps("d_st", [P, 2, 2, GW])
        s_ps = ps("d_s", [P, ITEM_BANKS, GW])
        o_ps = ps("d_o", [P, GW])

        block = ctx.enter_context(nc.Block())

        def heads(eng, body):
            with eng.Fori(0, NH // 2 - 1) as pair:
                for b in range(2):
                    body(2 * pair + b, b, True)
            body(NH - 2, 0, True)
            body(NH - 1, 1, False)

        @block.sync
        def _(sp):
            def load(h, b):
                for n, part in enumerate(Q_PARTS):
                    nc.sync.dma_start(q[n * HD:(n + 1) * HD, b], m.parts_dram[part, bass.ds(h * HD, HD)]).then_inc(stack_in[b], 16)
                for n, part in enumerate(K_PARTS):
                    nc.sync.dma_start(k[n * HD:(n + 1) * HD, b], m.parts_dram[3 + part, bass.ds(h * HD, HD)]).then_inc(stack_in[b], 16)

            def max_rows(h, b):
                sp.wait_ge(maxT_copied, h + 1)
                nc.sync.dma_start(m.max_dram.rearrange("a (t c) -> (a t) c", c=P), maxT[:]).then_inc(max_row_in, 16)
                sp.wait_ge(max_row_in, 16 * h + 16)
                nc.sync.dma_start(q[SROWS:MROWS, b], m.max_dram).then_inc(max_in, 16)
            load(0, 0)
            load(1, 1)
            max_rows(0, 0)

            def body(h, b, more):
                if more:
                    max_rows(h + 1, 1 - b)
                if more and not (isinstance(h, int) and h + 2 >= NH):
                    sp.wait_ge(exp_made, FREE_ST + len(PAIRS) * (h + 1))
                    load(h + 2, b)
            heads(sp, body)

        @block.tensor
        def _(pe):
            def chunk(h, b, i, slot):
                t, c = CHUNKS[i]
                w = min(GW, (t + 1) * P - c * GW)
                if i == 0:
                    pe.wait_ge(stack_in[b], 192 * ((h - b) // 2) + 192)
                last = c == t // GT
                mm = nc.tensor.matmul(s_ps[:, slot, 0:w], q[0:SROWS, b, t * P:(t + 1) * P], k[0:SROWS, b, c * GW:c * GW + w],
                                      start=True, stop=not last)
                if last:
                    mm = nc.tensor.matmul(s_ps[:, slot, w - P:w], m.identb[:], m.cmask[:, 2], start=False, stop=True)
                mm.then_inc(s_made, 1)

            def item(h, b, which, more):
                n, slot = item_count(h, which, more), item_slot(h, b, which, more)
                if not (isinstance(n, int) and n < ITEM_BANKS):
                    pe.wait_ge(s_read, n - ITEM_BANKS + 1)
                kind, i = which
                if kind == "chunk":
                    chunk(h + 1, 1 - b, i, slot)
                elif kind == "maxima":
                    pe.wait_ge(split_made, h + 2)
                    nc.tensor.transpose(s_ps[0:3 * NT, slot, 0:P // 2].bitcast(BF16), max_parts[:].rearrange("p a t -> p (a t)"),
                                        m.identb[:]).then_inc(s_made, 1)
                else:
                    pe.wait_ge(o_read, FREE_O + NG * h + i + 1)
                    for t in range(GT):
                        mm = nc.tensor.transpose(s_ps[:, slot, t * P:(t + 1) * P], sums[:, i % 2, t * P:(t + 1) * P], m.ident[:])
                    mm.then_inc(s_made, 1)

            def scores(h, b, n):
                g, j0 = PAIRS[n]
                col = P * max(0, j0 - GT * g)
                if n == 0:
                    pe.wait_ge(max_in, 16 * h + 16)
                pe.wait_ge(exp_made, FREE_ST + len(PAIRS) * h + n - 1)
                for j in range(2):
                    diagonal = j0 >= GT * g
                    mm = nc.tensor.matmul(st[:, n % 2, j, col:GW], k[0:MROWS, b, (j0 + j) * P:(j0 + j + 1) * P],
                                          q[0:MROWS, b, g * GW + col:(g + 1) * GW], start=True, stop=not diagonal)
                    if diagonal:
                        mm = nc.tensor.matmul(st[:, n % 2, j, col:col + P * (j + 1)], m.identb[:],
                                              m.cmask[:, 1 - j:2].rearrange("p a i -> p (a i)"), start=False, stop=True)
                mm.then_inc(st_made, 1)

            def sum_values(h, b, quad):
                g, j0 = PAIRS[2 * quad]
                pe.wait_ge(exp_made, FREE_ST + len(PAIRS) * h + 2 * quad + 2)
                if quad == 0:
                    pe.wait_ge(v_in, h + 1)
                if j0 == 0:
                    pe.wait_ge(o_read, FREE_O + NG * h + g)
                if g == 0:
                    for c in range(4):
                        nc.tensor.matmul(o_ps[32 * c:32 * c + 32], no_v[0:SROWS], k[0:SROWS, b, 0:GW],
                                         start=True, stop=False, skip_group_check=True)
                for c in range(4):
                    col = P * c if j0 == GT * g else 0
                    mm = nc.tensor.matmul(o_ps[32 * c:32 * c + 32, col:GW], vh[:, b, j0 + c],
                                          probs[:, (2 * quad + c // 2) % 4, c % 2, col:GW],
                                          start=(j0 == 0 and g > 0), stop=(j0 == GT * g), skip_group_check=True)
                mm.then_inc(pv_done, 2)

            pe.sem_inc(pv_done, FREE_PROBS)
            pe.wait_ge(rows_set, 3)
            for which in FIRST_ITEMS:
                item(-1, 1, which, True)
            for n in range(2):
                scores(0, 0, n)

            def body(h, b, more):
                for quad in range(NQUAD):
                    items = [i for i in ITEMS[quad] if more or i[0] == "sums"]
                    third = -(-len(items) // 3)
                    for which in items[:third]:
                        item(h, b, which, more)
                    for j in range(2):
                        if quad + 1 < NQUAD:
                            scores(h, b, 2 * quad + 2 + j)
                        elif more:
                            scores(h + 1, 1 - b, j)
                        for which in items[third * (j + 1):third * (j + 2)]:
                            item(h, b, which, more)
                    sum_values(h, b, quad)
                item(h, b, ("sums", NG - 1), more)
            heads(pe, body)

        @block.scalar
        def _(act):
            act.sem_inc(exp_made, FREE_ST)
            act.sem_inc(o_read, FREE_O)

            def copy_sums(h, g):
                quad = (g + 1) * (g + 2) // 2 - 1
                act.wait_ge(pv_done, FREE_PROBS + len(PAIRS) * h + 2 * quad + 2)
                nc.scalar.copy(sums[:, g % 2], o_ps[:]).then_inc(o_read, 1)

            def exponentials(h, n):
                g, j0 = PAIRS[n]
                col = P * max(0, j0 - GT * g)
                act.wait_ge(st_made, len(PAIRS) * h + n + 1)
                act.wait_ge(pv_done, FREE_PROBS + len(PAIRS) * h + n - 3)
                nc.scalar.activation(probs[:, n % 4, :, col:GW], st[:, n % 2, :, col:GW], ACT.Exp).then_inc(exp_made, 1)

            exponentials(0, 0)

            def body(h, b, more):
                for n in range(1, len(PAIRS)):
                    exponentials(h, n)
                    if n % 2 == 0 and n // 2 - 1 in GROUP_END:
                        copy_sums(h, GROUP_END[n // 2 - 1])
                if more:
                    exponentials(h + 1, 0)
                copy_sums(h, NG - 1)
            heads(act, body)

        @block.vector
        def _(dve):
            def split_maxima(h):
                nc.vector.tensor_reduce(neg_max[:], chunk_max[:], AX.X, ALU.max, negate=True).then_inc(max_made, 1)
                dve.wait_ge(max_made, 4 * h + 1)
                nc.vector.tensor_copy(max_parts[:, 0], neg_max[:]).then_inc(max_made, 1)
                dve.wait_ge(max_made, 4 * h + 2)
                nc.vector.tensor_tensor(max_rest[:], neg_max[:], max_parts[:, 0], ALU.subtract).then_inc(max_made, 1)
                dve.wait_ge(max_made, 4 * h + 3)
                nc.vector.tensor_copy(max_parts[:, 1], max_rest[:]).then_inc(max_made, 1)
                dve.wait_ge(max_made, 4 * h + 4)
                nc.vector.tensor_tensor(max_parts[:, 2], max_rest[:], max_parts[:, 1], ALU.subtract).then_inc(split_made, 1)

            def item(h, b, which, more):
                n, slot = item_count(h, which, more), item_slot(h, b, which, more)
                kind, i = which
                if kind == "chunk":
                    t, c = CHUNKS[i]
                    w = min(GW, (t + 1) * P - c * GW)
                    dve.wait_ge(s_made, n + 1)
                    nc.vector.tensor_reduce(chunk_max[:, t, c:c + 1], s_ps[:, slot, 0:w], AX.X, ALU.max).then_inc(s_read, 1)
                    if i == len(CHUNKS) - 1:
                        dve.wait_ge(s_read, n + 1)
                        split_maxima(h + 1)
                elif kind == "maxima":
                    dve.wait_ge(s_made, n + 1)
                    if not (isinstance(h, int) and h < 0):
                        dve.wait_ge(max_row_in, 16 * (h + 1))
                    nc.vector.tensor_copy(maxT[:], s_ps[0:3 * NT, slot, 0:P // 2].bitcast(BF16)).then_inc(s_read, 1)
                    dve.wait_ge(s_read, n + 1)
                    dve.sem_inc(maxT_copied, 1)
                else:
                    pass_gate(dve, sem, s_made, n + 1)
                    nc.vector.tensor_reduce(m.O[:, GT * i:GT * (i + 1), h],
                                            s_ps[:, slot].rearrange("p (t c d) -> p t d c", t=GT, c=4)[:, :, 0:HD + 1],
                                            AX.X, ALU.add).then_inc(s_read, 1)

            nc.vector.memset(k[SROWS:MROWS], 1.0).then_inc(rows_set, 1)
            nc.vector.memset(no_v[:], 0.0).then_inc(rows_set, 1)
            nc.vector.memset(chunk_max[:], -3e38).then_inc(rows_set, 1)
            dve.wait_ge(rows_set, 3)
            for which in FIRST_ITEMS:
                item(-1, 1, which, True)

            def body(h, b, more):
                for which in HEAD_ITEMS if more else LAST_ITEMS:
                    item(h, b, which, more)
            heads(dve, body)

        @block.gpsimd
        def _(pool):
            nc.gpsimd.memset(vh[:], 0.0).then_inc(v_cleared, 1)
            pool.wait_ge(v_cleared, 1)
            nc.gpsimd.tensor_copy(vh[:, 0, :, 0:HD + 1], m.V[:, :, 0]).then_inc(v_in, 1)

            def body(h, b, more):
                if more:
                    pass_gate(pool, sem, pv_done, FREE_PROBS + len(PAIRS) * h)
                    nc.gpsimd.tensor_copy(vh[:, 1 - b, :, 0:HD + 1], m.V[:, :, h + 1]).then_inc(v_in, 1)
            heads(pool, body)


def project_out(nc, m, sem):
    X = m.X
    with ExitStack() as ctx:
        def sb(name, shape, dt=F32):
            return ctx.enter_context(nc.sbuf_tensor(name, shape, dt))

        def ps(name, shape, dt=F32):
            return ctx.enter_context(nc.psum_tensor(name, shape, dt))

        names = "w_in recip_made o_made oT_made oT_copied y_made base_made joined stats_made mv_made eps_added rstd_made".split()
        (w_in, recip_made, o_made, oT_made, oT_copied, y_made, base_made, joined, stats_made, mv_made, eps_added,
         rstd_made) = (ctx.enter_context(nc.semaphore("e_" + n)) for n in names)
        stats = sb("e_stats", [P, 2, nc.vector.BN_STATS_DIM])
        mv = sb("e_mv", [P, 2, 2])
        shifted_var = sb("e_shifted_var", [P, 2, 1])
        rstd = sb("e_rstd", [P, 2, 1])
        mid_in, late_out = ([ctx.enter_context(nc.semaphore(f"e_{n}{i}")) for i in range(2)] for n in ("mid_in", "late_out"))
        w = sb("e_w", [P, KC, D])
        bias = sb("e_bias", [P, D])
        recip = sb("e_recip", [P, 2, NH])
        o = sb("e_o", [P, 2, D])
        oT = sb("e_oT", [P, 2, KC, P])
        mid = sb("e_mid", [P, 2, D])
        base = sb("e_base", [P, 2, D])
        late = sb("e_late", [P, 2, D])
        oT_ps = ps("e_oT_ps", [P, 2, 512])
        y_ps = ps("e_y_ps", [P, 2, 512])
        block = ctx.enter_context(nc.Block())

        @block.sync
        def _(sp):
            nc.sync.dma_start(w[:], m.cwo_dram).then_inc(w_in, 16)
            nc.sync.dma_start(bias[:], m.cbo_dram.partition_broadcast(P)).then_inc(w_in, 16)

            def load(pair, odd):
                a = tile_at(pair, 0, odd)
                if exists(pair, odd, -2):
                    sp.wait_ge(base_made, a.count - 1)
                nc.sync.dma_start(mid[:, a.slot], m.mid_dram[bass.ts(a.place, P)]).then_inc(mid_in[a.slot], 16)
            for s in range(2):
                load(s // 2, s % 2)
            with sp.Fori(1, NT // 2) as pair:
                for odd in range(2):
                    load(pair, odd)

        @block.tensor
        def _(pe):
            def step(pair, odd):
                if exists(pair, odd, 0):
                    a = tile_at(pair, 0, odd)
                    pe.wait_ge(o_made, a.count + 1)
                    if exists(pair, odd, -2):
                        pe.wait_ge(oT_copied, a.count - 1)
                    for c in range(KC):
                        mm = nc.tensor.transpose(oT_ps[:, a.slot, c * P:(c + 1) * P], o[:, a.slot, c * P:(c + 1) * P], m.ident[:])
                    mm.then_inc(oT_made, 1)
                if exists(pair, odd, -1):
                    a = tile_at(pair, 0, odd, -1)
                    pe.wait_ge(oT_copied, a.count + 1)
                    if exists(pair, odd, -3):
                        pe.wait_ge(joined, a.count - 1)
                    else:
                        pe.wait_ge(w_in, 32)
                    for c in range(KC):
                        mm = nc.tensor.matmul(y_ps[:, a.slot, 0:D], oT[:, a.slot, c], w[:, c], start=(c == 0), stop=(c == KC - 1))
                    mm.then_inc(y_made, 1)
            stepped(pe, step, 0, NT, 2)

        @block.scalar
        def _(act):
            def step(pair, odd):
                if exists(pair, odd, 0):
                    a = tile_at(pair, 0, odd)
                    act.wait_ge(oT_made, a.count + 1)
                    if exists(pair, odd, -2):
                        act.wait_ge(y_made, a.count - 1)
                    nc.scalar.copy(oT[:, a.slot], oT_ps[:, a.slot, 0:D].rearrange("p (c t) -> p c t", t=P)).then_inc(oT_copied, 1)
                if exists(pair, odd, -2):
                    a = tile_at(pair, 0, odd, -2)
                    act.wait_ge(joined, a.count + 1)
                    nc.scalar.dma_start(m.late_dram[bass.ts(a.place, P)], late[:, a.slot]).then_inc(late_out[a.slot], 16)
            stepped(act, step, 0, NT + 1)
            for slot in range(2):
                act.wait_ge(late_out[slot], 16 * (NT // 2))

        @block.vector
        def _(dve):
            def step(pair, odd):
                if exists(pair, odd, 0):
                    a = tile_at(pair, 0, odd)
                    nc.vector.reciprocal(recip[:, a.slot], m.O[:, a.place, :, HD]).then_inc(recip_made, 1)
                    pass_gate(dve, sem, recip_made, a.count + 1)
                    if exists(pair, odd, -2):
                        pass_gate(dve, sem, oT_made, a.count - 1)
                    nc.vector.tensor_tensor(o[:, a.slot].rearrange("p (h d) -> p h d", d=HD), m.O[:, a.place, :, 0:HD],
                                            recip[:, a.slot].unsqueeze(2).broadcast_to([P, NH, HD]), ALU.mult).then_inc(o_made, 1)
                if exists(pair, odd, -2):
                    a = tile_at(pair, 0, odd, -2)
                    dve.wait_ge(base_made, a.count + 1)
                    if exists(pair, odd, -4):
                        dve.wait_ge(late_out[a.slot], 16 * a.turn)
                    dve.wait_ge(y_made, a.count + 1)
                    nc.vector.tensor_tensor(late[:, a.slot], base[:, a.slot], y_ps[:, a.slot, 0:D], ALU.add).then_inc(joined, 1)
                if exists(pair, odd, -3):
                    a = tile_at(pair, 0, odd, -3)
                    pass_gate(dve, sem, rstd_made, a.count + 1)
                    nc.vector.tensor_scalar(X[:, a.place], late[:, a.slot], mv[:, a.slot, 0:1], rstd[:, a.slot], ALU.subtract, ALU.mult)
                if exists(pair, odd, -2):
                    a = tile_at(pair, 0, odd, -2)
                    pass_gate(dve, sem, joined, a.count + 1)
                    nc.vector.bn_stats(stats[:, a.slot], late[:, a.slot]).then_inc(stats_made, 1)
                    pass_gate(dve, sem, stats_made, a.count + 1)
                    nc.vector.bn_aggr(mv[:, a.slot], stats[:, a.slot]).then_inc(mv_made, 1)
            stepped(dve, step, 0, NT + 2, 2)

        @block.gpsimd
        def _(pool):
            pool.wait_ge(w_in, 32)

            def step(pair, odd):
                if exists(pair, odd, 0):
                    a = tile_at(pair, 0, odd)
                    pool.wait_ge(mid_in[a.slot], 16 * a.turn + 16)
                    if exists(pair, odd, -2):
                        pool.wait_ge(joined, a.count - 1)
                    nc.gpsimd.tensor_tensor(base[:, a.slot], mid[:, a.slot], bias[:], ALU.add).then_inc(base_made, 1)
                if exists(pair, odd, -2):
                    a = tile_at(pair, 0, odd, -2)
                    pass_gate(pool, sem, mv_made, a.count + 1)
                    nc.gpsimd.tensor_scalar(shifted_var[:, a.slot], mv[:, a.slot, 1:2], EPS, None, ALU.add).then_inc(eps_added, 1)
                    pool.wait_ge(eps_added, a.count + 1)
                    nc.gpsimd.tensor_tensor(rstd[:, a.slot], shifted_var[:, a.slot], m.minus_half[:, 0:1], ALU.pow).then_inc(rstd_made, 1)
            stepped(pool, step, 0, NT + 1)


ATTENTION_SEMS = """h_in:2 rope_in:2 w_attn_in rope_made hT_made hT_copied qkT_made qkT_copied pT_made pT_copied
    scores_made masked nbias_made probs_made rsum_made probs_normal o_summed oT_copied out_made x_added
    qk_made v_made v_copied squared qk_read ssq_made ssq_kept rnorm_made k_turned qk_rotated window_cleared
    w1_high_made mhT_high_made mhT_split
    w_high_made w_split hT_split""".split()
MLP_SEMS = """mh_in w_mlp_in stats_made mv_made eps_added rstd_made ln_applied mhT_made mhT_copied ag_made gelu_made
    u_made y_made xb_made mx_added""".split()


class Memory:
    pass


def window_masks():
    i, j = np.arange(P)[:, None], np.arange(P)[None, :]
    own = np.where(j > i, NEG, 0.0)
    past = np.where(j < i, NEG, 0.0)
    even, odd = np.concatenate([own, past], 1), np.concatenate([past, own], 1)
    first = np.concatenate([own, np.full((P, P), NEG)], 1)
    return np.stack([even, odd, first], 1).astype(np.float32)


def window_tables():
    half = np.arange(0, WD, 2, dtype=np.float32)
    inv = (np.float32(1.0) / np.float32(10000.0) ** (half / np.float32(WD))).astype(np.float32)
    t = np.arange(S, dtype=np.float32)
    freqs = t[:, None] * inv[None, :]
    base = (half + np.float32(0.4 * WD)) / np.float32(1.4 * WD)
    power = (t - np.float32(S // 2)) / np.float32(P // 2)
    scale = base[None, :].astype(np.float64) ** power[:, None].astype(np.float64)
    two = lambda a: np.concatenate([a, a], -1)
    cos, sin = two(np.cos(freqs.astype(np.float64))), np.sin(freqs.astype(np.float64))
    sin = np.concatenate([-sin, sin], -1)
    scale = two(scale)
    tables = np.stack([8.0 * cos * scale, 8.0 * sin * scale, cos / scale, sin / scale], 1)
    return np.ascontiguousarray(tables.reshape(NT, P, 4, WD).astype(np.float32))


def build(nc, a, out):
    with ExitStack() as ctx:
        m, made = Memory(), {}

        def sb(name, shape, dt=F32):
            return ctx.enter_context(nc.sbuf_tensor(name, shape, dt))

        for name in ATTENTION_SEMS + MLP_SEMS + ["consts_in", "gates_passed"]:
            name, _, n = name.partition(":")
            each = [ctx.enter_context(nc.semaphore(name + (str(i) if n else ""))) for i in range(int(n or 1))]
            made[name] = each if n else each[0]
        sem = namedtuple("Semaphores", made)(**made)

        m.X = sb("X", [P, NT, D])
        m.ident = sb("ident", [P, P])
        m.identb = sb("identb", [P, P], BF16)
        m.cmask = sb("cmask", [P, 3, P], BF16)
        m.masks = sb("masks", [P, 3, 2 * P])
        m.mask_first = m.masks[:, 2]
        m.zeros = sb("zeros", [1, P])
        m.minus_half = sb("minus_half", [P, 2 * WH])
        m.wqkv = sb("wqkv", [P, KC, 3 * INNER])
        m.wo = sb("wo", [P, INNER // P, D])
        m.scales = sb("scales", [P, 4, WD])
        m.w1 = sb("w1", [P, KC, 2 * HID])
        m.w2 = sb("w2", [P, NC, D])
        m.b1 = sb("b1", [P, 2, NC])
        m.ln = sb("ln", [P, 2, KC])
        m.b2 = sb("b2", [P, D])

        m.wqkv_dram = a["wqkv"].rearrange("l (c p) n -> l p c n", p=P)
        m.wo_dram = a["wo"].rearrange("l (c p) n -> l p c n", p=P)
        m.scales_dram = a["scales"]
        m.rope_dram, m.x_dram = a["rope"], a["x"]
        m.cwqkv_dram = a["cwqkv"].rearrange("(c p) n -> p c n", p=P)
        m.cwo_dram = a["cwo"].rearrange("(c p) n -> p c n", p=P)
        m.cbias_dram, m.cbo_dram, m.crope_dram = a["cbias"], a["cbo"], a["crope"]
        m.mid_dram = nc.dram_tensor("mid_dram", [S, D], F32).ap()
        m.late_dram = nc.dram_tensor("late_dram", [S, D], F32).ap()
        m.max_dram = nc.dram_tensor("max_dram", [3, S], BF16).ap()
        m.parts_dram = nc.dram_tensor("parts_dram", [6, D, S], BF16).ap()

        full = (NC - 1) * CW
        def mlp_weights(l):
            loads = [(m.w1[:], a["w1"].rearrange("l (c p) n -> l p c n", p=P)[l]),
                     (m.w2[0:CW, 0:NC - 1], a["w2"][:, 0:full].rearrange("l (c p) n -> l p c n", p=CW)[l]),
                     (m.w2[0:HID - full, NC - 1], a["w2"][l, full:HID]),
                     (m.ln[:], a["ln"][l]),
                     (m.b1[:], a["b1"][l]),
                     (m.b2[:], a["b2"][l].partition_broadcast(P))]
            return loads
        m.mlp_weights = mlp_weights
        m.attention_weights = lambda l: [(m.wqkv[:], m.wqkv_dram[l]), (m.scales[:], m.scales_dram[l].partition_broadcast(P)),
                                         (m.wo[:], m.wo_dram[l])]
        m.w_mlp_count = lambda before: 16 * 6 * (before // NG) + 16 * 6
        m.w_attn_count = lambda before: 16 * 3 * (before // (NT // 2)) + 16 * 3

        with nc.Block() as block:
            @block.sync
            def _(sp):
                nc.sync.dma_start(m.ident[:], a["ident"]).then_inc(sem.consts_in, 16)
                nc.sync.dma_start(m.masks[:], a["masks"]).then_inc(sem.consts_in, 16)
                nc.sync.dma_start(m.identb[:], a["identb"]).then_inc(sem.consts_in, 16)
                nc.sync.dma_start(m.cmask[:], a["cmask"]).then_inc(sem.consts_in, 16)
                sp.wait_ge(sem.consts_in, 64)

            @block.gpsimd
            def _(pool):
                nc.gpsimd.memset(m.zeros[:], 0.0)
                nc.gpsimd.memset(m.minus_half[:], -0.5)

        def stack(call):
            m.tag = f"_s{call}"
            with ExitStack() as of_stack:
                def sb(name, shape, dt=F32):
                    return of_stack.enter_context(nc.sbuf_tensor(name + m.tag, shape, dt))
                m.mlp_h = sb("mlp_h", [P, GT, D])
                m.mlp_hn = sb("mlp_hn", [P, GT, D])
                m.mlp_stats = sb("mlp_stats", [P, GT, nc.vector.BN_STATS_DIM])
                m.mlp_mv = sb("mlp_mv", [P, GT, 2])
                m.mlp_var = sb("mlp_var", [P, GT])
                m.mlp_rstd = sb("mlp_rstd", [P, GT])
                m.w1_parts = [sb("w1" + n, [P, KC, 2 * HID], F32R) for n in ("_high", "_low")]
                with nc.Fori(0, DEPTH) as layer:
                    m.layer = layer
                    window_attention(nc, m, sem, (call * DEPTH + layer) * (NT // 2))
                    mlp(nc, m, sem, (call * DEPTH + layer) * NG)

        normalise_input(nc, m, sem)
        stack(0)
        with nc.sbuf_tensor("V", [P, NT, NH, HD + 1], F32) as m.V:
            project_heads(nc, m, sem)
            with nc.sbuf_tensor("O", [P, NT, NH, HD + 1], F32) as m.O:
                causal_attention(nc, m, sem)
                project_out(nc, m, sem)
        stack(1)
        join_output(nc, m, out)


def causal_tables():
    dim = np.arange(HD // 2, dtype=np.float32)
    div = np.exp((np.float32(2.0) * dim / np.float32(HD) * np.float32(np.log(10000.0))).astype(np.float32)).astype(np.float32)
    theta = (np.arange(S, dtype=np.float32)[:, None] / div[None, :]).astype(np.float32).astype(np.float64)
    cos = np.repeat(np.cos(theta), 2, -1)
    sin = np.stack([-np.sin(theta), np.sin(theta)], -1).reshape(S, HD)
    both = np.stack([cos, sin], 1)
    tables = np.stack([both * HD ** -0.5, both], 1)
    return np.ascontiguousarray(tables.reshape(NT, P, 2, 2, HD).astype(np.float32))


def causal_masks():
    i, j = np.arange(P)[:, None], np.arange(P)[None, :]
    masks = np.stack([np.full((P, P), NEG), np.where(i > j, NEG, 0.0), np.where(j > i, NEG, 0.0)], 1)
    return np.ascontiguousarray(masks.astype(mybir.dt.np(BF16)))


def arrays(i):
    f = lambda n: np.ascontiguousarray(i["L0_" + n])
    swap = lambda s: np.concatenate([s[:, WD // 2:], s[:, :WD // 2]], 1)
    qs, ks = f("ffn_q_scale"), f("ffn_k_scale")
    b1 = np.zeros((DEPTH, 2, NC * CW), np.float32)
    b1[:, :, :HID] = f("ffn_b1").reshape(DEPTH, 2, HID)
    b1 = np.pad(b1.reshape(DEPTH, 2, NC, CW), ((0, 0), (0, 0), (0, 0), (0, P - CW)))
    b1 = np.ascontiguousarray(b1.transpose(0, 3, 1, 2))
    ln = np.stack([f("ffn_ln_g"), f("ffn_ln_b")], 1).reshape(DEPTH, 2, KC, P)
    return {
        "x": f("attn_x").reshape(S, D),
        "wqkv": f("ffn_wqkv"), "wo": f("ffn_wo"), "scales": np.ascontiguousarray(np.stack([qs, swap(qs), ks, swap(ks)], 1)),
        "w1": f("ffn_w1"), "b1": b1, "w2": f("ffn_w2"), "b2": f("ffn_b2"), "ln": np.ascontiguousarray(ln.transpose(0, 3, 1, 2)),
        "cwqkv": np.ascontiguousarray(np.concatenate([f("attn_wq").T, f("attn_wk").T, f("attn_wv").T], 1)),
        "cbias": np.concatenate([f("attn_bq"), f("attn_bk"), f("attn_bv")]), "cwo": np.ascontiguousarray(f("attn_wo").T), "cbo": f("attn_bo"),
        "crope": causal_tables(), "cmask": causal_masks(), "identb": np.eye(P, dtype=mybir.dt.np(BF16)),
        "rope": window_tables(), "masks": window_masks(), "ident": np.eye(P, dtype=np.float32),
    }


def kernel(**inputs):
    import concourse.bacc as bacc
    from concourse.bass_utils import run_bass_kernel_spmd

    nc = bacc.Bacc("TRN2", target_bir_lowering=False, num_devices=1)
    laid_out = arrays({name: np.asarray(v) for name, v in inputs.items()})
    tensors = {name: nc.dram_tensor(f"in_{name}_dram", v.shape, mybir.dt.from_np(v.dtype), kind="ExternalInput").ap()
               for name, v in laid_out.items()}
    out = nc.dram_tensor("out_dram", [S, D], F32, kind="ExternalOutput").ap()
    build(nc, tensors, out)
    result = run_bass_kernel_spmd(nc, [{f"in_{name}_dram": v for name, v in laid_out.items()}], core_ids=[0])
    return result.results[0]["out_dram"].reshape(1, S, D)
```
